# Optimizing a Trainium2 kernel written in Bass

```python
import numpy as np
import jax
import jax.numpy as jnp

def _softmax(x, axis=-1):
    return jax.nn.softmax(x, axis=axis)

def _gelu(x):
    return jax.nn.gelu(x, approximate=True)

def _silu(x):
    return jax.nn.silu(x)

def _sigmoid(x):
    return jax.nn.sigmoid(x)

def _layernorm(x, axis=-1, eps=1e-05):
    m = jnp.mean(x, axis=axis, keepdims=True)
    v = jnp.var(x, axis=axis, keepdims=True)
    return (x - m) / jnp.sqrt(v + eps)

def _scatter_add(tgt, idx, src, axis=0):
    return tgt.at[idx].add(src)

def _segment_sum(src, seg, n):
    return jax.ops.segment_sum(src, seg, n)
kernel_name = 'mk_seq_preln_d2_jaxref_r8_5d52ce'

def setup_inputs(seed: int=0):
    np.random.seed(seed)
    _w = jnp.asarray

    def _L0_attn_setup():
        import jax, jax.numpy as jnp
        import numpy as np
        EMBED = 512
        H = 32
        KV = 8
        D = EMBED // H
        REP = H // KV

        def _rope(t, cos, sin):
            t = t.reshape(*t.shape[:-1], 2, D // 2)
            t1, t2 = (t[..., 0, :], t[..., 1, :])
            return jnp.concatenate([t1 * cos - t2 * sin, t1 * sin + t2 * cos], axis=-1)
        key = jax.random.key(seed)
        ks = jax.random.split(key, 7)
        B, S = (1, 256)
        x = jax.random.normal(ks[0], (B, S, EMBED), dtype=jnp.float32)
        wq = jax.random.normal(ks[1], (EMBED, EMBED), dtype=jnp.float32) * 0.02
        bq = jax.random.normal(ks[2], (EMBED,), dtype=jnp.float32) * 0.02
        wk = jax.random.normal(ks[3], (EMBED, KV * D), dtype=jnp.float32) * 0.02
        bk = jax.random.normal(ks[4], (KV * D,), dtype=jnp.float32) * 0.02
        wv = jax.random.normal(ks[5], (EMBED, KV * D), dtype=jnp.float32) * 0.02
        bv = jax.random.normal(ks[6], (KV * D,), dtype=jnp.float32) * 0.02
        return {'x': x, 'wq': wq, 'bq': bq, 'wk': wk, 'bk': bk, 'wv': wv, 'bv': bv}
    _L0_attn_in = _L0_attn_setup()

    def _L0_ffn_setup():
        import jax, jax.numpy as jnp
        import numpy as np
        NF4_CODE = jnp.array([-1.0, -0.6961928009986877, -0.5250730514526367, -0.39491748809814453, -0.28444138169288635, -0.18477343022823334, -0.09105003625154495, 0.0, 0.07958029955625534, 0.16093020141124725, 0.24611230194568634, 0.33791524171829224, 0.44070982933044434, 0.5626170039176941, 0.7229568362236023, 1.0], dtype=jnp.float32)
        BLOCKSIZE = 64

        def nf4_quant_dequant(w):
            shape = w.shape
            flat = w.reshape(-1, BLOCKSIZE)
            absmax = jnp.max(jnp.abs(flat), axis=1, keepdims=True)
            normalized = flat / jnp.where(absmax == 0, 1.0, absmax)
            bounds = (NF4_CODE[:-1] + NF4_CODE[1:]) * 0.5
            idx = jnp.searchsorted(bounds, normalized)
            return (NF4_CODE[idx] * absmax).reshape(shape)
        key = jax.random.key(seed)
        k1, k2, k3, kx = jax.random.split(key, 4)
        D, H = (512, 1376)
        scale = 0.02
        w1 = jax.random.normal(k1, (H, D), jnp.float32) * scale
        w2 = jax.random.normal(k2, (H, D), jnp.float32) * scale
        w3 = jax.random.normal(k3, (D, H), jnp.float32) * scale
        x = jax.random.normal(kx, (2, 256, D), jnp.float32)
        return {'x': x, 'w1': w1, 'w2': w2, 'w3': w3}
    _L0_ffn_in = _L0_ffn_setup()

    def _L1_attn_setup():
        import jax, jax.numpy as jnp
        import numpy as np
        H = 512
        D = 1024
        N = 16
        K = 4
        R = 32
        BATCH = 1
        L = 256
        EPS = 1e-06

        def _rmsnorm(x, w):
            return x * jax.lax.rsqrt(jnp.mean(x * x, axis=-1, keepdims=True) + EPS) * w
        key = jax.random.key(seed)
        ks = jax.random.split(key, 10)
        s = 0.02
        return {'hidden_states': jax.random.normal(ks[0], (BATCH, L, H), jnp.float32), 'W_in': jax.random.normal(ks[1], (2 * D, H), jnp.float32) * s, 'conv_w': jax.random.normal(ks[2], (D, K), jnp.float32) * s, 'conv_b': jax.random.normal(ks[3], (D,), jnp.float32) * s, 'Wx': jax.random.normal(ks[4], (R + 2 * N, D), jnp.float32) * s, 'dt_ln_w': jnp.ones((R,), jnp.float32), 'b_ln_w': jnp.ones((N,), jnp.float32), 'c_ln_w': jnp.ones((N,), jnp.float32), 'Wdt': jax.random.normal(ks[5], (D, R), jnp.float32) * s, 'dt_bias': jax.random.normal(ks[6], (D,), jnp.float32) * s, 'A': -jnp.exp(jax.random.normal(ks[7], (D, N), jnp.float32) * 0.5), 'D_param': jnp.ones((D,), jnp.float32), 'W_out': jax.random.normal(ks[8], (H, D), jnp.float32) * s}
    _L1_attn_in = _L1_attn_setup()

    def _L1_ffn_setup():
        import jax, jax.numpy as jnp
        import numpy as np
        TOP_K = 2
        SCALING = 32.0 / 64.0
        key = jax.random.key(seed)
        ks = jax.random.split(key, 6)
        Bsz, S, Din, Dout, R, E = (4, 256, 512, 512, 64, 16)
        x = jax.random.normal(ks[0], (Bsz, S, Din), dtype=jnp.float32)
        base_w = jax.random.normal(ks[1], (Dout, Din), dtype=jnp.float32) * 0.02
        base_b = jax.random.normal(ks[2], (Dout,), dtype=jnp.float32) * 0.02
        A = jax.random.normal(ks[3], (R, Din), dtype=jnp.float32) * (1.0 / np.sqrt(Din))
        B = jax.random.normal(ks[4], (E, Dout, R), dtype=jnp.float32) * 0.02
        router_w = jax.random.normal(ks[5], (E, Din), dtype=jnp.float32) * 0.02
        return {'x': x, 'base_w': base_w, 'base_b': base_b, 'A': A, 'B': B, 'router_w': router_w}
    _L1_ffn_in = _L1_ffn_setup()
    _d = {'L0_attn_x': _L0_attn_in['x'], 'L0_attn_wq': _L0_attn_in['wq'], 'L0_attn_bq': _L0_attn_in['bq'], 'L0_attn_wk': _L0_attn_in['wk'], 'L0_attn_bk': _L0_attn_in['bk'], 'L0_attn_wv': _L0_attn_in['wv'], 'L0_attn_bv': _L0_attn_in['bv'], 'L0_ffn_w1': _L0_ffn_in['w1'], 'L0_ffn_w2': _L0_ffn_in['w2'], 'L0_ffn_w3': _L0_ffn_in['w3'], 'L1_attn_W_in': _L1_attn_in['W_in'], 'L1_attn_conv_w': _L1_attn_in['conv_w'], 'L1_attn_conv_b': _L1_attn_in['conv_b'], 'L1_attn_Wx': _L1_attn_in['Wx'], 'L1_attn_dt_ln_w': _L1_attn_in['dt_ln_w'], 'L1_attn_b_ln_w': _L1_attn_in['b_ln_w'], 'L1_attn_c_ln_w': _L1_attn_in['c_ln_w'], 'L1_attn_Wdt': _L1_attn_in['Wdt'], 'L1_attn_dt_bias': _L1_attn_in['dt_bias'], 'L1_attn_A': _L1_attn_in['A'], 'L1_attn_D_param': _L1_attn_in['D_param'], 'L1_attn_W_out': _L1_attn_in['W_out'], 'L1_ffn_base_w': _L1_ffn_in['base_w'], 'L1_ffn_base_b': _L1_ffn_in['base_b'], 'L1_ffn_A': _L1_ffn_in['A'], 'L1_ffn_B': _L1_ffn_in['B'], 'L1_ffn_router_w': _L1_ffn_in['router_w']}
    _x0 = _d['L0_attn_x']
    _d['L0_attn_x'] = jax.random.normal(jax.random.fold_in(jax.random.key(seed), 1), (2, 512, 512), dtype=_x0.dtype)
    del _x0
    return _d

def reference(L0_attn_x, L0_attn_wq, L0_attn_bq, L0_attn_wk, L0_attn_bk, L0_attn_wv, L0_attn_bv, L0_ffn_w1, L0_ffn_w2, L0_ffn_w3, L1_attn_W_in, L1_attn_conv_w, L1_attn_conv_b, L1_attn_Wx, L1_attn_dt_ln_w, L1_attn_b_ln_w, L1_attn_c_ln_w, L1_attn_Wdt, L1_attn_dt_bias, L1_attn_A, L1_attn_D_param, L1_attn_W_out, L1_ffn_base_w, L1_ffn_base_b, L1_ffn_A, L1_ffn_B, L1_ffn_router_w):

    def _L0_attn_ref(x, wq, bq, wk, bk, wv, bv):
        import jax, jax.numpy as jnp
        import numpy as np
        EMBED = 512
        H = 32
        KV = 8
        D = EMBED // H
        REP = H // KV

        def _rope(t, cos, sin):
            t = t.reshape(*t.shape[:-1], 2, D // 2)
            t1, t2 = (t[..., 0, :], t[..., 1, :])
            return jnp.concatenate([t1 * cos - t2 * sin, t1 * sin + t2 * cos], axis=-1)
        B, S, E = x.shape
        xq = (x @ wq + bq).reshape(B, S, H, D)
        xk = (x @ wk + bk).reshape(B, S, KV, D)
        xv = (x @ wv + bv).reshape(B, S, KV, D)
        inv_freq = 1.0 / 10000.0 ** (jnp.arange(0, D, 2, dtype=jnp.float32) / D)
        ang = jnp.arange(S, dtype=jnp.float32)[:, None] * inv_freq[None, :]
        cos, sin = (jnp.cos(ang)[:, None, :], jnp.sin(ang)[:, None, :])
        q = _rope(xq, cos, sin)
        k = _rope(xk, cos, sin)
        k = jnp.repeat(k, REP, axis=2)
        v = jnp.repeat(xv, REP, axis=2)
        scores = jnp.einsum('bqhd,bkhd->bhqk', q, k) / jnp.sqrt(jnp.float32(D))
        probs = jax.nn.softmax(scores.astype(jnp.float32), axis=-1)
        out = jnp.einsum('bhqk,bkhd->bqhd', probs, v).reshape(B, S, E)
        return out

    def _L0_ffn_ref(x, w1, w2, w3):
        import jax, jax.numpy as jnp
        import numpy as np
        NF4_CODE = jnp.array([-1.0, -0.6961928009986877, -0.5250730514526367, -0.39491748809814453, -0.28444138169288635, -0.18477343022823334, -0.09105003625154495, 0.0, 0.07958029955625534, 0.16093020141124725, 0.24611230194568634, 0.33791524171829224, 0.44070982933044434, 0.5626170039176941, 0.7229568362236023, 1.0], dtype=jnp.float32)
        BLOCKSIZE = 64

        def nf4_quant_dequant(w):
            shape = w.shape
            flat = w.reshape(-1, BLOCKSIZE)
            absmax = jnp.max(jnp.abs(flat), axis=1, keepdims=True)
            normalized = flat / jnp.where(absmax == 0, 1.0, absmax)
            bounds = (NF4_CODE[:-1] + NF4_CODE[1:]) * 0.5
            idx = jnp.searchsorted(bounds, normalized)
            return (NF4_CODE[idx] * absmax).reshape(shape)
        dq1 = nf4_quant_dequant(w1)
        dq2 = nf4_quant_dequant(w2)
        dq3 = nf4_quant_dequant(w3)
        gate = jnp.einsum('bsd,hd->bsh', x, dq1)
        up = jnp.einsum('bsd,hd->bsh', x, dq2)
        h = jax.nn.silu(gate) * up
        return jnp.einsum('bsh,dh->bsd', h, dq3)

    def _L1_attn_ref(hidden_states, W_in, conv_w, conv_b, Wx, dt_ln_w, b_ln_w, c_ln_w, Wdt, dt_bias, A, D_param, W_out):
        import jax, jax.numpy as jnp
        import numpy as np
        H = 512
        D = 1024
        N = 16
        K = 4
        R = 32
        BATCH = 1
        L = 256
        EPS = 1e-06

        def _rmsnorm(x, w):
            return x * jax.lax.rsqrt(jnp.mean(x * x, axis=-1, keepdims=True) + EPS) * w
        proj = hidden_states @ W_in.T
        u, gate = jnp.split(proj, 2, axis=-1)
        x = jnp.transpose(u, (0, 2, 1))
        x = jax.lax.conv_general_dilated(x, conv_w[:, None, :], window_strides=(1,), padding=[(K - 1, 0)], dimension_numbers=('NCH', 'OIH', 'NCH'), feature_group_count=D)
        u = jax.nn.silu(jnp.transpose(x, (0, 2, 1)) + conv_b)
        ssm_p = u @ Wx.T
        dt, Bm, Cm = jnp.split(ssm_p, [R, R + N], axis=-1)
        dt = _rmsnorm(dt, dt_ln_w)
        Bm = _rmsnorm(Bm, b_ln_w)
        Cm = _rmsnorm(Cm, c_ln_w)
        delta = jax.nn.softplus(dt @ Wdt.T + dt_bias)

        def step(state, xs):
            d_t, B_t, C_t, u_t = xs
            dA = jnp.exp(d_t[..., None] * A)
            state = dA * state + (d_t * u_t)[..., None] * B_t[:, None, :]
            y_t = jnp.einsum('bdn,bn->bd', state, C_t)
            return (state, y_t)
        init = jnp.zeros((hidden_states.shape[0], D, N), hidden_states.dtype)
        xs = (jnp.swapaxes(delta, 0, 1), jnp.swapaxes(Bm, 0, 1), jnp.swapaxes(Cm, 0, 1), jnp.swapaxes(u, 0, 1))
        _, ys = jax.lax.scan(step, init, xs)
        y = jnp.swapaxes(ys, 0, 1) + u * D_param
        y = y * jax.nn.silu(gate)
        return y @ W_out.T

    def _L1_ffn_ref(x, base_w, base_b, A, B, router_w):
        import jax, jax.numpy as jnp
        import numpy as np
        TOP_K = 2
        SCALING = 32.0 / 64.0
        base_out = jnp.einsum('bsi,oi->bso', x, base_w) + base_b
        res_hidden = jnp.einsum('bsi,ri->bsr', x, A)
        logits = jnp.einsum('bsi,ei->bse', x, router_w)
        probs = jax.nn.softmax(logits, axis=-1)
        topw, topi = jax.lax.top_k(probs, TOP_K)
        topw = topw / (jnp.sum(topw, axis=-1, keepdims=True) + 1e-06)
        num_experts = B.shape[0]
        combine = jnp.sum(jax.nn.one_hot(topi, num_experts, dtype=x.dtype) * topw[..., None], axis=-2)
        delta = jnp.einsum('bse,bsr,eor->bso', combine, res_hidden, B)
        return base_out + delta * SCALING
    x = L0_attn_x
    x = x + _L0_attn_ref(_layernorm(x, axis=-1), L0_attn_wq, L0_attn_bq, L0_attn_wk, L0_attn_bk, L0_attn_wv, L0_attn_bv)
    x = x + _L0_ffn_ref(_layernorm(x, axis=-1), L0_ffn_w1, L0_ffn_w2, L0_ffn_w3)
    x = x + _L1_attn_ref(_layernorm(x, axis=-1), L1_attn_W_in, L1_attn_conv_w, L1_attn_conv_b, L1_attn_Wx, L1_attn_dt_ln_w, L1_attn_b_ln_w, L1_attn_c_ln_w, L1_attn_Wdt, L1_attn_dt_bias, L1_attn_A, L1_attn_D_param, L1_attn_W_out)
    x = x + _L1_ffn_ref(_layernorm(x, axis=-1), L1_ffn_base_w, L1_ffn_base_b, L1_ffn_A, L1_ffn_B, L1_ffn_router_w)
    return x

_drawn_inputs = setup_inputs


def setup_inputs(seed=0):
    import zlib

    import numpy as np

    out = dict(_drawn_inputs(seed))
    spreads = {'L1_attn_dt_ln_w': (1.0, 0.6),
     'L1_attn_b_ln_w': (1.0, 0.6),
     'L1_attn_c_ln_w': (1.0, 0.6),
     'L1_attn_D_param': (1.0, 0.6)}
    factors = {'L0_attn_wq': 8.0,
     'L0_attn_bq': 8.0,
     'L0_attn_wk': 8.0,
     'L0_attn_bk': 8.0,
     'L0_attn_wv': 3.079,
     'L1_attn_W_in': 3.874,
     'L1_attn_conv_w': 4.694,
     'L1_attn_conv_b': 5.026,
     'L1_attn_Wx': 4.372,
     'L1_attn_Wdt': 8.0,
     'L1_attn_dt_bias': 8.0,
     'L1_attn_A': 8.0,
     'L1_attn_W_out': 3.811,
     'L1_ffn_base_b': 17.516,
     'L1_ffn_A': 6.078,
     'L1_ffn_B': 6.091,
     'L1_ffn_router_w': 6.514}
    for name, (base, spread) in spreads.items():
        noise = np.random.default_rng([zlib.crc32(name.encode()), seed]).standard_normal(out[name].shape)
        drawn = base * np.exp(spread * noise) if base else spread * noise
        out[name] = jnp.asarray(drawn.astype(out[name].dtype))
    for name, factor in factors.items():
        out[name] = (out[name] * factor).astype(out[name].dtype)
    return out
```

```python
from contextlib import ExitStack

import numpy as np

import concourse.bass as bass
from concourse import mybir

F32 = mybir.dt.float32
BF16 = mybir.dt.bfloat16
U32 = mybir.dt.uint32
ALU = mybir.AluOpType
ACT = mybir.ActivationFunctionType
AXX = mybir.AxisListType.X

P = 128
NB, S, E = 2, 512, 512
NT = NB * S // P
TS_ = S // P
EC = E // P
BANK = 512
H, KV, HD = 32, 8, 16
REP = H // KV
GC = (REP + 1) * HD
QK = KV * GC
NG = NB * KV
PARTS = 6
KROWS = PARTS * HD
HF = 1376
NH = -(-HF // P)
BLK = 64
DI, NS, RK, KC = 1024, 16, 32, 4
DC = DI // P
SP_ = 80
UNITS = DC * NB * 4 * 4
NE, RR = 16, 64
LC = RR + NE

NF4 = np.array([-1.0, -0.6961928009986877, -0.5250730514526367, -0.39491748809814453, -0.28444138169288635,
                -0.18477343022823334, -0.09105003625154495, 0.0, 0.07958029955625534, 0.16093020141124725,
                0.24611230194568634, 0.33791524171829224, 0.44070982933044434, 0.5626170039176941,
                0.7229568362236023, 1.0], np.float32)
EDGES = (NF4[:-1] + NF4[1:]) * np.float32(0.5)
STEPS = NF4[1:] - NF4[:-1]


def sign_args():
    out = []
    for e in EDGES:
        up = np.nextafter(e, np.float32(np.inf))
        for s in (1.5, 1.25, 1.125, 1.75, 1.0625, 1.875, 1.375, 1.625):
            c = np.float32(-float(e) * s)
            for c in (c, np.nextafter(c, np.float32(-1e9)), np.nextafter(c, np.float32(1e9))):
                if float(e) * s < -float(c) < float(up) * s:
                    break
            else:
                continue
            break
        else:
            raise AssertionError("no scale separates the edge")
        out.append((s, float(c)))
    return out


SIGNS = sign_args()

CONSTS = {}


def constants():
    at, parts = 0, []

    def put(name, a):
        nonlocal at
        full = np.zeros((P, a.shape[1]), np.float32)
        full[:a.shape[0]] = a
        CONSTS[name] = (at, a.shape[1])
        parts.append(full)
        at += a.shape[1]

    p = np.arange(P)
    put("ident", np.eye(P, dtype=np.float32))
    put("spread", np.concatenate([((p[:, None] % 32) == (8 * s + p[None, :] // NS)) for s in range(4)], 1).astype(np.float32))
    put("gather", np.concatenate([(np.arange(32)[None, :] == (8 * s + p[:, None] // NS)) for s in range(4)], 1).astype(np.float32))
    mean = np.zeros((SP_, SP_), np.float32)
    for a, n in ((0, RK), (RK, NS), (64, NS)):
        mean[a:a + n, a:a + n] = 1.0 / n
    put("mean", mean)
    rep = np.zeros((SP_, P), np.float32)
    for a in (RK, 64):
        for n in range(NS):
            rep[a + n, n::NS] = 1.0
    put("rep", rep)
    freq = (1.0 / 10000.0 ** (np.arange(0, HD, 2, dtype=np.float32) / np.float32(HD))).astype(np.float32)
    ang = np.arange(S, dtype=np.float32)[:, None] * freq[None, :]
    for name, f in (("cos", np.cos), ("sin", np.sin)):
        t = f(ang).astype(np.float32)
        t = np.concatenate([t, t], 1).reshape(TS_, P, HD).transpose(1, 0, 2).reshape(P, TS_ * HD)
        put(name, t)
    put("iota", np.tile(np.arange(NE, dtype=np.float32), (P, 1)))
    put("edge_bias", np.tile(np.array([c for _, c in SIGNS], np.float32), (P, 1)))
    put("eps", np.full((P, 1), 1e-6, np.float32))
    put("one", np.ones((P, 1), np.float32))
    put("mhalf", np.full((P, 4), -0.5, np.float32))
    put("ones_row", np.ones((1, P), np.float32))
    return np.concatenate(parts, 1)


CONST = constants()


def build(nc, STOP, x, cst, wqkv, bqkv, w1, w2, w3, w_in, conv, wx, lnw, wdt, acol, w_out, base_w, base_b, lora_a, lora_b, out):
    ctx = ExitStack()
    with ctx:
        sem = lambda name: ctx.enter_context(nc.semaphore(name))
        arena = ctx.enter_context(nc.sbuf_tensor("arena", [P, 53200], F32))
        psum = ctx.enter_context(nc.psum_tensor("psum", [P, 8 * BANK], F32))

        def at(off, n, rows=P):
            return arena[0:rows, off:off + n]

        def at16(off, n, rows=P):
            return arena[0:rows, off:off + n // 2].bitcast(BF16)

        def bank(b, n=1, rows=P):
            return psum[0:rows, b * BANK:(b + n) * BANK]

        X = at(0, NT * E).rearrange("p (i e) -> p i e", e=E)
        XNT = at(4096, EC * NB * S).rearrange("p (c t) -> p c t", c=EC)
        NCST = CONST.shape[1]
        C = at(8192, NCST)
        const = lambda name, rows=P: C[0:rows, CONSTS[name][0]:CONSTS[name][0] + CONSTS[name][1]]
        assert NCST <= 1408
        small = 9600
        ST6 = at(small, 48).rearrange("p (i s) -> p i s", s=6)
        MV = at(small + 48, 16).rearrange("p (i s) -> p i s", s=2)
        VARE = at(small + 64, 8)
        RSTD = at(small + 72, 8)
        identb = at16(small + 80, P)
        XN = at(small + 144, 2 * E).rearrange("p (k e) -> p k e", e=E)
        R0 = small + 144 + 1024
        ident = const("ident")
        o = R0
        WQ = at(o, EC * 768).rearrange("p (c n) -> p c n", c=EC); o += EC * 768
        BQ = at(o, 768, 1); o += 768
        R = at(o, NT * QK).rearrange("p (i n) -> p i n", i=NT); o += NT * QK
        V1 = at(o, NT * KV * 32).rearrange("p (i k d) -> p i k d", i=NT, k=KV); o += NT * KV * 32
        QC = at(o, QK).rearrange("p (h d) -> p h d", d=HD); o += QK
        QS = at(o, QK).rearrange("p (h d) -> p h d", d=HD); o += QK
        SKW = TS_ * 5 * KROWS
        SK = at16(o, 2 * SKW).rearrange("p (k t s q d) -> p k t s q d", k=2, t=TS_, s=5, d=HD)
        SKF = at16(o, 2 * SKW).rearrange("p (k t s c) -> p k t s c", k=2, t=TS_, s=5); o += SKW
        RES = at(o, TS_ * GC).rearrange("p (t s d) -> p t s d", t=TS_, d=HD); o += TS_ * GC
        LO = at16(o, TS_ * GC).rearrange("p (t s d) -> p t s d", t=TS_, d=HD); o += TS_ * GC // 2
        QT = at16(o, 4 * 5 * S).rearrange("p (k s t) -> p k s t", k=4, s=5); o += 4 * 5 * S // 2
        PR = at(o, 3 * REP * S).rearrange("p (k j t) -> p k j t", k=3, j=REP); o += 3 * REP * S
        OS = at(o, 2 * S).rearrange("p (k t) -> p k t", k=2); o += 2 * S
        MX = at(o, 32).rearrange("p (k t j) -> p k t j", k=2, t=TS_); o += 32
        MS = at16(o, 64).rearrange("p (k t m j) -> p k t m j", k=2, t=TS_, m=2)
        MSF = at16(o, 64).rearrange("p (k t c) -> p k t c", k=2, t=TS_); o += 32
        MTS = at16(o, 2 * S).rearrange("p (k t) -> p k t", k=2); o += S
        REC = at(o, 16).rearrange("p (t j) -> p t j", j=REP); o += 16
        TMP = at(o, TS_ * REP * HD).rearrange("p (t j d) -> p t j d", t=TS_, j=REP); o += TS_ * REP * HD
        assert o <= 41000, o
        o = R0
        HT = at(o, NH * NB * S).rearrange("p (h t) -> p h t", h=NH); o += NH * NB * S
        DQ3 = at(o, NH * E).rearrange("p (h e) -> p h e", h=NH); o += NH * E
        DQT = at(o, 2 * 2 * E).rearrange("p (k w c h) -> p k w c h", k=2, w=2, c=EC); o += 2 * 2 * E
        SG = at(o, NB * S); o += NB * S
        W3V = at(o, BANK); o += BANK
        W3M = at(o, 2 * BANK).rearrange("p (k n) -> p k n", k=2); o += 2 * BANK
        W3T = at(o, 2 * BANK).rearrange("p (k n) -> p k n", k=2); o += 2 * BANK
        W3A = at(o, 2 * BANK).rearrange("p (k n) -> p k n", k=2); o += 2 * BANK
        AM = at(o, 4 * 16).rearrange("p (q n) -> p q n", q=4); o += 64
        AM3 = at(o, 4 * 86).rearrange("p (q n) -> p q n", q=4); o += 4 * 86
        NV = at(o, 2 * E); o += 2 * E
        NTB = at(o, 2 * 2 * E).rearrange("p (k n) -> p k n", k=2); o += 4 * E
        NACC = at(o, 2 * E); o += 2 * E
        DQ = at(o, 2 * 2 * E).rearrange("p (k w e) -> p k w e", k=2, w=2); o += 4 * E
        assert o <= 41000, o
        W3F = at(41000, 4 * HF)
        W3R = at(41000, 4 * HF).rearrange("p (j r h) -> p j r h", j=2, r=2)
        WR = at(46504, 2 * 2 * E).rearrange("p (k w e) -> p k w e", k=2, w=2)
        WI = at(41000, EC * 2 * DI).rearrange("p (c n) -> p c n", c=EC)
        U = at(R0, DC * NB * S).rearrange("p (c t) -> p c t", c=DC)
        GS = at(R0 + 8192, DC * NB * S).rearrange("p (c t) -> p c t", c=DC)
        DU = at(R0 + 16384, DC * NB * S).rearrange("p (c t) -> p c t", c=DC)
        D = at(R0 + 24576, DC * NB * S).rearrange("p (c t) -> p c t", c=DC)
        CV = at(49192, 2 * NB * S).rearrange("p (k t) -> p k t", k=2)
        WX = at(51240, DC * SP_).rearrange("p (c n) -> p c n", c=DC)
        AC = at(51880, P)
        CP = at(52008, DC * 7).rearrange("p (c n) -> p c n", n=7)
        LW = at(52064, 1, SP_)
        WD = at(52065, DI, RK)
        o = R0 + 32768
        SS = at(o, NB * S, SP_)
        SQ = at(o + 1024, NB * S, SP_)
        RMS = at(o + 2048, NB * S, SP_)
        PN = at(o + 3072, NB * S, SP_)
        MXB = at(o + 1024, 2 * NB * S).rearrange("p (k t) -> p k t", k=2)
        BR = at(49192, NB * S)
        CR = at(50216, NB * S)
        GN, AN = 6, 3
        G = at(o, GN * S).rearrange("p (k t) -> p k t", k=GN)
        DA = at(o + GN * S, AN * S).rearrange("p (k t) -> p k t", k=AN)
        DB = at(o + (GN + AN) * S, 2 * S).rearrange("p (k t) -> p k t", k=2)
        HS = [at(51240, S), at(52065, S), at(52577, S)]
        YT = XN[:, 0, :]
        WO = at(4096, DC * E).rearrange("p (c n) -> p c n", c=DC)
        o = R0 + 16384
        BF = at(o, NE * RR * E // P).rearrange("p (c n) -> p c n", c=NE * RR // P); o += NE * RR * E // P
        BW = at(o, EC * E).rearrange("p (c n) -> p c n", c=EC); o += EC * E
        LA = at(o, EC * LC).rearrange("p (c n) -> p c n", c=EC); o += EC * LC
        BB = at(o, E, 1); o += E
        LG = at(o, NT * LC).rearrange("p (i n) -> p i n", i=NT); o += NT * LC
        PB = at(o, NT * NE).rearrange("p (i n) -> p i n", i=NT); o += NT * NE
        OH1 = at(o, NT * NE).rearrange("p (i n) -> p i n", i=NT); o += NT * NE
        OH2 = at(o, NT * NE).rearrange("p (i n) -> p i n", i=NT); o += NT * NE
        V8 = at(o, NT * 8).rearrange("p (i n) -> p i n", i=NT); o += NT * 8
        I8 = at(o, NT * 8).bitcast(U32).rearrange("p (i n) -> p i n", i=NT); o += NT * 8
        IF = at(o, NT * 2).rearrange("p (i n) -> p i n", i=NT); o += NT * 2
        W12 = at(o, NT * 2).rearrange("p (i n) -> p i n", i=NT); o += NT * 2
        R8 = at(o, 4 * NT).rearrange("p (q i) -> p q i", q=4); o += 4 * NT
        Z = at(o, 2 * NE * RR).rearrange("p (k e r) -> p k e r", k=2, e=NE)
        ZF = at(o, 2 * NE * RR).rearrange("p (k c n) -> p k c n", k=2, c=8); o += 2 * NE * RR
        ZT = at(o, 2 * NE * RR).rearrange("p (k c n) -> p k c n", k=2, c=8); o += 2 * NE * RR
        assert o <= R0 + 32768

        ld_x = [sem("ld_x0"), sem("ld_x1")]
        ld_const, ld_qkv, ld_w3, ld_wi, ld_scan, ld_wo, ld_moe = (
            sem(n) for n in ("ld_const", "ld_qkv", "ld_w3", "ld_wi", "ld_scan", "ld_wo", "ld_moe"))
        ld_w12 = [sem("ld_w12a"), sem("ld_w12b")]
        init_done = sem("init_done")
        ln_var, ln_rstd, ln_xn, ln_tr, ln_ev = (sem(n) for n in ("ln_var", "ln_rstd", "ln_xn", "ln_tr", "ln_ev"))
        qkv_done, rope_read, rope_done, v_done = (sem(n) for n in ("qkv_done", "rope_read", "rope_done", "v_done"))
        sk_ready, sk_tr, qt_ev = (sem(n) for n in ("sk_ready", "sk_tr", "qt_ev"))
        max_ps, max_read, ms_ready, mt_tr, mt_ev, ld_rows = (
            sem(n) for n in ("max_ps", "max_read", "ms_ready", "mt_tr", "mt_ev", "ld_rows"))
        st_ps, exp_done, pv_done, os_ev, et_tr, et_used, x_attn = (
            sem(n) for n in ("st_ps", "exp_done", "pv_done", "os_ev", "et_tr", "et_used", "x_attn"))
        am3_done, w3_v, w3_t, w3_add, w3_dq, w3_tr, w3_ev = (
            sem(n) for n in ("am3_done", "w3_v", "w3_t", "w3_add", "w3_dq", "w3_tr", "w3_ev"))
        nf_v, dq_done, dq_tr, dq_ev, gu_ps, silu_done, ht_done, y_ps, x_ffn = (
            sem(n) for n in ("nf_v", "dq_done", "dq_tr", "dq_ev", "gu_ps", "silu_done", "ht_done", "y_ps", "x_ffn"))
        u_ps, conv_done, u_done, g_ps, gs_done, ssm_ps, ss_ev, sq_done, ms_ps, rr_done, pn_done = (
            sem(n) for n in ("u_ps", "conv_done", "u_done", "g_ps", "gs_done", "ssm_ps", "ss_ev", "sq_done",
                             "ms_ps", "rr_done", "pn_done"))
        dt_ps, sp_done, mx_done, d_done, du_done, bc_ps, bc_ev = (
            sem(n) for n in ("dt_ps", "sp_done", "mx_done", "d_done", "du_done", "bc_ps", "bc_ev"))
        drep, durep, da_done, dbu_done, scan_done, g_done, ysum, y_read, y_done = (
            sem(n) for n in ("drep", "durep", "da_done", "dbu_done", "scan_done", "g_done", "ysum", "y_read", "y_done"))
        abs_done = sem("abs_done")
        wo_ps, x_scan = sem("wo_ps"), sem("x_scan")
        lg_ps, lg_ev, lg_sub, lg_exp, route_done, z_done, z_tr, z_ev, out_ps, out_done, st_out = (
            sem(n) for n in ("lg_ps", "lg_ev", "lg_sub", "lg_exp", "route_done", "z_done", "z_tr", "z_ev", "out_ps",
                             "out_done", "st_out"))
        dve_step, act_step, pool_step = sem("dve_step"), sem("act_step"), sem("pool_step")

        ROWS_LD = 2 * REP * 16

        class Steps:

            def __init__(self, eng, s):
                self.eng, self.s, self.n = eng, s, 0

            def step(self, ins):
                self.n += 1
                ins.then_inc(self.s, 1)
                return self.n

            def wait(self, n=None):
                self.eng.wait_ge(self.s, self.n if n is None else n)

        block = ctx.enter_context(nc.Block())
        V, A, G_, T = nc.vector, nc.scalar, nc.gpsimd, nc.tensor
        ht_rows = lambda h: min(P, HF - h * P)
        w3_cols = lambda c: (c * BANK, min(BANK, 4 * HF - c * BANK))
        W3C = -(-4 * HF // BANK)
        pairs = [dc + half * DC for dc in range(DC) for half in range(2)]

        @block.sync
        def _(sp):
            sp.dma_start(C, cst).then_inc(ld_const, 16)
            xv = x.rearrange("(i p) e -> p i e", p=P)
            sp.dma_start(X[:, 0:TS_, :], xv[:, 0:TS_, :]).then_inc(ld_x[0], 16)
            sp.dma_start(WQ, wqkv.rearrange("(c p) n -> p c n", p=P)).then_inc(ld_qkv, 16)
            sp.dma_start(BQ, bqkv).then_inc(ld_qkv, 16)
            sp.dma_start(X[:, TS_:NT, :], xv[:, TS_:NT, :]).then_inc(ld_x[1], 16)
            if STOP >= 2:
                sp.dma_start(W3F.rearrange("p (j n) -> p j n", j=2),
                             w3.rearrange("(j p r) h -> p j (r h)", p=P, r=2)).then_inc(ld_w3, 16)

            def load_w12(h):
                n = ht_rows(h)
                sp.dma_start(WR[0:n, h % 2, 0, :], w1[h * P:h * P + n, :]).then_inc(ld_w12[h % 2], 16)
                sp.dma_start(WR[0:n, h % 2, 1, :], w2[h * P:h * P + n, :]).then_inc(ld_w12[h % 2], 16)

            if STOP >= 2:
                load_w12(0)
                load_w12(1)
            if STOP >= 3:
                sp.dma_start(WX, wx.rearrange("(c p) n -> p c n", p=P)).then_inc(ld_scan, 16)
                sp.dma_start(AC, acol).then_inc(ld_scan, 16)
                sp.dma_start(CP, conv.rearrange("(c p) n -> p c n", p=P)).then_inc(ld_scan, 16)
                sp.dma_start(LW, lnw).then_inc(ld_scan, 16)
                sp.dma_start(WD, wdt).then_inc(ld_scan, 16)
            for g in range(NG):
                sp.wait_ge(mt_ev, g + 1)
                for m in range(2):
                    for j in range(REP):
                        sp.dma_start(QT[KROWS + m:KROWS + m + 1, g % 4, j, :],
                                     MTS[REP * m + j:REP * m + j + 1, g % 2, :]).then_inc(ld_rows, 16)
            if STOP >= 2:
                for h in range(2, NH):
                    sp.wait_ge(nf_v, h - 1)
                    load_w12(h)
            if STOP >= 3:
                sp.wait_ge(nf_v, NH)
                sp.wait_ge(w3_tr, NH)
                sp.dma_start(WI, w_in.rearrange("(c p) n -> p c n", p=P)).then_inc(ld_wi, 16)
                sp.wait_ge(g_ps, DC)
                sp.dma_start(WO, w_out.rearrange("(c p) n -> p c n", p=P)).then_inc(ld_wo, 16)
            if STOP >= 4:
                sp.wait_ge(ysum, UNITS)
                sp.wait_ge(dbu_done, UNITS)
                sp.dma_start(BF, lora_b.rearrange("(c p) n -> p c n", p=P)).then_inc(ld_moe, 16)
                sp.dma_start(BW, base_w.rearrange("(c p) n -> p c n", p=P)).then_inc(ld_moe, 16)
                sp.dma_start(LA, lora_a.rearrange("(c p) n -> p c n", p=P)).then_inc(ld_moe, 16)
                sp.dma_start(BB, base_b).then_inc(ld_moe, 16)
            ov = out.rearrange("(i p) e -> p i e", p=P)
            if STOP >= 4:
                for i in range(NT):
                    sp.wait_ge(out_done, i + 1)
                    sp.dma_start(ov[:, i, :], X[:, i, :]).then_inc(st_out, 16)
                sp.wait_ge(st_out, 16 * NT)
            else:
                s_, n_ = {1: (x_attn, NG), 2: (x_ffn, NT), 3: (x_scan, NT)}[STOP]
                sp.wait_ge(s_, n_)
                sp.dma_start(ov, X).then_inc(st_out, 16)
                sp.wait_ge(st_out, 16)

        @block.vector
        def _(dve):
            own = Steps(dve, dve_step)

            def layernorm(k):
                for half in range(2):
                    tiles = range(TS_ * half, TS_ * half + TS_)
                    if k == 0:
                        dve.wait_ge(ld_x[half], 16)
                    elif half == 0:
                        dve.wait_ge((None, x_attn, x_ffn, x_scan)[k], (None, NG, NT, NT)[k])
                    for i in tiles:
                        n = own.step(V.bn_stats(ST6[:, i, :], X[:, i, :]))
                    for i in tiles:
                        own.wait(n - TS_ + 1 + i % TS_)
                        m = own.step(V.bn_aggr(MV[:, i, :], ST6[:, i, :]))
                    own.wait(m)
                    V.tensor_scalar(VARE[:, tiles[0]:tiles[0] + TS_], MV[:, tiles[0]:tiles[0] + TS_, 1], 1e-5, None,
                                    ALU.add).then_inc(ln_var, 1)
                for i in range(NT):
                    if i % TS_ == 0:
                        dve.wait_ge(ln_rstd, 2 * k + i // TS_ + 1)
                    if NT * k + i >= 2:
                        dve.wait_ge(ln_tr, NT * k + i - 1)
                    V.tensor_scalar(XN[:, i % 2, :], X[:, i, :], MV[:, i, 0:1], RSTD[:, i:i + 1],
                                    ALU.subtract, ALU.mult).then_inc(ln_xn, 1)

            dve.wait_ge(ld_const, 16)
            V.tensor_copy(identb, ident).then_inc(init_done, 1)
            V.memset(V1, 0.0).then_inc(init_done, 1)
            dve.wait_ge(init_done, 2)
            V.memset(V1[:, :, :, HD:HD + 1], 1.0).then_inc(init_done, 1)
            V.memset(QT[KROWS:KROWS + 2, :, REP, :], 1.0).then_inc(init_done, 1)
            layernorm(0)

            def rope(i):
                base = (i % 2) * 2 * BANK
                dve.wait_ge(qkv_done, i + 1)
                ps = psum[:, base:base + QK].rearrange("p (h d) -> p h d", d=HD)
                t = i % TS_
                cos, sin = (const(n)[:, t * HD:t * HD + HD].unsqueeze(1).broadcast_to([P, QK // HD, HD])
                            for n in ("cos", "sin"))
                if i:
                    dve.wait_ge(rope_done, i)
                own.step(V.tensor_tensor(QC, ps, cos, ALU.mult))
                V.tensor_tensor(QS, ps, sin, ALU.mult).then_inc(rope_read, 1)
                dve.wait_ge(rope_read, i + 1)
                r = R[:, i, :].rearrange("p (h d) -> p h d", d=HD)
                V.tensor_tensor(r[:, :, 0:HD // 2], QC[:, :, 0:HD // 2], QS[:, :, HD // 2:HD], ALU.subtract)
                V.tensor_tensor(r[:, :, HD // 2:HD], QS[:, :, 0:HD // 2], QC[:, :, HD // 2:HD], ALU.add)\
                 .then_inc(rope_done, 1)

            for i in range(NT):
                rope(i)

            def row_max(g, t):
                if t == 0 and g >= 2:
                    dve.wait_ge(ms_ready, g - 1)
                for j in range(REP):
                    n = (g * TS_ + t) * REP + j
                    dve.wait_ge(max_ps, n + 1)
                    V.tensor_reduce(MX[:, g % 2, t, j:j + 1], bank(n % 2), AXX, ALU.max, negate=True)\
                     .then_inc(max_read, 1)

            def evac_stack(g, r):
                n = 3 * g + r
                dve.wait_ge(sk_tr, n + 1)
                w = 2 if r < 2 else 1
                V.tensor_copy(QT[0:KROWS, g % 4, 2 * r:2 * r + w, :],
                              bank(7)[0:KROWS].bitcast(BF16)[:, 0:w * S].rearrange("p (s t) -> p s t", s=w))\
                 .then_inc(qt_ev, 1)

            def finish(g):
                b, kv = g // KV, g % KV
                dve.wait_ge(et_tr, g + 1)
                o_ps = bank(7).rearrange("p (t j d) -> p t j d", t=TS_, d=32)
                if g:
                    dve.wait_ge(et_used, g)
                    dve.wait_ge(x_attn, g)
                own.step(V.reciprocal(REC, o_ps[:, :, :, HD]))
                own.wait()
                V.tensor_tensor(TMP, o_ps[:, :, :, 0:HD],
                                REC.unsqueeze(3).broadcast_to([P, TS_, REP, HD]), ALU.mult).then_inc(et_used, 1)
                dve.wait_ge(et_used, g + 1)
                xs = X[:, TS_ * b:TS_ * b + TS_, REP * HD * kv:REP * HD * kv + REP * HD]
                V.tensor_tensor(xs, xs, TMP.rearrange("p t j d -> p t (j d)"), ALU.add).then_inc(x_attn, 1)

            for n in range(-3, NG + 1):
                for t in range(TS_):
                    if 0 <= n + 2 < NG:
                        row_max(n + 2, t)
                    if 0 <= n + 3 < NG and t < 3:
                        evac_stack(n + 3, t)
                    if 0 <= n - 1 and t == 3:
                        finish(n - 1)
            if STOP < 2:
                return

            dve.wait_ge(et_tr, NG)
            dve.wait_ge(pv_done, NG * TS_)
            dve.wait_ge(ld_w3, 16)
            own.step(V.tensor_reduce(AM3[:, 0, :], W3F.rearrange("p (n k) -> p n k", k=BLK), AXX, ALU.max,
                                     apply_absolute_value=True))
            own.wait()
            own.step(V.tensor_scalar(AM3[:, 1, :], AM3[:, 0, :], 0.0, None, ALU.is_equal))
            own.wait()
            own.step(V.tensor_tensor(AM3[:, 2, :], AM3[:, 0, :], AM3[:, 1, :], ALU.add))
            own.wait()
            V.reciprocal(AM3[:, 3, :], AM3[:, 2, :]).then_inc(am3_done, 1)
            layernorm(1)

            def nf4(h):
                n = ht_rows(h)
                am = AM[0:n]
                raw = WR[0:n, h % 2].rearrange("p w e -> p (w e)").rearrange("p (b k) -> p b k", k=BLK)
                dve.wait_ge(ld_w12[h % 2], 32 * (h // 2 + 1))
                if h:
                    dve.wait_ge(dq_done, h)
                own.step(V.tensor_reduce(am[:, 0, :], raw, AXX, ALU.max, apply_absolute_value=True))
                own.wait()
                own.step(V.tensor_scalar(am[:, 1, :], am[:, 0, :], 0.0, None, ALU.is_equal))
                own.wait()
                own.step(V.tensor_tensor(am[:, 2, :], am[:, 0, :], am[:, 1, :], ALU.add))
                own.wait()
                own.step(V.reciprocal(am[:, 3, :], am[:, 2, :]))
                own.wait()
                v, acc = NV[0:n], NACC[0:n]
                b3 = lambda a: a.rearrange("p (b k) -> p b k", k=BLK)
                rb = lambda a: a.unsqueeze(2).broadcast_to([n, 2 * E // BLK, BLK])
                V.tensor_tensor(b3(v), raw, rb(am[:, 3, :]), ALU.mult).then_inc(nf_v, 1)
                dve.wait_ge(nf_v, h + 1)

                def edge(i):
                    return own.step(V.tensor_scalar(NTB[0:n, i % 2, :], v, float(EDGES[i]), float(STEPS[i]),
                                                    ALU.is_gt, ALU.mult))

                edge(0)
                last = edge(1)
                own.wait(last)
                added = own.step(V.scalar_tensor_tensor(acc, NTB[0:n, 0, :], float(NF4[0]), NTB[0:n, 1, :],
                                                        ALU.add, ALU.add))
                own.wait(added)
                made = edge(2)
                for i in range(3, len(EDGES) + 1):
                    before = added
                    if i < len(EDGES):
                        nxt = edge(i)
                    own.wait(max(made, before))
                    added = own.step(V.tensor_tensor(acc, acc, NTB[0:n, (i - 1) % 2, :], ALU.add))
                    if i < len(EDGES):
                        made = nxt
                        own.wait(added)
                own.wait(added)
                if h >= 2:
                    dve.wait_ge(dq_tr, h - 1)
                V.tensor_tensor(b3(DQ[0:n, h % 2].rearrange("p w e -> p (w e)")), b3(acc), rb(am[:, 0, :]), ALU.mult)\
                 .then_inc(dq_done, 1)

            def w3_finish(c):
                a, n = w3_cols(c)
                dve.wait_ge(w3_add, (len(EDGES) - 1) * (c + 1))
                k0 = float(np.float32(float(NF4[0]) + float(STEPS.astype(np.float64).sum()) / 2))
                b3 = lambda q: q.rearrange("p (b k) -> p b k", k=BLK)
                V.scalar_tensor_tensor(b3(W3F[:, a:a + n]), b3(W3A[:, c % 2, 0:n]), k0,
                                       AM3[:, 0, a // BLK:(a + n) // BLK].unsqueeze(2).broadcast_to([P, n // BLK, BLK]),
                                       ALU.add, ALU.mult).then_inc(w3_dq, 1)

            def hidden(h):
                n = ht_rows(h)
                dve.wait_ge(silu_done, h + 1)
                V.tensor_tensor(HT[0:n, h, :], SG[0:n], bank(4, 2)[0:n], ALU.mult).then_inc(ht_done, 1)

            for h in range(NH + 1):
                if h < NH:
                    nf4(h)
                if h:
                    hidden(h - 1)
                    w3_finish(h - 1)
            for i in range(NT):
                dve.wait_ge(y_ps, i + 1)
                V.tensor_tensor(X[:, i, :], X[:, i, :], bank(i % 2), ALU.add).then_inc(x_ffn, 1)
            if STOP < 3:
                return

            layernorm(2)
            dve.wait_ge(ld_scan, 16 * 5)
            for c in range(DC):
                dve.wait_ge(u_ps, c + 1)
                if c >= 2:
                    dve.wait_ge(u_done, c - 1)
                ps = bank(0, 2).rearrange("p (b t) -> p b t", b=NB)
                cv = CV[:, c % 2, :].rearrange("p (b t) -> p b t", b=NB)
                own.step(V.tensor_scalar(cv, ps, CP[:, c, KC - 1:KC], CP[:, c, KC:KC + 1], ALU.mult, ALU.add))
                for lag in range(1, KC):
                    own.wait()
                    ins = V.scalar_tensor_tensor(cv[:, :, lag:S], ps[:, :, 0:S - lag], CP[:, c, KC - 1 - lag:KC - lag],
                                                 cv[:, :, lag:S], ALU.mult, ALU.add)
                    if lag < KC - 1:
                        own.step(ins)
                    else:
                        ins.then_inc(conv_done, 1)
            dve.wait_ge(rr_done, 1)
            dve.wait_ge(ss_ev, 1)
            V.scalar_tensor_tensor(PN, SS, LW[:, 0:1], RMS, ALU.mult, ALU.mult).then_inc(pn_done, 1)
            dve.wait_ge(pn_done, 1)
            for c in range(DC):
                dve.wait_ge(abs_done, c + 1)
                if c >= 2:
                    dve.wait_ge(d_done, c - 1)
                V.tensor_scalar(MXB[:, c % 2, :], bank(2 * (c % 2), 2), CP[:, c, 5:6], 0.0, ALU.add, ALU.max)\
                 .then_inc(mx_done, 1)
                dve.wait_ge(mx_done, c + 1)
                dve.wait_ge(sp_done, c + 1)
                V.tensor_tensor(D[:, c, :], MXB[:, c % 2, :], CV[:, c % 2, :], ALU.add).then_inc(d_done, 1)
                dve.wait_ge(d_done, c + 1)
                V.tensor_tensor(DU[:, c, :], D[:, c, :], U[:, c, :], ALU.mult).then_inc(du_done, 1)
            dve.wait_ge(bc_ev, 2)

            def times_b(m):
                b = m // 16 % NB
                dve.wait_ge(durep, m + 1)
                if m >= 2:
                    dve.wait_ge(scan_done, m - 1)
                V.tensor_tensor(DB[:, m % 2, :], bank(4 + m % 3), BR[:, b * S:b * S + S], ALU.mult).then_inc(dbu_done, 1)

            def scan(m):
                dve.wait_ge(dbu_done, m + 1)
                dve.wait_ge(da_done, m + 1)
                if m >= 3:
                    dve.wait_ge(g_done, m - 2)
                V.tensor_tensor_scan(HS[m % 3], DA[:, m % AN, :], DB[:, m % 2, :], 0.0, ALU.mult, ALU.add)\
                 .then_inc(scan_done, 1)

            def gate(k):
                c, b = k // NB, k % NB
                dve.wait_ge(ysum, 16 * (k + 1))
                if k:
                    dve.wait_ge(y_done, k)
                V.scalar_tensor_tensor(YT, U[:, c, b * S:b * S + S], CP[:, c, 6:7], bank(7), ALU.mult, ALU.add)\
                 .then_inc(y_read, 1)
                dve.wait_ge(y_read, k + 1)
                g = GS[:, c, b * S:b * S + S]
                V.tensor_tensor(g, g, YT, ALU.mult).then_inc(y_done, 1)

            times_b(0)
            for m in range(UNITS):
                if m + 1 < UNITS:
                    times_b(m + 1)
                scan(m)
                if m >= 16 and m % 16 == 2:
                    gate(m // 16 - 1)
            gate(UNITS // 16 - 1)
            for i in range(NT):
                dve.wait_ge(wo_ps, i + 1)
                V.tensor_tensor(X[:, i, :], X[:, i, :], bank(i % 2), ALU.add).then_inc(x_scan, 1)
            if STOP < 4:
                return

            layernorm(3)
            r8 = lambda q: R8[:, q, :]
            rb = lambda a, n: a.unsqueeze(2).broadcast_to([P, NT, n])
            dve.wait_ge(lg_ev, NT)
            own.step(V.tensor_reduce(r8(0), LG[:, :, RR:LC], AXX, ALU.max))
            own.wait()
            V.tensor_tensor(PB, LG[:, :, RR:LC], rb(r8(0), NE), ALU.subtract).then_inc(lg_sub, 1)
            dve.wait_ge(lg_exp, 1)
            own.step(V.reduce_sum(r8(1), PB, AXX))
            own.wait()
            own.step(V.reciprocal(r8(2), r8(1)))
            own.wait()
            own.step(V.tensor_tensor(OH1, PB, rb(r8(2), NE), ALU.mult))
            own.wait()
            for i in range(NT):
                own.step(V.max(V8[:, i, :], OH1[:, i, :]))
            for i in range(NT):
                own.wait(own.n - i - NT + i + 1 if i == 0 else None)
                own.step(V.max_index(I8[:, i, :], V8[:, i, :], OH1[:, i, :]))
            own.wait()
            own.step(V.tensor_copy(IF, I8[:, :, 0:2]))
            own.step(V.tensor_tensor(r8(3), V8[:, :, 0], V8[:, :, 1], ALU.add))
            own.wait()
            own.step(V.tensor_scalar(r8(0), r8(3), 1e-6, None, ALU.add))
            own.wait()
            own.step(V.reciprocal(r8(1), r8(0)))
            own.wait()
            own.step(V.tensor_scalar(r8(2), r8(1), 0.5, None, ALU.mult))
            own.wait()
            own.step(V.tensor_tensor(W12, V8[:, :, 0:2], rb(r8(2), 2), ALU.mult))
            iota = const("iota").unsqueeze(1).broadcast_to([P, NT, NE])
            for k, oh in enumerate((OH1, OH2)):
                own.wait()
                own.step(V.tensor_tensor(oh, iota, rb(IF[:, :, k], NE), ALU.is_equal))
                own.wait()
                own.step(V.tensor_tensor(oh, oh, rb(W12[:, :, k], NE), ALU.mult))
            own.wait()
            own.step(V.tensor_tensor(PB, OH1, OH2, ALU.add))
            own.wait()

            def low_rank(i):
                if i >= 2:
                    dve.wait_ge(z_tr, i - 1)
                V.tensor_tensor(Z[:, i % 2], PB[:, i, :].unsqueeze(2).broadcast_to([P, NE, RR]),
                                LG[:, i, 0:RR].unsqueeze(1).broadcast_to([P, NE, RR]), ALU.mult).then_inc(z_done, 1)

            for i in range(NT + 1):
                if i < NT:
                    low_rank(i)
                if i:
                    dve.wait_ge(out_ps, i)
                    V.tensor_tensor(X[:, i - 1, :], X[:, i - 1, :], bank((i - 1) % 2), ALU.add).then_inc(out_done, 1)

        @block.gpsimd
        def _(pool):
            own = Steps(pool, pool_step)

            def rstd(k):
                for half in range(2):
                    pool.wait_ge(ln_var, 2 * k + half + 1)
                    G_.tensor_tensor(RSTD[:, TS_ * half:TS_ * half + TS_], VARE[:, TS_ * half:TS_ * half + TS_],
                                     const("mhalf"), ALU.pow).then_inc(ln_rstd, 1)

            pool.wait_ge(ld_const, 16)
            rstd(0)

            def stack(g):
                b, kv = g // KV, g % KV
                r = R[:, TS_ * b:TS_ * b + TS_, GC * kv:GC * kv + GC].rearrange("p t (s d) -> p t s d", d=HD)
                sk = SK[:, g % 2]
                pool.wait_ge(rope_done, TS_ * (b + 1))
                if g >= 2:
                    pool.wait_ge(sk_tr, 3 * (g - 1))
                if g:
                    pool.wait_ge(sk_ready, g)
                own.step(G_.tensor_copy(sk[:, :, :, 0, :], r))
                own.wait()
                own.step(G_.tensor_tensor(RES, r, sk[:, :, :, 0, :], ALU.subtract))
                own.wait()
                own.step(G_.tensor_copy(sk[:, :, :, 4, :], RES))
                own.wait()
                own.step(G_.tensor_tensor(LO, RES, sk[:, :, :, 4, :], ALU.subtract))
                q, k = sk[:, :, 0:REP], sk[:, :, REP]
                for dst, src in ((1, 0), (2, 0), (3, 4)):
                    own.step(G_.tensor_copy(q[:, :, :, dst, :], q[:, :, :, src, :]))
                for dst, src in ((1, 4), (3, 0), (5, 0)):
                    n = own.step(G_.tensor_copy(k[:, :, dst, :], k[:, :, src, :]))
                own.wait()
                own.step(G_.tensor_copy(q[:, :, :, 5, :], LO[:, :, 0:REP]))
                own.wait()
                G_.tensor_copy(k[:, :, 2, :], LO[:, :, REP]).then_inc(sk_ready, 1)

            def split_max(g):
                pool.wait_ge(max_read, TS_ * REP * (g + 1))
                if g >= 2:
                    pool.wait_ge(mt_tr, g - 1)
                own.step(G_.tensor_copy(MS[:, g % 2, :, 0, :], MX[:, g % 2]))
                own.wait()
                G_.tensor_tensor(MS[:, g % 2, :, 1, :], MX[:, g % 2], MS[:, g % 2, :, 0, :], ALU.subtract)\
                  .then_inc(ms_ready, 1)

            for n in range(-4, NG):
                if n + 4 < NG:
                    stack(n + 4)
                if 0 <= n + 2 < NG:
                    split_max(n + 2)
            if STOP < 2:
                return

            rstd(1)
            pool.wait_ge(am3_done, 1)
            for c in range(W3C):
                a, n = w3_cols(c)
                b3 = lambda q: q.rearrange("p (b k) -> p b k", k=BLK)
                if c:
                    pool.wait_ge(w3_t, len(EDGES) * c)
                G_.tensor_tensor(b3(W3V[:, 0:n]), b3(W3F[:, a:a + n]),
                                 AM3[:, 3, a // BLK:(a + n) // BLK].unsqueeze(2).broadcast_to([P, n // BLK, BLK]),
                                 ALU.mult).then_inc(w3_v, 1)
                acc = W3A[:, c % 2, 0:n]
                for i in range(1, len(EDGES)):
                    k = (len(EDGES) - 1) * c + i
                    pool.wait_ge(w3_t, len(EDGES) * c + i + 1)
                    if k > 1:
                        pool.wait_ge(w3_add, k - 1)
                    G_.tensor_tensor(acc, acc, W3T[:, i % 2, 0:n], ALU.add).then_inc(w3_add, 1)
            if STOP < 3:
                return
            rstd(2)
            for m in range(UNITS):
                b = m // 16 % NB
                pool.wait_ge(bc_ev, 2)
                pool.wait_ge(scan_done, m + 1)
                if m >= GN:
                    pool.wait_ge(ysum, m - GN + 1)
                G_.tensor_tensor(G[:, m % GN, :], HS[m % 3], CR[:, b * S:b * S + S], ALU.mult).then_inc(g_done, 1)
            if STOP < 4:
                return
            rstd(3)

        @block.scalar
        def _(act):
            own = Steps(act, act_step)

            def evac_ln(k):
                for i in range(NT):
                    act.wait_ge(ln_tr, NT * k + i + 1)
                    A.activation(XNT[:, :, i * P:i * P + P], bank(6 + i % 2).rearrange("p (c t) -> p c t", c=EC), ACT.Copy)\
                     .then_inc(ln_ev, 1)

            evac_ln(0)
            act.wait_ge(init_done, 4)
            for i in range(NT):
                act.wait_ge(rope_read, i + 1)
                base = (i % 2) * 2 * BANK + QK
                A.activation(V1[:, i, :, 0:HD], psum[:, base:base + KV * HD].rearrange("p (k d) -> p k d", d=HD), ACT.Copy)\
                 .then_inc(v_done, 1)

            def exps(step):
                if step >= 3:
                    act.wait_ge(pv_done, step - 2)
                for q in range(2):
                    n = 2 * step + q
                    act.wait_ge(st_ps, n + 1)
                    A.activation(PR[:, step % 3, 2 * q:2 * q + 2, :],
                                 bank(2 + 2 * q, 2).rearrange("p (j t) -> p j t", j=2), ACT.Exp, scale=HD ** -0.5)\
                     .then_inc(exp_done, 1)

            for n in range(-1, NG + 1):
                for t in range(TS_):
                    if 0 <= n < NG:
                        exps(TS_ * n + t)
                    if t == 0:
                        if 0 <= n + 1 < NG:
                            act.wait_ge(mt_tr, n + 2)
                            if n + 1 >= 2:
                                act.wait_ge(ld_rows, ROWS_LD * n)
                            A.activation(MTS[0:2 * REP, (n + 1) % 2, :], bank(7)[0:2 * REP].bitcast(BF16)[:, 0:S], ACT.Copy)\
                             .then_inc(mt_ev, 1)
                        if n >= 1:
                            act.wait_ge(pv_done, TS_ * n)
                            if n >= 3:
                                act.wait_ge(et_tr, n - 2)
                            A.activation(OS[:, (n - 1) % 2, :], bank(6), ACT.Copy).then_inc(os_ev, 1)
            if STOP < 2:
                return

            evac_ln(1)

            def w3_chunk(c):
                a, n = w3_cols(c)
                act.wait_ge(w3_v, c + 1)
                ne = len(EDGES)

                def sign(i):
                    if ne * c + i >= 2:
                        act.wait_ge(w3_t, ne * c + i - 1)
                    return own.step(A.activation(W3M[:, i % 2, 0:n], W3V[:, 0:n], ACT.Sign, scale=float(SIGNS[i][0]),
                                                 bias=const("edge_bias")[:, i:i + 1]))

                nxt = sign(0)
                for i in range(ne):
                    made = nxt
                    if i + 1 < ne:
                        nxt = sign(i + 1)
                    own.wait(made)
                    if i == 0:
                        dst = W3A[:, c % 2, 0:n]
                        if c >= 2:
                            act.wait_ge(w3_dq, c - 1)
                    else:
                        dst = W3T[:, i % 2, 0:n]
                        k = (ne - 1) * c + i
                        if k - 2 >= 1:
                            act.wait_ge(w3_add, k - 2)
                    A.activation(dst, W3M[:, i % 2, 0:n], ACT.Copy, scale=float(STEPS[i]) / 2).then_inc(w3_t, 1)

            for h in range(NH):
                n = ht_rows(h)
                for w in range(2):
                    act.wait_ge(dq_tr, h + 1)
                    if h >= 2:
                        act.wait_ge(gu_ps, h - 1)
                    A.activation(DQT[:, h % 2, w, :, 0:n], bank(w).rearrange("p (c h) -> p c h", c=EC)[:, :, 0:n], ACT.Copy)\
                     .then_inc(dq_ev, 1)
                w3_chunk(h)
                act.wait_ge(gu_ps, h + 1)
                if h:
                    act.wait_ge(ht_done, h)
                A.activation(SG[0:n], bank(2, 2)[0:n], ACT.Silu).then_inc(silu_done, 1)
            for h in range(NH):
                n = ht_rows(h)
                act.wait_ge(w3_tr, h + 1)
                A.activation(DQ3[0:n, h, :].rearrange("p (j q r) -> p j r q", j=2, r=2),
                             bank(6 + h % 2)[0:n].rearrange("p (j r q) -> p j r q", j=2, r=2), ACT.Copy).then_inc(w3_ev, 1)
            if STOP < 3:
                return

            evac_ln(2)
            for c in range(DC):
                act.wait_ge(conv_done, c + 1)
                A.activation(U[:, c, :], CV[:, c % 2, :], ACT.Silu).then_inc(u_done, 1)
                act.wait_ge(g_ps, c + 1)
                A.activation(GS[:, c, :], bank(2, 2), ACT.Silu).then_inc(gs_done, 1)
            act.wait_ge(ssm_ps, 1)
            A.activation(SQ, bank(4, 2)[0:SP_], ACT.Square).then_inc(sq_done, 1)
            A.activation(SS, bank(4, 2)[0:SP_], ACT.Copy).then_inc(ss_ev, 1)
            act.wait_ge(ms_ps, 1)
            own.step(A.activation(RMS, bank(6, 2)[0:SP_], ACT.Ln, bias=const("eps", SP_)))
            own.wait()
            A.activation(RMS, RMS, ACT.Exp, scale=-0.5).then_inc(rr_done, 1)
            for c in range(DC):
                act.wait_ge(dt_ps, c + 1)
                if c >= 2:
                    act.wait_ge(d_done, c - 1)
                A.activation(CV[:, c % 2, :], bank(2 * (c % 2), 2), ACT.Abs, bias=CP[:, c, 5:6]).then_inc(abs_done, 1)
                act.wait_ge(abs_done, c + 1)
                own.step(A.activation(CV[:, c % 2, :], CV[:, c % 2, :], ACT.Exp, scale=-1.0))
                own.wait()
                A.activation(CV[:, c % 2, :], CV[:, c % 2, :], ACT.Ln, bias=const("one")).then_inc(sp_done, 1)
            act.wait_ge(d_done, DC)
            for k, dst in enumerate((BR, CR)):
                act.wait_ge(bc_ps, k + 1)
                A.activation(dst, bank(4 + 2 * k, 2), ACT.Copy).then_inc(bc_ev, 1)
            for m in range(UNITS):
                chunk, i, s = m // 32, m % 4, m // 4 % 4
                act.wait_ge(drep, m + 1)
                if m >= AN:
                    act.wait_ge(scan_done, m - AN + 1)
                A.activation(DA[:, m % AN, :], bank(i), ACT.Exp, scale=AC[:, chunk * 16 + 4 * i + s:chunk * 16 + 4 * i + s + 1])\
                 .then_inc(da_done, 1)
            if STOP < 4:
                return

            evac_ln(3)
            for i in range(NT):
                act.wait_ge(lg_ps, i + 1)
                A.activation(LG[:, i, :], bank(4 + i % 2)[:, 0:LC], ACT.Copy).then_inc(lg_ev, 1)
            act.wait_ge(lg_sub, 1)
            A.activation(PB, PB, ACT.Exp).then_inc(lg_exp, 1)
            for i in range(NT):
                act.wait_ge(z_tr, i + 1)
                if i >= 2:
                    act.wait_ge(out_ps, i - 1)
                A.activation(ZT[:, i % 2], bank(2 + 2 * (i % 2), 2).rearrange("p (c n) -> p c n", c=8), ACT.Copy)\
                 .then_inc(z_ev, 1)

        @block.tensor
        def _(pe):
            def transpose_ln(k):
                for i in range(NT):
                    pe.wait_ge(ln_xn, NT * k + i + 1)
                    if i >= 2:
                        pe.wait_ge(ln_ev, NT * k + i - 1)
                    for c in range(EC):
                        mm = T.transpose(bank(6 + i % 2)[:, c * P:c * P + P], XN[:, i % 2, c * P:c * P + P], ident)
                    mm.then_inc(ln_tr, 1)

            pe.wait_ge(ld_const, 16)
            transpose_ln(0)
            pe.wait_ge(ld_qkv, 32)
            for i in range(NT):
                pe.wait_ge(ln_ev, i + 1)
                if i >= 2:
                    pe.wait_ge(rope_read, i - 1)
                    pe.wait_ge(v_done, i - 1)
                for a, n in ((0, BANK), (BANK, 768 - BANK)):
                    o_ = psum[:, (i % 2) * 2 * BANK + a:(i % 2) * 2 * BANK + a + n]
                    T.matmul(o_, const("ones_row", 1), BQ[:, a:a + n], start=True, stop=False)
                    for c in range(EC):
                        mm = T.matmul(o_, XNT[:, c, i * P:i * P + P], WQ[:, c, a:a + n], start=False, stop=(c == EC - 1))
                mm.then_inc(qkv_done, 1)

            used = {"mt": 0, "qt": 0, "et": 0}

            def bank7_free():
                for s_, n_ in ((mt_ev, used["mt"]), (qt_ev, used["qt"]), (et_used, used["et"])):
                    if n_:
                        pe.wait_ge(s_, n_)

            def turn_stack(g, r):
                pe.wait_ge(sk_ready, g + 1)
                bank7_free()
                used["qt"] += 1
                dst = bank(7)[0:KROWS].bitcast(BF16)
                for s in range(2 * r, min(2 * r + 2, 5)):
                    for t in range(TS_):
                        c = ((s - 2 * r) * TS_ + t) * P
                        mm = T.transpose(dst[:, c:c + P], SKF[:, g % 2, t, s, :], identb)
                mm.then_inc(sk_tr, 1)

            def score_rows(g, t):
                pe.wait_ge(qt_ev, 3 * (g + 1))
                for j in range(REP):
                    n = (g * TS_ + t) * REP + j
                    if n >= 2:
                        pe.wait_ge(max_read, n - 1)
                    T.matmul(bank(n % 2), QT[0:KROWS, g % 4, j, t * P:t * P + P], QT[0:KROWS, g % 4, REP, :],
                             start=True, stop=True).then_inc(max_ps, 1)

            def turn_max(g):
                pe.wait_ge(ms_ready, g + 1)
                bank7_free()
                used["mt"] += 1
                for t in range(TS_):
                    mm = T.transpose(bank(7)[0:2 * REP].bitcast(BF16)[:, t * P:t * P + P], MSF[:, g % 2, t, :], identb)
                mm.then_inc(mt_tr, 1)

            def score_cols(g, t):
                pe.wait_ge(ld_rows, ROWS_LD * (g + 1))
                for q in range(2):
                    n = 2 * (g * TS_ + t) + q
                    if n >= 2:
                        pe.wait_ge(exp_done, n - 1)
                    for j in range(2 * q, 2 * q + 2):
                        mm = T.matmul(bank(2 + j), QT[0:KROWS + 2, g % 4, REP, t * P:t * P + P],
                                      QT[0:KROWS + 2, g % 4, j, :], start=True, stop=True)
                    mm.then_inc(st_ps, 1)

            def values(step):
                g, t = step // TS_, step % TS_
                pe.wait_ge(exp_done, 2 * step + 2)
                if t == 0 and g:
                    pe.wait_ge(os_ev, g)
                for j in range(REP):
                    mm = T.matmul(bank(6)[32 * j:32 * j + 32], V1[:, TS_ * (g // KV) + t, g % KV, :],
                                  PR[:, step % 3, j, :], start=(t == 0), stop=(t == TS_ - 1))
                mm.then_inc(pv_done, 1)

            def turn_out(g):
                pe.wait_ge(os_ev, g + 1)
                bank7_free()
                used["et"] += 1
                for t in range(TS_):
                    mm = T.transpose(bank(7)[:, t * P:t * P + P], OS[:, g % 2, t * P:t * P + P], ident)
                mm.then_inc(et_tr, 1)

            pe.wait_ge(init_done, 4)
            pe.wait_ge(rope_read, NT)
            pe.wait_ge(v_done, NT)
            for n in range(-3, NG + 1):
                for t in range(TS_):
                    if 0 <= n < NG:
                        score_cols(n, t)
                    if 0 <= n + 2 < NG:
                        score_rows(n + 2, t)
                    if 0 <= TS_ * n + t - 1 < TS_ * NG:
                        values(TS_ * n + t - 1)
                    if t == 0 and 0 <= n + 1 < NG:
                        turn_max(n + 1)
                    if t < 3 and 0 <= n + 3 < NG:
                        turn_stack(n + 3, t)
                    if t == 3 and n >= 1:
                        turn_out(n - 1)
            if STOP < 2:
                return

            bank7_free()
            pe.wait_ge(os_ev, NG)
            transpose_ln(1)
            for h in range(NH):
                n = ht_rows(h)
                pe.wait_ge(dq_done, h + 1)
                if h:
                    pe.wait_ge(dq_ev, 2 * h)
                for w in range(2):
                    for c in range(EC):
                        mm = T.transpose(bank(w)[:, c * P:c * P + n], DQ[0:n, h % 2, w, c * P:c * P + P], ident[0:n, 0:n])
                mm.then_inc(dq_tr, 1)
                pe.wait_ge(dq_ev, 2 * (h + 1))
                if h == 0:
                    pe.wait_ge(ln_ev, 2 * NT)
                else:
                    pe.wait_ge(ht_done, h)
                for w in range(2):
                    for b in range(NB):
                        for c in range(EC):
                            mm = T.matmul(bank(2 + 2 * w + b)[0:n], DQT[:, h % 2, w, c, 0:n], XNT[:, c, b * S:b * S + S],
                                          start=(c == 0), stop=(c == EC - 1))
                mm.then_inc(gu_ps, 1)
            pe.wait_ge(w3_dq, W3C)
            for h in range(NH):
                n = ht_rows(h)
                if h >= 2:
                    pe.wait_ge(w3_ev, h - 1)
                for j in range(2):
                    for r in range(2):
                        mm = T.transpose(bank(6 + h % 2)[0:n, (2 * j + r) * P:(2 * j + r) * P + P],
                                         W3R[:, j, r, h * P:h * P + n], ident)
                mm.then_inc(w3_tr, 1)
            pe.wait_ge(ht_done, NH)
            pe.wait_ge(w3_ev, NH)
            for i in range(NT):
                if i >= 2:
                    pe.wait_ge(x_ffn, i - 1)
                for h in range(NH):
                    n = ht_rows(h)
                    mm = T.matmul(bank(i % 2), HT[0:n, h, i * P:i * P + P], DQ3[0:n, h, :], start=(h == 0), stop=(h == NH - 1))
                mm.then_inc(y_ps, 1)
            if STOP < 3:
                return

            transpose_ln(2)
            pe.wait_ge(x_ffn, NT)
            pe.wait_ge(ld_wi, 16)
            pe.wait_ge(ld_scan, 16 * 5)
            pe.wait_ge(ln_ev, 3 * NT)

            def to_ssm(c):
                pe.wait_ge(u_done, c + 1)
                for b in range(NB):
                    mm = T.matmul(bank(4 + b)[0:SP_], WX[:, c, :], U[:, c, b * S:b * S + S], start=(c == 0), stop=(c == DC - 1))
                if c == DC - 1:
                    mm.then_inc(ssm_ps, 1)

            for c in range(DC):
                for half in range(2):
                    if c:
                        pe.wait_ge((conv_done, gs_done)[half], c)
                    for b in range(NB):
                        for e in range(EC):
                            mm = T.matmul(bank(2 * half + b), WI[:, e, half * DI + c * P:half * DI + c * P + P],
                                          XNT[:, e, b * S:b * S + S], start=(e == 0), stop=(e == EC - 1))
                    mm.then_inc((u_ps, g_ps)[half], 1)
                if c >= 1:
                    to_ssm(c - 1)
            to_ssm(DC - 1)
            pe.wait_ge(sq_done, 1)
            for b in range(NB):
                mm = T.matmul(bank(6 + b)[0:SP_], const("mean", SP_), SQ[:, b * S:b * S + S], start=True, stop=True)
            mm.then_inc(ms_ps, 1)
            pe.wait_ge(pn_done, 1)
            pe.wait_ge(gs_done, DC)
            for c in range(DC):
                if c >= 2:
                    pe.wait_ge(sp_done, c - 1)
                    pe.wait_ge(mx_done, c - 1)
                for b in range(NB):
                    mm = T.matmul(bank(2 * (c % 2) + b), WD[:, c * P:c * P + P], PN[0:RK, b * S:b * S + S], start=True, stop=True)
                mm.then_inc(dt_ps, 1)
            for k, a in enumerate((RK, 64)):
                for b in range(NB):
                    mm = T.matmul(bank(4 + 2 * k + b), const("rep")[a:a + NS], PN[a:a + NS, b * S:b * S + S], start=True, stop=True)
                mm.then_inc(bc_ps, 1)
            pe.wait_ge(du_done, DC)
            pe.wait_ge(sp_done, DC)
            pe.wait_ge(bc_ev, 2)

            def sum_states(Q):
                for i in range(4):
                    m = 4 * Q + i
                    s, k = Q % 4, Q // 4
                    if s == 0 and i == 0 and k:
                        pe.wait_ge(y_read, k)
                    pe.wait_ge(g_done, m + 1)
                    T.matmul(bank(7)[32 * i:32 * i + 32], const("gather")[:, 32 * s:32 * s + 32], G[:, m % GN, :],
                             start=(s == 0), stop=(s == 3)).then_inc(ysum, 1)

            for Q in range(UNITS // 4 + 1):
                if Q < UNITS // 4:
                    c, b, s = Q // 8, Q // 4 % NB, Q % 4
                    for i in range(4):
                        m = 4 * Q + i
                        if Q:
                            pe.wait_ge(da_done, m - 3)
                        T.matmul(bank(i), const("spread")[32 * i:32 * i + 32, s * P:s * P + P],
                                 D[32 * i:32 * i + 32, c, b * S:b * S + S], start=True, stop=True).then_inc(drep, 1)
                    for i in range(4):
                        m = 4 * Q + i
                        if m >= 3:
                            pe.wait_ge(dbu_done, m - 2)
                        T.matmul(bank(4 + m % 3), const("spread")[32 * i:32 * i + 32, s * P:s * P + P],
                                 DU[32 * i:32 * i + 32, c, b * S:b * S + S], start=True, stop=True).then_inc(durep, 1)
                if Q:
                    sum_states(Q - 1)
            pe.wait_ge(ld_wo, 16)
            pe.wait_ge(y_done, UNITS // 16)
            for i in range(NT):
                if i >= 2:
                    pe.wait_ge(x_scan, i - 1)
                for c in range(DC):
                    mm = T.matmul(bank(i % 2), GS[:, c, i * P:i * P + P], WO[:, c, :], start=(c == 0), stop=(c == DC - 1))
                mm.then_inc(wo_ps, 1)
            if STOP < 4:
                return

            transpose_ln(3)
            pe.wait_ge(x_scan, NT)
            pe.wait_ge(ld_moe, 64)
            pe.wait_ge(ln_ev, 4 * NT)
            for i in range(NT):
                if i >= 2:
                    pe.wait_ge(lg_ev, i - 1)
                for c in range(EC):
                    mm = T.matmul(bank(4 + i % 2)[:, 0:LC], XNT[:, c, i * P:i * P + P], LA[:, c, :], start=(c == 0), stop=(c == EC - 1))
                mm.then_inc(lg_ps, 1)
            pe.wait_ge(lg_ev, NT)
            for i in range(NT + 1):
                if i < NT:
                    pe.wait_ge(z_done, i + 1)
                    if i >= 2:
                        pe.wait_ge(z_ev, i - 1)
                    for c in range(8):
                        mm = T.transpose(bank(2 + 2 * (i % 2), 2)[:, c * P:c * P + P], ZF[:, i % 2, c, :], ident)
                    mm.then_inc(z_tr, 1)
                    if i >= 2:
                        pe.wait_ge(out_done, i - 1)
                    T.matmul(bank(i % 2), const("ones_row", 1), BB, start=True, stop=False)
                    for c in range(EC):
                        T.matmul(bank(i % 2), XNT[:, c, i * P:i * P + P], BW[:, c, :], start=False, stop=False)
                if i:
                    pe.wait_ge(z_ev, i)
                    for c in range(8):
                        mm = T.matmul(bank((i - 1) % 2), ZT[:, (i - 1) % 2, c, :], BF[:, c, :], start=False, stop=(c == 7))
                    mm.then_inc(out_ps, 1)


def kernel(**inputs):
    import concourse.bacc as _bacc
    from concourse.bass_utils import run_bass_kernel_spmd as _run

    STOP = 4
    a = {k: np.asarray(v) for k, v in inputs.items()}
    q = a["L0_attn_wq"].reshape(E, KV, REP * HD)
    k = a["L0_attn_wk"].reshape(E, KV, HD)
    bq, bk = a["L0_attn_bq"].reshape(1, KV, REP * HD), a["L0_attn_bk"].reshape(1, KV, HD)
    wqkv = np.concatenate([np.concatenate([q, k], 2).reshape(E, QK), a["L0_attn_wv"]], 1)
    bqkv = np.concatenate([np.concatenate([bq, bk], 2).reshape(1, QK), a["L0_attn_bv"].reshape(1, KV * HD)], 1)
    conv = np.concatenate([a["L1_attn_conv_w"], a["L1_attn_conv_b"][:, None], a["L1_attn_dt_bias"][:, None],
                           a["L1_attn_D_param"][:, None]], 1)
    wx = a["L1_attn_Wx"].T
    wxp = np.zeros((DI, SP_), np.float32)
    wxp[:, 0:RK + NS] = wx[:, 0:RK + NS]
    wxp[:, 64:SP_] = wx[:, RK + NS:]
    lnw = np.zeros((SP_, 1), np.float32)
    lnw[0:RK, 0] = a["L1_attn_dt_ln_w"]
    lnw[RK:RK + NS, 0] = a["L1_attn_b_ln_w"]
    lnw[64:SP_, 0] = a["L1_attn_c_ln_w"]
    arrays = {
        "x": a["L0_attn_x"].reshape(NB * S, E), "cst": CONST, "wqkv": wqkv, "bqkv": bqkv,
        "w1": a["L0_ffn_w1"], "w2": a["L0_ffn_w2"], "w3": a["L0_ffn_w3"],
        "w_in": a["L1_attn_W_in"].T, "conv": conv, "wx": wxp, "lnw": lnw, "wdt": a["L1_attn_Wdt"].T,
        "acol": a["L1_attn_A"].reshape(DI * NS // P, P).T, "w_out": a["L1_attn_W_out"].T,
        "base_w": a["L1_ffn_base_w"].T, "base_b": a["L1_ffn_base_b"].reshape(1, E),
        "lora_a": np.concatenate([a["L1_ffn_A"].T, a["L1_ffn_router_w"].T], 1),
        "lora_b": a["L1_ffn_B"].transpose(0, 2, 1).reshape(NE * RR, E),
    }
    arrays = {n: np.ascontiguousarray(v) for n, v in arrays.items()}
    nc = _bacc.Bacc("TRN2", target_bir_lowering=False, num_devices=1)
    args = [nc.dram_tensor(n, v.shape, F32, kind="ExternalInput").ap() for n, v in arrays.items()]
    out = nc.dram_tensor("out", (NB * S, E), F32, kind="ExternalOutput").ap()
    build(nc, STOP, *args, out)
    r = _run(nc, [arrays], core_ids=[0])
    return r.results[0]["out"].reshape(NB, S, E)
```

```python
from contextlib import ExitStack

import numpy as np

import concourse.bass as bass
from concourse import mybir

F32 = mybir.dt.float32
BF16 = mybir.dt.bfloat16
U32 = mybir.dt.uint32
ALU = mybir.AluOpType
ACT = mybir.ActivationFunctionType
AXX = mybir.AxisListType.X

P = 128
NB, S, E = 2, 512, 512
NT = NB * S // P
TS_ = S // P
EC = E // P
BANK = 512
H, KV, HD = 32, 8, 16
REP = H // KV
GC = (REP + 1) * HD
QK = KV * GC
NG = NB * KV
PARTS = 6
KROWS = PARTS * HD
HF = 1376
NH = -(-HF // P)
BLK = 64
DI, NS, RK, KC = 1024, 16, 32, 4
DC = DI // P
SP_ = 80
UNITS = DC * NB * NS
NE, RR = 16, 64
LC = RR + NE

NF4 = np.array([-1.0, -0.6961928009986877, -0.5250730514526367, -0.39491748809814453, -0.28444138169288635,
                -0.18477343022823334, -0.09105003625154495, 0.0, 0.07958029955625534, 0.16093020141124725,
                0.24611230194568634, 0.33791524171829224, 0.44070982933044434, 0.5626170039176941,
                0.7229568362236023, 1.0], np.float32)
EDGES = (NF4[:-1] + NF4[1:]) * np.float32(0.5)
STEPS = NF4[1:] - NF4[:-1]


def sign_args():
    out = []
    for e in EDGES:
        up = np.nextafter(e, np.float32(np.inf))
        for s in (1.5, 1.25, 1.125, 1.75, 1.0625, 1.875, 1.375, 1.625):
            c = np.float32(-float(e) * s)
            for c in (c, np.nextafter(c, np.float32(-1e9)), np.nextafter(c, np.float32(1e9))):
                if float(e) * s < -float(c) < float(up) * s:
                    break
            else:
                continue
            break
        else:
            raise AssertionError("no scale separates the edge")
        out.append((s, float(c)))
    return out


SIGNS = sign_args()

CONSTS = {}


def constants():
    at, parts = 0, []

    def put(name, a):
        nonlocal at
        full = np.zeros((P, a.shape[1]), np.float32)
        full[:a.shape[0]] = a
        CONSTS[name] = (at, a.shape[1])
        parts.append(full)
        at += a.shape[1]

    p = np.arange(P)
    put("ident", np.eye(P, dtype=np.float32))
    mean = np.zeros((SP_, SP_), np.float32)
    for a, n in ((0, RK), (RK, NS), (64, NS)):
        mean[a:a + n, a:a + n] = 1.0 / n
    put("mean", mean)
    pick = np.zeros((SP_, NS), np.float32)
    for part in range(3):
        pick[32 * part:32 * part + NS] = np.eye(NS)
    put("pick", pick)
    freq = (1.0 / 10000.0 ** (np.arange(0, HD, 2, dtype=np.float32) / np.float32(HD))).astype(np.float32)
    ang = np.arange(S, dtype=np.float32)[:, None] * freq[None, :]
    for name, f in (("cos", np.cos), ("sin", np.sin)):
        t = f(ang).astype(np.float32)
        t = np.concatenate([t, t], 1).reshape(TS_, P, HD).transpose(1, 0, 2).reshape(P, TS_ * HD)
        put(name, t)
    put("iota", np.tile(np.arange(NE, dtype=np.float32), (P, 1)))
    put("edge_bias", np.tile(np.array([c for _, c in SIGNS], np.float32), (P, 1)))
    put("eps", np.full((P, 1), 1e-6, np.float32))
    put("one", np.ones((P, 1), np.float32))
    put("mhalf", np.full((P, 4), -0.5, np.float32))
    put("ones_row", np.ones((1, P), np.float32))
    return np.concatenate(parts, 1)


CONST = constants()


def build(nc, STOP, x, cst, wqkv, bqkv, w1, w2, w3, w_in, conv, wx, lnw, wdt, acol, w_out, base_w, base_b, lora_a, lora_b, out):
    ctx = ExitStack()
    with ctx:
        sem = lambda name: ctx.enter_context(nc.semaphore(name))
        arena = ctx.enter_context(nc.sbuf_tensor("arena", [P, 53200], F32))
        psum = ctx.enter_context(nc.psum_tensor("psum", [P, 8 * BANK], F32))

        def at(off, n, rows=P):
            return arena[0:rows, off:off + n]

        def at16(off, n, rows=P):
            return arena[0:rows, off:off + n // 2].bitcast(BF16)

        def bank(b, n=1, rows=P):
            return psum[0:rows, b * BANK:(b + n) * BANK]

        X = at(0, NT * E).rearrange("p (i e) -> p i e", e=E)
        XNT = at(4096, EC * NB * S).rearrange("p (c t) -> p c t", c=EC)
        NCST = CONST.shape[1]
        C = at(8192, NCST)
        const = lambda name, rows=P: C[0:rows, CONSTS[name][0]:CONSTS[name][0] + CONSTS[name][1]]
        assert NCST <= 1408
        small = 9600
        ST6 = at(small, 48).rearrange("p (i s) -> p i s", s=6)
        MV = at(small + 48, 16).rearrange("p (i s) -> p i s", s=2)
        VARE = at(small + 64, 8)
        RSTD = at(small + 72, 8)
        identb = at16(small + 80, P)
        XN = at(small + 144, 2 * E).rearrange("p (k e) -> p k e", e=E)
        R0 = small + 144 + 1024
        ident = const("ident")
        o = R0
        WQ = at(o, EC * 768).rearrange("p (c n) -> p c n", c=EC); o += EC * 768
        BQ = at(o, 768, 1); o += 768
        R = at(o, NT * QK).rearrange("p (i n) -> p i n", i=NT); o += NT * QK
        V1 = at(o, NT * KV * 32).rearrange("p (i k d) -> p i k d", i=NT, k=KV); o += NT * KV * 32
        QC = at(o, QK).rearrange("p (h d) -> p h d", d=HD); o += QK
        QS = at(o, QK).rearrange("p (h d) -> p h d", d=HD); o += QK
        SKW = TS_ * 5 * KROWS
        SK = at16(o, 2 * SKW).rearrange("p (k t s q d) -> p k t s q d", k=2, t=TS_, s=5, d=HD)
        SKF = at16(o, 2 * SKW).rearrange("p (k t s c) -> p k t s c", k=2, t=TS_, s=5); o += SKW
        RES = at(o, TS_ * GC).rearrange("p (t s d) -> p t s d", t=TS_, d=HD); o += TS_ * GC
        LO = at16(o, TS_ * GC).rearrange("p (t s d) -> p t s d", t=TS_, d=HD); o += TS_ * GC // 2
        QT = at16(o, 4 * 5 * S).rearrange("p (k s t) -> p k s t", k=4, s=5); o += 4 * 5 * S // 2
        PR = at(o, 3 * REP * S).rearrange("p (k j t) -> p k j t", k=3, j=REP); o += 3 * REP * S
        OS = at(o, 2 * S).rearrange("p (k t) -> p k t", k=2); o += 2 * S
        MX = at(o, 32).rearrange("p (k t j) -> p k t j", k=2, t=TS_); o += 32
        MS = at16(o, 64).rearrange("p (k t m j) -> p k t m j", k=2, t=TS_, m=2)
        MSF = at16(o, 64).rearrange("p (k t c) -> p k t c", k=2, t=TS_); o += 32
        MTS = at16(o, 2 * S).rearrange("p (k t) -> p k t", k=2); o += S
        REC = at(o, 16).rearrange("p (t j) -> p t j", j=REP); o += 16
        TMP = at(o, TS_ * REP * HD).rearrange("p (t j d) -> p t j d", t=TS_, j=REP); o += TS_ * REP * HD
        assert o <= 41000, o
        o = R0
        HT = at(o, NH * NB * S).rearrange("p (h t) -> p h t", h=NH); o += NH * NB * S
        DQ3 = at(o, NH * E).rearrange("p (h e) -> p h e", h=NH); o += NH * E
        DQT = at(o, 2 * 2 * E).rearrange("p (k w c h) -> p k w c h", k=2, w=2, c=EC); o += 2 * 2 * E
        SG = at(o, NB * S); o += NB * S
        W3V = at(o, BANK); o += BANK
        W3M = at(o, 2 * BANK).rearrange("p (k n) -> p k n", k=2); o += 2 * BANK
        W3T = at(o, 2 * BANK).rearrange("p (k n) -> p k n", k=2); o += 2 * BANK
        W3A = at(o, 2 * BANK).rearrange("p (k n) -> p k n", k=2); o += 2 * BANK
        AM = at(o, 4 * 16).rearrange("p (q n) -> p q n", q=4); o += 64
        AM3 = at(o, 4 * 86).rearrange("p (q n) -> p q n", q=4); o += 4 * 86
        NV = at(o, 2 * E); o += 2 * E
        NTB = at(o, 2 * 2 * E).rearrange("p (k n) -> p k n", k=2); o += 4 * E
        NACC = at(o, 2 * E); o += 2 * E
        DQ = at(o, 2 * 2 * E).rearrange("p (k w e) -> p k w e", k=2, w=2); o += 4 * E
        assert o <= 41000, o
        W3F = at(41000, 4 * HF)
        W3R = at(41000, 4 * HF).rearrange("p (j r h) -> p j r h", j=2, r=2)
        WR = at(46504, 2 * 2 * E).rearrange("p (k w e) -> p k w e", k=2, w=2)
        WI = at(41000, EC * 2 * DI).rearrange("p (c n) -> p c n", c=EC)
        U = at(R0, DC * NB * S).rearrange("p (c t) -> p c t", c=DC)
        GS = at(R0 + 8192, DC * NB * S).rearrange("p (c t) -> p c t", c=DC)
        CR = at(R0 + 16384, NS * NB * S).rearrange("p (n t) -> p n t", n=NS)
        CV = at(49192, 2 * NB * S).rearrange("p (k t) -> p k t", k=2)
        WX = at(51240, DC * SP_).rearrange("p (c n) -> p c n", c=DC)
        AC = at(51880, P)
        CP = at(52008, DC * 7).rearrange("p (c n) -> p c n", n=7)
        LW = at(52064, 1, SP_)
        WD = at(52065, DI, RK)
        o = R0 + 32768
        SS = at(o, NB * S, SP_)
        SQ = at(o + 1024, NB * S, SP_)
        RMS = at(o + 2048, NB * S, SP_)
        PN = at(o + 3072, NB * S, SP_)
        WB = at16(o + 4096, 3 * NB * S, SP_).rearrange("p (k t) -> p k t", k=3)
        BS = at16(4096, NB * S, SP_)
        CS = WB[:, 2, :]
        RES2 = at(o + 1024, NB * S, SP_)
        PICK = at16(4096 + 512, NS * P, SP_).rearrange("p (n m) -> p n m", n=NS)
        GN = 5
        G = at(4096 + 1536, GN * S).rearrange("p (k t) -> p k t", k=GN)
        D = at(o, 2 * S).rearrange("p (k t) -> p k t", k=2)
        SPL = at(o + 1024, 2 * S).rearrange("p (k t) -> p k t", k=2)
        MXB = at(o + 4096, 2 * S).rearrange("p (k t) -> p k t", k=2)
        DU = at(49192, 2 * S).rearrange("p (k t) -> p k t", k=2)
        DB = [at(o + 5120, S), at(50728, S)]
        HS = [at(o + 2048, S), at(o + 2560, S), at(50216, S)]
        YT = XN[:, 0, :]
        WO = at(R0, DC * E).rearrange("p (c n) -> p c n", c=DC)
        o = R0 + 16384
        BF = at(o, NE * RR * E // P).rearrange("p (c n) -> p c n", c=NE * RR // P); o += NE * RR * E // P
        BW = at(o, EC * E).rearrange("p (c n) -> p c n", c=EC); o += EC * E
        LA = at(o, EC * LC).rearrange("p (c n) -> p c n", c=EC); o += EC * LC
        BB = at(o, E, 1); o += E
        LG = at(o, NT * LC).rearrange("p (i n) -> p i n", i=NT); o += NT * LC
        PB = at(o, NT * NE).rearrange("p (i n) -> p i n", i=NT); o += NT * NE
        OH1 = at(o, NT * NE).rearrange("p (i n) -> p i n", i=NT); o += NT * NE
        OH2 = at(o, NT * NE).rearrange("p (i n) -> p i n", i=NT); o += NT * NE
        V8 = at(o, NT * 8).rearrange("p (i n) -> p i n", i=NT); o += NT * 8
        I8 = at(o, NT * 8).bitcast(U32).rearrange("p (i n) -> p i n", i=NT); o += NT * 8
        IF = at(o, NT * 2).rearrange("p (i n) -> p i n", i=NT); o += NT * 2
        W12 = at(o, NT * 2).rearrange("p (i n) -> p i n", i=NT); o += NT * 2
        R8 = at(o, 4 * NT).rearrange("p (q i) -> p q i", q=4); o += 4 * NT
        Z = at(o, 2 * NE * RR).rearrange("p (k e r) -> p k e r", k=2, e=NE)
        ZF = at(o, 2 * NE * RR).rearrange("p (k c n) -> p k c n", k=2, c=8); o += 2 * NE * RR
        ZT = at(o, 2 * NE * RR).rearrange("p (k c n) -> p k c n", k=2, c=8); o += 2 * NE * RR
        assert o <= R0 + 32768

        ld_x = [sem("ld_x0"), sem("ld_x1")]
        ld_const, ld_qkv, ld_w3, ld_wi, ld_scan, ld_wo, ld_moe = (
            sem(n) for n in ("ld_const", "ld_qkv", "ld_w3", "ld_wi", "ld_scan", "ld_wo", "ld_moe"))
        ld_w12 = [sem("ld_w12a"), sem("ld_w12b")]
        init_done = sem("init_done")
        ln_var, ln_rstd, ln_xn, ln_tr, ln_ev = (sem(n) for n in ("ln_var", "ln_rstd", "ln_xn", "ln_tr", "ln_ev"))
        qkv_done, rope_read, rope_done, v_done = (sem(n) for n in ("qkv_done", "rope_read", "rope_done", "v_done"))
        sk_ready, sk_tr, qt_ev = (sem(n) for n in ("sk_ready", "sk_tr", "qt_ev"))
        max_ps, max_read, ms_ready, mt_tr, mt_ev, ld_rows = (
            sem(n) for n in ("max_ps", "max_read", "ms_ready", "mt_tr", "mt_ev", "ld_rows"))
        st_ps, exp_done, pv_done, os_ev, et_tr, et_used, x_attn = (
            sem(n) for n in ("st_ps", "exp_done", "pv_done", "os_ev", "et_tr", "et_used", "x_attn"))
        am3_done, w3_v, w3_t, w3_add, w3_dq, w3_tr, w3_ev = (
            sem(n) for n in ("am3_done", "w3_v", "w3_t", "w3_add", "w3_dq", "w3_tr", "w3_ev"))
        nf_v, dq_done, dq_tr, dq_ev, gu_ps, silu_done, ht_done, y_ps, x_ffn = (
            sem(n) for n in ("nf_v", "dq_done", "dq_tr", "dq_ev", "gu_ps", "silu_done", "ht_done", "y_ps", "x_ffn"))
        u_ps, conv_done, u_done, g_ps, gs_done, ssm_ps, ss_ev, sq_done, ms_ps, rr_done, pn_done = (
            sem(n) for n in ("u_ps", "conv_done", "u_done", "g_ps", "gs_done", "ssm_ps", "ss_ev", "sq_done",
                             "ms_ps", "rr_done", "pn_done"))
        pick_done, bs_done, c_ps, c_ev_act, c_ev_dve = (
            sem(n) for n in ("pick_done", "bs_done", "c_ps", "c_ev_act", "c_ev_dve"))
        dt_ps, sp_done, mx_done, d_done, du_done = (sem(n) for n in ("dt_ps", "sp_done", "mx_done", "d_done", "du_done"))
        b_ps, da_done, dbu_done, scan_done, g_done, ysum, y_read, y_done = (
            sem(n) for n in ("b_ps", "da_done", "dbu_done", "scan_done", "g_done", "ysum", "y_read", "y_done"))
        abs_done = sem("abs_done")
        wo_ps, x_scan = sem("wo_ps"), sem("x_scan")
        lg_ps, lg_ev, lg_sub, lg_exp, route_done, z_done, z_tr, z_ev, out_ps, out_done, st_out = (
            sem(n) for n in ("lg_ps", "lg_ev", "lg_sub", "lg_exp", "route_done", "z_done", "z_tr", "z_ev", "out_ps",
                             "out_done", "st_out"))
        dve_step, act_step, pool_step = sem("dve_step"), sem("act_step"), sem("pool_step")

        ROWS_LD = 2 * REP * 16

        class Steps:

            def __init__(self, eng, s):
                self.eng, self.s, self.n = eng, s, 0

            def step(self, ins):
                self.n += 1
                ins.then_inc(self.s, 1)
                return self.n

            def wait(self, n=None):
                self.eng.wait_ge(self.s, self.n if n is None else n)

        block = ctx.enter_context(nc.Block())
        V, A, G_, T = nc.vector, nc.scalar, nc.gpsimd, nc.tensor
        ht_rows = lambda h: min(P, HF - h * P)
        w3_cols = lambda c: (c * BANK, min(BANK, 4 * HF - c * BANK))
        W3C = -(-4 * HF // BANK)
        pairs = [dc + half * DC for dc in range(DC) for half in range(2)]

        @block.sync
        def _(sp):
            sp.dma_start(C, cst).then_inc(ld_const, 16)
            xv = x.rearrange("(i p) e -> p i e", p=P)
            sp.dma_start(X[:, 0:TS_, :], xv[:, 0:TS_, :]).then_inc(ld_x[0], 16)
            sp.dma_start(WQ, wqkv.rearrange("(c p) n -> p c n", p=P)).then_inc(ld_qkv, 16)
            sp.dma_start(BQ, bqkv).then_inc(ld_qkv, 16)
            sp.dma_start(X[:, TS_:NT, :], xv[:, TS_:NT, :]).then_inc(ld_x[1], 16)
            if STOP >= 2:
                sp.dma_start(W3F.rearrange("p (j n) -> p j n", j=2),
                             w3.rearrange("(j p r) h -> p j (r h)", p=P, r=2)).then_inc(ld_w3, 16)

            def load_w12(h):
                n = ht_rows(h)
                sp.dma_start(WR[0:n, h % 2, 0, :], w1[h * P:h * P + n, :]).then_inc(ld_w12[h % 2], 16)
                sp.dma_start(WR[0:n, h % 2, 1, :], w2[h * P:h * P + n, :]).then_inc(ld_w12[h % 2], 16)

            if STOP >= 2:
                load_w12(0)
                load_w12(1)
            if STOP >= 3:
                sp.dma_start(WX, wx.rearrange("(c p) n -> p c n", p=P)).then_inc(ld_scan, 16)
                sp.dma_start(AC, acol).then_inc(ld_scan, 16)
                sp.dma_start(CP, conv.rearrange("(c p) n -> p c n", p=P)).then_inc(ld_scan, 16)
                sp.dma_start(LW, lnw).then_inc(ld_scan, 16)
                sp.dma_start(WD, wdt).then_inc(ld_scan, 16)
            for g in range(NG):
                sp.wait_ge(mt_ev, g + 1)
                for m in range(2):
                    for j in range(REP):
                        sp.dma_start(QT[KROWS + m:KROWS + m + 1, g % 4, j, :],
                                     MTS[REP * m + j:REP * m + j + 1, g % 2, :]).then_inc(ld_rows, 16)
            if STOP >= 2:
                for h in range(2, NH):
                    sp.wait_ge(nf_v, h - 1)
                    load_w12(h)
            if STOP >= 3:
                sp.wait_ge(nf_v, NH)
                sp.wait_ge(w3_tr, NH)
                sp.dma_start(WI, w_in.rearrange("(c p) n -> p c n", p=P)).then_inc(ld_wi, 16)
                sp.wait_ge(y_done, UNITS // NS // 2)
                sp.dma_start(WO, w_out.rearrange("(c p) n -> p c n", p=P)).then_inc(ld_wo, 16)
            if STOP >= 4:
                sp.wait_ge(g_done, UNITS)
                sp.dma_start(BF, lora_b.rearrange("(c p) n -> p c n", p=P)).then_inc(ld_moe, 16)
                sp.dma_start(BW, base_w.rearrange("(c p) n -> p c n", p=P)).then_inc(ld_moe, 16)
                sp.dma_start(LA, lora_a.rearrange("(c p) n -> p c n", p=P)).then_inc(ld_moe, 16)
                sp.dma_start(BB, base_b).then_inc(ld_moe, 16)
            ov = out.rearrange("(i p) e -> p i e", p=P)
            if STOP >= 4:
                for i in range(NT):
                    sp.wait_ge(out_done, i + 1)
                    sp.dma_start(ov[:, i, :], X[:, i, :]).then_inc(st_out, 16)
                sp.wait_ge(st_out, 16 * NT)
            else:
                s_, n_ = {1: (x_attn, NG), 2: (x_ffn, NT), 3: (x_scan, NT)}[STOP]
                sp.wait_ge(s_, n_)
                sp.dma_start(ov, X).then_inc(st_out, 16)
                sp.wait_ge(st_out, 16)

        @block.vector
        def _(dve):
            own = Steps(dve, dve_step)

            def layernorm(k):
                for half in range(2):
                    tiles = range(TS_ * half, TS_ * half + TS_)
                    if k == 0:
                        dve.wait_ge(ld_x[half], 16)
                    elif half == 0:
                        dve.wait_ge((None, x_attn, x_ffn, x_scan)[k], (None, NG, NT, NT)[k])
                    for i in tiles:
                        n = own.step(V.bn_stats(ST6[:, i, :], X[:, i, :]))
                    for i in tiles:
                        own.wait(n - TS_ + 1 + i % TS_)
                        m = own.step(V.bn_aggr(MV[:, i, :], ST6[:, i, :]))
                    own.wait(m)
                    V.tensor_scalar(VARE[:, tiles[0]:tiles[0] + TS_], MV[:, tiles[0]:tiles[0] + TS_, 1], 1e-5, None,
                                    ALU.add).then_inc(ln_var, 1)
                for i in range(NT):
                    if i % TS_ == 0:
                        dve.wait_ge(ln_rstd, 2 * k + i // TS_ + 1)
                    if NT * k + i >= 2:
                        dve.wait_ge(ln_tr, NT * k + i - 1)
                    V.tensor_scalar(XN[:, i % 2, :], X[:, i, :], MV[:, i, 0:1], RSTD[:, i:i + 1],
                                    ALU.subtract, ALU.mult).then_inc(ln_xn, 1)

            dve.wait_ge(ld_const, 16)
            V.tensor_copy(identb, ident).then_inc(init_done, 1)
            V.memset(V1, 0.0).then_inc(init_done, 1)
            dve.wait_ge(init_done, 2)
            V.memset(V1[:, :, :, HD:HD + 1], 1.0).then_inc(init_done, 1)
            V.memset(QT[KROWS:KROWS + 2, :, REP, :], 1.0).then_inc(init_done, 1)
            layernorm(0)

            def rope(i):
                base = (i % 2) * 2 * BANK
                dve.wait_ge(qkv_done, i + 1)
                ps = psum[:, base:base + QK].rearrange("p (h d) -> p h d", d=HD)
                t = i % TS_
                cos, sin = (const(n)[:, t * HD:t * HD + HD].unsqueeze(1).broadcast_to([P, QK // HD, HD])
                            for n in ("cos", "sin"))
                if i:
                    dve.wait_ge(rope_done, i)
                own.step(V.tensor_tensor(QC, ps, cos, ALU.mult))
                V.tensor_tensor(QS, ps, sin, ALU.mult).then_inc(rope_read, 1)
                dve.wait_ge(rope_read, i + 1)
                r = R[:, i, :].rearrange("p (h d) -> p h d", d=HD)
                V.tensor_tensor(r[:, :, 0:HD // 2], QC[:, :, 0:HD // 2], QS[:, :, HD // 2:HD], ALU.subtract)
                V.tensor_tensor(r[:, :, HD // 2:HD], QS[:, :, 0:HD // 2], QC[:, :, HD // 2:HD], ALU.add)\
                 .then_inc(rope_done, 1)

            for i in range(NT):
                rope(i)

            def row_max(g, t):
                if t == 0 and g >= 2:
                    dve.wait_ge(ms_ready, g - 1)
                for j in range(REP):
                    n = (g * TS_ + t) * REP + j
                    dve.wait_ge(max_ps, n + 1)
                    V.tensor_reduce(MX[:, g % 2, t, j:j + 1], bank(n % 2), AXX, ALU.max, negate=True)\
                     .then_inc(max_read, 1)

            def evac_stack(g, r):
                n = 3 * g + r
                dve.wait_ge(sk_tr, n + 1)
                w = 2 if r < 2 else 1
                V.tensor_copy(QT[0:KROWS, g % 4, 2 * r:2 * r + w, :],
                              bank(7)[0:KROWS].bitcast(BF16)[:, 0:w * S].rearrange("p (s t) -> p s t", s=w))\
                 .then_inc(qt_ev, 1)

            def finish(g):
                b, kv = g // KV, g % KV
                dve.wait_ge(et_tr, g + 1)
                o_ps = bank(7).rearrange("p (t j d) -> p t j d", t=TS_, d=32)
                if g:
                    dve.wait_ge(et_used, g)
                    dve.wait_ge(x_attn, g)
                own.step(V.reciprocal(REC, o_ps[:, :, :, HD]))
                own.wait()
                V.tensor_tensor(TMP, o_ps[:, :, :, 0:HD],
                                REC.unsqueeze(3).broadcast_to([P, TS_, REP, HD]), ALU.mult).then_inc(et_used, 1)
                dve.wait_ge(et_used, g + 1)
                xs = X[:, TS_ * b:TS_ * b + TS_, REP * HD * kv:REP * HD * kv + REP * HD]
                V.tensor_tensor(xs, xs, TMP.rearrange("p t j d -> p t (j d)"), ALU.add).then_inc(x_attn, 1)

            for n in range(-3, NG + 1):
                for t in range(TS_):
                    if 0 <= n + 2 < NG:
                        row_max(n + 2, t)
                    if 0 <= n + 3 < NG and t < 3:
                        evac_stack(n + 3, t)
                    if 0 <= n - 1 and t == 3:
                        finish(n - 1)
            if STOP < 2:
                return

            dve.wait_ge(et_tr, NG)
            dve.wait_ge(pv_done, NG * TS_)
            dve.wait_ge(ld_w3, 16)
            own.step(V.tensor_reduce(AM3[:, 0, :], W3F.rearrange("p (n k) -> p n k", k=BLK), AXX, ALU.max,
                                     apply_absolute_value=True))
            own.wait()
            own.step(V.tensor_scalar(AM3[:, 1, :], AM3[:, 0, :], 0.0, None, ALU.is_equal))
            own.wait()
            own.step(V.tensor_tensor(AM3[:, 2, :], AM3[:, 0, :], AM3[:, 1, :], ALU.add))
            own.wait()
            V.reciprocal(AM3[:, 3, :], AM3[:, 2, :]).then_inc(am3_done, 1)
            layernorm(1)

            def nf4(h):
                n = ht_rows(h)
                am = AM[0:n]
                raw = WR[0:n, h % 2].rearrange("p w e -> p (w e)").rearrange("p (b k) -> p b k", k=BLK)
                dve.wait_ge(ld_w12[h % 2], 32 * (h // 2 + 1))
                if h:
                    dve.wait_ge(dq_done, h)
                own.step(V.tensor_reduce(am[:, 0, :], raw, AXX, ALU.max, apply_absolute_value=True))
                own.wait()
                own.step(V.tensor_scalar(am[:, 1, :], am[:, 0, :], 0.0, None, ALU.is_equal))
                own.wait()
                own.step(V.tensor_tensor(am[:, 2, :], am[:, 0, :], am[:, 1, :], ALU.add))
                own.wait()
                own.step(V.reciprocal(am[:, 3, :], am[:, 2, :]))
                own.wait()
                v, acc = NV[0:n], NACC[0:n]
                b3 = lambda a: a.rearrange("p (b k) -> p b k", k=BLK)
                rb = lambda a: a.unsqueeze(2).broadcast_to([n, 2 * E // BLK, BLK])
                V.tensor_tensor(b3(v), raw, rb(am[:, 3, :]), ALU.mult).then_inc(nf_v, 1)
                dve.wait_ge(nf_v, h + 1)

                def edge(i):
                    return own.step(V.tensor_scalar(NTB[0:n, i % 2, :], v, float(EDGES[i]), float(STEPS[i]),
                                                    ALU.is_gt, ALU.mult))

                edge(0)
                last = edge(1)
                own.wait(last)
                added = own.step(V.scalar_tensor_tensor(acc, NTB[0:n, 0, :], float(NF4[0]), NTB[0:n, 1, :],
                                                        ALU.add, ALU.add))
                own.wait(added)
                made = edge(2)
                for i in range(3, len(EDGES) + 1):
                    before = added
                    if i < len(EDGES):
                        nxt = edge(i)
                    own.wait(max(made, before))
                    added = own.step(V.tensor_tensor(acc, acc, NTB[0:n, (i - 1) % 2, :], ALU.add))
                    if i < len(EDGES):
                        made = nxt
                        own.wait(added)
                own.wait(added)
                if h >= 2:
                    dve.wait_ge(dq_tr, h - 1)
                V.tensor_tensor(b3(DQ[0:n, h % 2].rearrange("p w e -> p (w e)")), b3(acc), rb(am[:, 0, :]), ALU.mult)\
                 .then_inc(dq_done, 1)

            def w3_finish(c):
                a, n = w3_cols(c)
                dve.wait_ge(w3_add, (len(EDGES) - 1) * (c + 1))
                k0 = float(np.float32(float(NF4[0]) + float(STEPS.astype(np.float64).sum()) / 2))
                b3 = lambda q: q.rearrange("p (b k) -> p b k", k=BLK)
                V.scalar_tensor_tensor(b3(W3F[:, a:a + n]), b3(W3A[:, c % 2, 0:n]), k0,
                                       AM3[:, 0, a // BLK:(a + n) // BLK].unsqueeze(2).broadcast_to([P, n // BLK, BLK]),
                                       ALU.add, ALU.mult).then_inc(w3_dq, 1)

            def hidden(h):
                n = ht_rows(h)
                dve.wait_ge(silu_done, h + 1)
                V.tensor_tensor(HT[0:n, h, :], SG[0:n], bank(4, 2)[0:n], ALU.mult).then_inc(ht_done, 1)

            for h in range(NH + 1):
                if h < NH:
                    nf4(h)
                if h:
                    hidden(h - 1)
                    w3_finish(h - 1)
            for i in range(NT):
                dve.wait_ge(y_ps, i + 1)
                V.tensor_tensor(X[:, i, :], X[:, i, :], bank(i % 2), ALU.add).then_inc(x_ffn, 1)
            if STOP < 3:
                return

            layernorm(2)
            dve.wait_ge(ld_scan, 16 * 5)
            for c in range(DC):
                dve.wait_ge(u_ps, c + 1)
                if c >= 2:
                    dve.wait_ge(u_done, c - 1)
                ps = bank(0, 2).rearrange("p (b t) -> p b t", b=NB)
                cv = CV[:, c % 2, :].rearrange("p (b t) -> p b t", b=NB)
                own.step(V.tensor_scalar(cv, ps, CP[:, c, KC - 1:KC], CP[:, c, KC:KC + 1], ALU.mult, ALU.add))
                for lag in range(1, KC):
                    own.wait()
                    ins = V.scalar_tensor_tensor(cv[:, :, lag:S], ps[:, :, 0:S - lag], CP[:, c, KC - 1 - lag:KC - lag],
                                                 cv[:, :, lag:S], ALU.mult, ALU.add)
                    if lag < KC - 1:
                        own.step(ins)
                    else:
                        ins.then_inc(conv_done, 1)
            dve.wait_ge(g_ps, DC)
            own.step(V.memset(BS, 0.0))
            own.step(V.memset(CS, 0.0))
            V.tensor_copy(PICK, const("pick", SP_).unsqueeze(2).broadcast_to([SP_, NS, P])).then_inc(pick_done, 1)
            own.wait()
            dve.wait_ge(rr_done, 1)
            dve.wait_ge(ss_ev, 1)
            V.scalar_tensor_tensor(PN, SS, LW[:, 0:1], RMS, ALU.mult, ALU.mult).then_inc(pn_done, 1)
            dve.wait_ge(pn_done, 1)
            for k, a in enumerate((RK, 64)):
                src, hi, mid, res = (t[a:a + NS] for t in (PN, WB[:, 0], WB[:, 1], RES2))
                dst = (BS, CS)[k]
                own.step(V.tensor_copy(hi, src))
                own.wait()
                own.step(V.tensor_tensor(res, src, hi, ALU.subtract))
                own.wait()
                own.step(V.tensor_copy(mid, res))
                own.wait()
                own.step(V.tensor_copy(dst[0:NS], hi))
                own.step(V.tensor_copy(dst[32:32 + NS], mid))
                V.tensor_tensor(dst[64:64 + NS], res, mid, ALU.subtract).then_inc(bs_done, 1)
            for n in range(1, NS, 2):
                dve.wait_ge(c_ps, n + 1)
                V.tensor_copy(CR[:, n, :], bank(2 * (n % 3), 2)).then_inc(c_ev_dve, 1)
            dve.wait_ge(c_ev_act, NS // 2)

            def delta_max(k):
                dve.wait_ge(abs_done, k + 1)
                if k >= 2:
                    dve.wait_ge(d_done, k - 1)
                V.tensor_scalar(MXB[:, k % 2, :], bank(7), CP[:, k // NB, 5:6], 0.0, ALU.add, ALU.max).then_inc(mx_done, 1)

            def delta(k):
                c, b = k // NB, k % NB
                dve.wait_ge(mx_done, k + 1)
                dve.wait_ge(sp_done, k + 1)
                if k >= 2:
                    dve.wait_ge(da_done, NS * (k - 1))
                V.tensor_tensor(D[:, k % 2, :], MXB[:, k % 2, :], SPL[:, k % 2, :], ALU.add).then_inc(d_done, 1)
                dve.wait_ge(d_done, k + 1)
                if k >= 2:
                    dve.wait_ge(dbu_done, NS * (k - 1))
                V.tensor_tensor(DU[:, k % 2, :], D[:, k % 2, :], U[:, c, b * S:b * S + S], ALU.mult).then_inc(du_done, 1)

            def times_b(m):
                dve.wait_ge(b_ps, m + 1)
                if m % NS == 0:
                    dve.wait_ge(du_done, m // NS + 1)
                if m >= 2:
                    dve.wait_ge(scan_done, m - 1)
                V.tensor_tensor(DB[m % 2], DU[:, m // NS % 2, :], bank(m % 3), ALU.mult).then_inc(dbu_done, 1)

            def scan(m):
                dve.wait_ge(dbu_done, m + 1)
                dve.wait_ge(da_done, m + 1)
                if m >= 3:
                    dve.wait_ge(g_done, m - 2)
                V.tensor_tensor_scan(HS[m % 3], bank(3 + m % 3), DB[m % 2], 0.0, ALU.mult, ALU.add)\
                 .then_inc(scan_done, 1)

            def gate(k):
                c, b = k // NB, k % NB
                dve.wait_ge(ysum, NS * (k + 1))
                if k:
                    dve.wait_ge(y_done, k)
                V.scalar_tensor_tensor(YT, U[:, c, b * S:b * S + S], CP[:, c, 6:7], bank(6), ALU.mult, ALU.add)\
                 .then_inc(y_read, 1)
                dve.wait_ge(y_read, k + 1)
                g = GS[:, c, b * S:b * S + S]
                V.tensor_tensor(g, g, YT, ALU.mult).then_inc(y_done, 1)

            NK = UNITS // NS
            delta_max(0)
            delta(0)
            times_b(0)
            for m in range(UNITS):
                k, n = m // NS, m % NS
                if m + 1 < UNITS:
                    times_b(m + 1)
                scan(m)
                if k >= 1 and n == 2:
                    gate(k - 1)
                if k + 1 < NK:
                    if n == 7:
                        delta_max(k + 1)
                    if n == 10:
                        delta(k + 1)
            gate(NK - 1)
            for i in range(NT):
                dve.wait_ge(wo_ps, i + 1)
                V.tensor_tensor(X[:, i, :], X[:, i, :], bank(i % 2), ALU.add).then_inc(x_scan, 1)
            if STOP < 4:
                return

            layernorm(3)
            r8 = lambda q: R8[:, q, :]
            rb = lambda a, n: a.unsqueeze(2).broadcast_to([P, NT, n])
            dve.wait_ge(lg_ev, NT)
            own.step(V.tensor_reduce(r8(0), LG[:, :, RR:LC], AXX, ALU.max))
            own.wait()
            V.tensor_tensor(PB, LG[:, :, RR:LC], rb(r8(0), NE), ALU.subtract).then_inc(lg_sub, 1)
            dve.wait_ge(lg_exp, 1)
            own.step(V.reduce_sum(r8(1), PB, AXX))
            own.wait()
            own.step(V.reciprocal(r8(2), r8(1)))
            own.wait()
            own.step(V.tensor_tensor(OH1, PB, rb(r8(2), NE), ALU.mult))
            own.wait()
            for i in range(NT):
                own.step(V.max(V8[:, i, :], OH1[:, i, :]))
            for i in range(NT):
                own.wait()
                own.step(V.max_index(I8[:, i, :], V8[:, i, :], OH1[:, i, :]))
            own.wait()
            own.step(V.tensor_copy(IF, I8[:, :, 0:2]))
            own.step(V.tensor_tensor(r8(3), V8[:, :, 0], V8[:, :, 1], ALU.add))
            own.wait()
            own.step(V.tensor_scalar(r8(0), r8(3), 1e-6, None, ALU.add))
            own.wait()
            own.step(V.reciprocal(r8(1), r8(0)))
            own.wait()
            own.step(V.tensor_scalar(r8(2), r8(1), 0.5, None, ALU.mult))
            own.wait()
            own.step(V.tensor_tensor(W12, V8[:, :, 0:2], rb(r8(2), 2), ALU.mult))
            iota = const("iota").unsqueeze(1).broadcast_to([P, NT, NE])
            for k, oh in enumerate((OH1, OH2)):
                own.wait()
                own.step(V.tensor_tensor(oh, iota, rb(IF[:, :, k], NE), ALU.is_equal))
                own.wait()
                own.step(V.tensor_tensor(oh, oh, rb(W12[:, :, k], NE), ALU.mult))
            own.wait()
            own.step(V.tensor_tensor(PB, OH1, OH2, ALU.add))
            own.wait()

            def low_rank(i):
                if i >= 2:
                    dve.wait_ge(z_tr, i - 1)
                V.tensor_tensor(Z[:, i % 2], PB[:, i, :].unsqueeze(2).broadcast_to([P, NE, RR]),
                                LG[:, i, 0:RR].unsqueeze(1).broadcast_to([P, NE, RR]), ALU.mult).then_inc(z_done, 1)

            for i in range(NT + 1):
                if i < NT:
                    low_rank(i)
                if i:
                    dve.wait_ge(out_ps, i)
                    V.tensor_tensor(X[:, i - 1, :], X[:, i - 1, :], bank((i - 1) % 2), ALU.add).then_inc(out_done, 1)

        @block.gpsimd
        def _(pool):
            own = Steps(pool, pool_step)

            def rstd(k):
                for half in range(2):
                    pool.wait_ge(ln_var, 2 * k + half + 1)
                    G_.tensor_tensor(RSTD[:, TS_ * half:TS_ * half + TS_], VARE[:, TS_ * half:TS_ * half + TS_],
                                     const("mhalf"), ALU.pow).then_inc(ln_rstd, 1)

            pool.wait_ge(ld_const, 16)
            rstd(0)

            def stack(g):
                b, kv = g // KV, g % KV
                r = R[:, TS_ * b:TS_ * b + TS_, GC * kv:GC * kv + GC].rearrange("p t (s d) -> p t s d", d=HD)
                sk = SK[:, g % 2]
                pool.wait_ge(rope_done, TS_ * (b + 1))
                if g >= 2:
                    pool.wait_ge(sk_tr, 3 * (g - 1))
                if g:
                    pool.wait_ge(sk_ready, g)
                own.step(G_.tensor_copy(sk[:, :, :, 0, :], r))
                own.wait()
                own.step(G_.tensor_tensor(RES, r, sk[:, :, :, 0, :], ALU.subtract))
                own.wait()
                own.step(G_.tensor_copy(sk[:, :, :, 4, :], RES))
                own.wait()
                own.step(G_.tensor_tensor(LO, RES, sk[:, :, :, 4, :], ALU.subtract))
                q, k = sk[:, :, 0:REP], sk[:, :, REP]
                for dst, src in ((1, 0), (2, 0), (3, 4)):
                    own.step(G_.tensor_copy(q[:, :, :, dst, :], q[:, :, :, src, :]))
                for dst, src in ((1, 4), (3, 0), (5, 0)):
                    n = own.step(G_.tensor_copy(k[:, :, dst, :], k[:, :, src, :]))
                own.wait()
                own.step(G_.tensor_copy(q[:, :, :, 5, :], LO[:, :, 0:REP]))
                own.wait()
                G_.tensor_copy(k[:, :, 2, :], LO[:, :, REP]).then_inc(sk_ready, 1)

            def split_max(g):
                pool.wait_ge(max_read, TS_ * REP * (g + 1))
                if g >= 2:
                    pool.wait_ge(mt_tr, g - 1)
                own.step(G_.tensor_copy(MS[:, g % 2, :, 0, :], MX[:, g % 2]))
                own.wait()
                G_.tensor_tensor(MS[:, g % 2, :, 1, :], MX[:, g % 2], MS[:, g % 2, :, 0, :], ALU.subtract)\
                  .then_inc(ms_ready, 1)

            for n in range(-4, NG):
                if n + 4 < NG:
                    stack(n + 4)
                if 0 <= n + 2 < NG:
                    split_max(n + 2)
            if STOP < 2:
                return

            rstd(1)
            pool.wait_ge(am3_done, 1)
            for c in range(W3C):
                a, n = w3_cols(c)
                b3 = lambda q: q.rearrange("p (b k) -> p b k", k=BLK)
                if c:
                    pool.wait_ge(w3_t, len(EDGES) * c)
                G_.tensor_tensor(b3(W3V[:, 0:n]), b3(W3F[:, a:a + n]),
                                 AM3[:, 3, a // BLK:(a + n) // BLK].unsqueeze(2).broadcast_to([P, n // BLK, BLK]),
                                 ALU.mult).then_inc(w3_v, 1)
                acc = W3A[:, c % 2, 0:n]
                for i in range(1, len(EDGES)):
                    k = (len(EDGES) - 1) * c + i
                    pool.wait_ge(w3_t, len(EDGES) * c + i + 1)
                    if k > 1:
                        pool.wait_ge(w3_add, k - 1)
                    G_.tensor_tensor(acc, acc, W3T[:, i % 2, 0:n], ALU.add).then_inc(w3_add, 1)
            if STOP < 3:
                return
            rstd(2)
            pool.wait_ge(c_ev_act, NS // 2)
            pool.wait_ge(c_ev_dve, NS // 2)
            for m in range(UNITS):
                b = m // NS % NB
                pool.wait_ge(scan_done, m + 1)
                if m >= GN:
                    pool.wait_ge(ysum, m - GN + 1)
                G_.tensor_tensor(G[:, m % GN, :], HS[m % 3], CR[:, m % NS, b * S:b * S + S], ALU.mult).then_inc(g_done, 1)
            if STOP < 4:
                return
            rstd(3)

        @block.scalar
        def _(act):
            own = Steps(act, act_step)

            def evac_ln(k):
                for i in range(NT):
                    act.wait_ge(ln_tr, NT * k + i + 1)
                    A.activation(XNT[:, :, i * P:i * P + P], bank(6 + i % 2).rearrange("p (c t) -> p c t", c=EC), ACT.Copy)\
                     .then_inc(ln_ev, 1)

            evac_ln(0)
            act.wait_ge(init_done, 4)
            for i in range(NT):
                act.wait_ge(rope_read, i + 1)
                base = (i % 2) * 2 * BANK + QK
                A.activation(V1[:, i, :, 0:HD], psum[:, base:base + KV * HD].rearrange("p (k d) -> p k d", d=HD), ACT.Copy)\
                 .then_inc(v_done, 1)

            def exps(step):
                if step >= 3:
                    act.wait_ge(pv_done, step - 2)
                for q in range(2):
                    n = 2 * step + q
                    act.wait_ge(st_ps, n + 1)
                    A.activation(PR[:, step % 3, 2 * q:2 * q + 2, :],
                                 bank(2 + 2 * q, 2).rearrange("p (j t) -> p j t", j=2), ACT.Exp, scale=HD ** -0.5)\
                     .then_inc(exp_done, 1)

            for n in range(-1, NG + 1):
                for t in range(TS_):
                    if 0 <= n < NG:
                        exps(TS_ * n + t)
                    if t == 0:
                        if 0 <= n + 1 < NG:
                            act.wait_ge(mt_tr, n + 2)
                            if n + 1 >= 2:
                                act.wait_ge(ld_rows, ROWS_LD * n)
                            A.activation(MTS[0:2 * REP, (n + 1) % 2, :], bank(7)[0:2 * REP].bitcast(BF16)[:, 0:S], ACT.Copy)\
                             .then_inc(mt_ev, 1)
                        if n >= 1:
                            act.wait_ge(pv_done, TS_ * n)
                            if n >= 3:
                                act.wait_ge(et_tr, n - 2)
                            A.activation(OS[:, (n - 1) % 2, :], bank(6), ACT.Copy).then_inc(os_ev, 1)
            if STOP < 2:
                return

            evac_ln(1)

            def w3_chunk(c):
                a, n = w3_cols(c)
                act.wait_ge(w3_v, c + 1)
                ne = len(EDGES)

                def sign(i):
                    if ne * c + i >= 2:
                        act.wait_ge(w3_t, ne * c + i - 1)
                    return own.step(A.activation(W3M[:, i % 2, 0:n], W3V[:, 0:n], ACT.Sign, scale=float(SIGNS[i][0]),
                                                 bias=const("edge_bias")[:, i:i + 1]))

                nxt = sign(0)
                for i in range(ne):
                    made = nxt
                    if i + 1 < ne:
                        nxt = sign(i + 1)
                    own.wait(made)
                    if i == 0:
                        dst = W3A[:, c % 2, 0:n]
                        if c >= 2:
                            act.wait_ge(w3_dq, c - 1)
                    else:
                        dst = W3T[:, i % 2, 0:n]
                        k = (ne - 1) * c + i
                        if k - 2 >= 1:
                            act.wait_ge(w3_add, k - 2)
                    A.activation(dst, W3M[:, i % 2, 0:n], ACT.Copy, scale=float(STEPS[i]) / 2).then_inc(w3_t, 1)

            for h in range(NH):
                n = ht_rows(h)
                for w in range(2):
                    act.wait_ge(dq_tr, h + 1)
                    if h >= 2:
                        act.wait_ge(gu_ps, h - 1)
                    A.activation(DQT[:, h % 2, w, :, 0:n], bank(w).rearrange("p (c h) -> p c h", c=EC)[:, :, 0:n], ACT.Copy)\
                     .then_inc(dq_ev, 1)
                w3_chunk(h)
                act.wait_ge(gu_ps, h + 1)
                if h:
                    act.wait_ge(ht_done, h)
                A.activation(SG[0:n], bank(2, 2)[0:n], ACT.Silu).then_inc(silu_done, 1)
            for h in range(NH):
                n = ht_rows(h)
                act.wait_ge(w3_tr, h + 1)
                A.activation(DQ3[0:n, h, :].rearrange("p (j q r) -> p j r q", j=2, r=2),
                             bank(6 + h % 2)[0:n].rearrange("p (j r q) -> p j r q", j=2, r=2), ACT.Copy).then_inc(w3_ev, 1)
            if STOP < 3:
                return

            evac_ln(2)
            for c in range(DC):
                act.wait_ge(conv_done, c + 1)
                A.activation(U[:, c, :], CV[:, c % 2, :], ACT.Silu).then_inc(u_done, 1)
                act.wait_ge(g_ps, c + 1)
                A.activation(GS[:, c, :], bank(2, 2), ACT.Silu).then_inc(gs_done, 1)
            act.wait_ge(ssm_ps, 1)
            A.activation(SQ, bank(4, 2)[0:SP_], ACT.Square).then_inc(sq_done, 1)
            A.activation(SS, bank(4, 2)[0:SP_], ACT.Copy).then_inc(ss_ev, 1)
            act.wait_ge(ms_ps, 1)
            own.step(A.activation(RMS, bank(6, 2)[0:SP_], ACT.Ln, bias=const("eps", SP_)))
            own.wait()
            A.activation(RMS, RMS, ACT.Exp, scale=-0.5).then_inc(rr_done, 1)
            for n in range(0, NS, 2):
                act.wait_ge(c_ps, n + 1)
                A.activation(CR[:, n, :], bank(2 * (n % 3), 2), ACT.Copy).then_inc(c_ev_act, 1)

            def softplus(k):
                buf = SPL[:, k % 2, :]
                act.wait_ge(dt_ps, k + 1)
                if k >= 2:
                    act.wait_ge(d_done, k - 1)
                A.activation(buf, bank(7), ACT.Abs, bias=CP[:, k // NB, 5:6]).then_inc(abs_done, 1)
                act.wait_ge(abs_done, k + 1)
                own.step(A.activation(buf, buf, ACT.Exp, scale=-1.0))
                own.wait()
                A.activation(buf, buf, ACT.Ln, bias=const("one")).then_inc(sp_done, 1)

            act.wait_ge(c_ev_dve, NS // 2)
            softplus(0)
            for m in range(UNITS):
                k, n = m // NS, m % NS
                if n == 0:
                    act.wait_ge(d_done, k + 1)
                if m >= 3:
                    act.wait_ge(scan_done, m - 2)
                A.activation(bank(3 + m % 3), D[:, k % 2, :], ACT.Exp, scale=AC[:, NS * (k // NB) + n:NS * (k // NB) + n + 1])\
                 .then_inc(da_done, 1)
                if n == 4 and k + 1 < UNITS // NS:
                    softplus(k + 1)
            if STOP < 4:
                return

            evac_ln(3)
            for i in range(NT):
                act.wait_ge(lg_ps, i + 1)
                A.activation(LG[:, i, :], bank(4 + i % 2)[:, 0:LC], ACT.Copy).then_inc(lg_ev, 1)
            act.wait_ge(lg_sub, 1)
            A.activation(PB, PB, ACT.Exp).then_inc(lg_exp, 1)
            for i in range(NT):
                act.wait_ge(z_tr, i + 1)
                if i >= 2:
                    act.wait_ge(out_ps, i - 1)
                A.activation(ZT[:, i % 2], bank(2 + 2 * (i % 2), 2).rearrange("p (c n) -> p c n", c=8), ACT.Copy)\
                 .then_inc(z_ev, 1)

        @block.tensor
        def _(pe):
            def transpose_ln(k):
                for i in range(NT):
                    pe.wait_ge(ln_xn, NT * k + i + 1)
                    if i >= 2:
                        pe.wait_ge(ln_ev, NT * k + i - 1)
                    for c in range(EC):
                        mm = T.transpose(bank(6 + i % 2)[:, c * P:c * P + P], XN[:, i % 2, c * P:c * P + P], ident)
                    mm.then_inc(ln_tr, 1)

            pe.wait_ge(ld_const, 16)
            transpose_ln(0)
            pe.wait_ge(ld_qkv, 32)
            for i in range(NT):
                pe.wait_ge(ln_ev, i + 1)
                if i >= 2:
                    pe.wait_ge(rope_read, i - 1)
                    pe.wait_ge(v_done, i - 1)
                for a, n in ((0, BANK), (BANK, 768 - BANK)):
                    o_ = psum[:, (i % 2) * 2 * BANK + a:(i % 2) * 2 * BANK + a + n]
                    T.matmul(o_, const("ones_row", 1), BQ[:, a:a + n], start=True, stop=False)
                    for c in range(EC):
                        mm = T.matmul(o_, XNT[:, c, i * P:i * P + P], WQ[:, c, a:a + n], start=False, stop=(c == EC - 1))
                mm.then_inc(qkv_done, 1)

            used = {"mt": 0, "qt": 0, "et": 0}

            def bank7_free():
                for s_, n_ in ((mt_ev, used["mt"]), (qt_ev, used["qt"]), (et_used, used["et"])):
                    if n_:
                        pe.wait_ge(s_, n_)

            def turn_stack(g, r):
                pe.wait_ge(sk_ready, g + 1)
                bank7_free()
                used["qt"] += 1
                dst = bank(7)[0:KROWS].bitcast(BF16)
                for s in range(2 * r, min(2 * r + 2, 5)):
                    for t in range(TS_):
                        c = ((s - 2 * r) * TS_ + t) * P
                        mm = T.transpose(dst[:, c:c + P], SKF[:, g % 2, t, s, :], identb)
                mm.then_inc(sk_tr, 1)

            def score_rows(g, t):
                pe.wait_ge(qt_ev, 3 * (g + 1))
                for j in range(REP):
                    n = (g * TS_ + t) * REP + j
                    if n >= 2:
                        pe.wait_ge(max_read, n - 1)
                    T.matmul(bank(n % 2), QT[0:KROWS, g % 4, j, t * P:t * P + P], QT[0:KROWS, g % 4, REP, :],
                             start=True, stop=True).then_inc(max_ps, 1)

            def turn_max(g):
                pe.wait_ge(ms_ready, g + 1)
                bank7_free()
                used["mt"] += 1
                for t in range(TS_):
                    mm = T.transpose(bank(7)[0:2 * REP].bitcast(BF16)[:, t * P:t * P + P], MSF[:, g % 2, t, :], identb)
                mm.then_inc(mt_tr, 1)

            def score_cols(g, t):
                pe.wait_ge(ld_rows, ROWS_LD * (g + 1))
                for q in range(2):
                    n = 2 * (g * TS_ + t) + q
                    if n >= 2:
                        pe.wait_ge(exp_done, n - 1)
                    for j in range(2 * q, 2 * q + 2):
                        mm = T.matmul(bank(2 + j), QT[0:KROWS + 2, g % 4, REP, t * P:t * P + P],
                                      QT[0:KROWS + 2, g % 4, j, :], start=True, stop=True)
                    mm.then_inc(st_ps, 1)

            def values(step):
                g, t = step // TS_, step % TS_
                pe.wait_ge(exp_done, 2 * step + 2)
                if t == 0 and g:
                    pe.wait_ge(os_ev, g)
                for j in range(REP):
                    mm = T.matmul(bank(6)[32 * j:32 * j + 32], V1[:, TS_ * (g // KV) + t, g % KV, :],
                                  PR[:, step % 3, j, :], start=(t == 0), stop=(t == TS_ - 1))
                mm.then_inc(pv_done, 1)

            def turn_out(g):
                pe.wait_ge(os_ev, g + 1)
                bank7_free()
                used["et"] += 1
                for t in range(TS_):
                    mm = T.transpose(bank(7)[:, t * P:t * P + P], OS[:, g % 2, t * P:t * P + P], ident)
                mm.then_inc(et_tr, 1)

            pe.wait_ge(init_done, 4)
            pe.wait_ge(rope_read, NT)
            pe.wait_ge(v_done, NT)
            for n in range(-3, NG + 1):
                for t in range(TS_):
                    if 0 <= n < NG:
                        score_cols(n, t)
                    if 0 <= n + 2 < NG:
                        score_rows(n + 2, t)
                    if 0 <= TS_ * n + t - 1 < TS_ * NG:
                        values(TS_ * n + t - 1)
                    if t == 0 and 0 <= n + 1 < NG:
                        turn_max(n + 1)
                    if t < 3 and 0 <= n + 3 < NG:
                        turn_stack(n + 3, t)
                    if t == 3 and n >= 1:
                        turn_out(n - 1)
            if STOP < 2:
                return

            bank7_free()
            pe.wait_ge(os_ev, NG)
            transpose_ln(1)
            for h in range(NH):
                n = ht_rows(h)
                pe.wait_ge(dq_done, h + 1)
                if h:
                    pe.wait_ge(dq_ev, 2 * h)
                for w in range(2):
                    for c in range(EC):
                        mm = T.transpose(bank(w)[:, c * P:c * P + n], DQ[0:n, h % 2, w, c * P:c * P + P], ident[0:n, 0:n])
                mm.then_inc(dq_tr, 1)
                pe.wait_ge(dq_ev, 2 * (h + 1))
                if h == 0:
                    pe.wait_ge(ln_ev, 2 * NT)
                else:
                    pe.wait_ge(ht_done, h)
                for w in range(2):
                    for b in range(NB):
                        for c in range(EC):
                            mm = T.matmul(bank(2 + 2 * w + b)[0:n], DQT[:, h % 2, w, c, 0:n], XNT[:, c, b * S:b * S + S],
                                          start=(c == 0), stop=(c == EC - 1))
                mm.then_inc(gu_ps, 1)
            pe.wait_ge(w3_dq, W3C)
            for h in range(NH):
                n = ht_rows(h)
                if h >= 2:
                    pe.wait_ge(w3_ev, h - 1)
                for j in range(2):
                    for r in range(2):
                        mm = T.transpose(bank(6 + h % 2)[0:n, (2 * j + r) * P:(2 * j + r) * P + P],
                                         W3R[:, j, r, h * P:h * P + n], ident)
                mm.then_inc(w3_tr, 1)
            pe.wait_ge(ht_done, NH)
            pe.wait_ge(w3_ev, NH)
            for i in range(NT):
                if i >= 2:
                    pe.wait_ge(x_ffn, i - 1)
                for h in range(NH):
                    n = ht_rows(h)
                    mm = T.matmul(bank(i % 2), HT[0:n, h, i * P:i * P + P], DQ3[0:n, h, :], start=(h == 0), stop=(h == NH - 1))
                mm.then_inc(y_ps, 1)
            if STOP < 3:
                return

            transpose_ln(2)
            pe.wait_ge(x_ffn, NT)
            pe.wait_ge(ld_wi, 16)
            pe.wait_ge(ld_scan, 16 * 5)
            pe.wait_ge(ln_ev, 3 * NT)

            def to_ssm(c):
                pe.wait_ge(u_done, c + 1)
                for b in range(NB):
                    mm = T.matmul(bank(4 + b)[0:SP_], WX[:, c, :], U[:, c, b * S:b * S + S], start=(c == 0), stop=(c == DC - 1))
                if c == DC - 1:
                    mm.then_inc(ssm_ps, 1)

            for c in range(DC):
                for half in range(2):
                    if c:
                        pe.wait_ge((conv_done, gs_done)[half], c)
                    for b in range(NB):
                        for e in range(EC):
                            mm = T.matmul(bank(2 * half + b), WI[:, e, half * DI + c * P:half * DI + c * P + P],
                                          XNT[:, e, b * S:b * S + S], start=(e == 0), stop=(e == EC - 1))
                    mm.then_inc((u_ps, g_ps)[half], 1)
                if c >= 1:
                    to_ssm(c - 1)
            to_ssm(DC - 1)
            pe.wait_ge(sq_done, 1)
            for b in range(NB):
                mm = T.matmul(bank(6 + b)[0:SP_], const("mean", SP_), SQ[:, b * S:b * S + S], start=True, stop=True)
            mm.then_inc(ms_ps, 1)
            pe.wait_ge(gs_done, DC)
            pe.wait_ge(pn_done, 1)

            def delta_in(k):
                if k:
                    pe.wait_ge(mx_done, k)
                T.matmul(bank(7), WD[:, k // NB * P:k // NB * P + P], PN[0:RK, k % NB * S:k % NB * S + S],
                         start=True, stop=True).then_inc(dt_ps, 1)

            pe.wait_ge(rr_done, 1)
            delta_in(0)
            pe.wait_ge(pick_done, 1)
            pe.wait_ge(bs_done, 2)
            for n in range(NS):
                if n >= 3:
                    m = n - 3
                    pe.wait_ge((c_ev_act, c_ev_dve)[m % 2], m // 2 + 1)
                for b in range(NB):
                    mm = T.matmul(bank(2 * (n % 3) + b), PICK[:, n, :], CS[:, b * S:b * S + S], start=True, stop=True)
                mm.then_inc(c_ps, 1)
            pe.wait_ge(c_ev_act, NS // 2)
            pe.wait_ge(c_ev_dve, NS // 2)

            def b_rows(m):
                b = m // NS % NB
                if m >= 3:
                    pe.wait_ge(dbu_done, m - 2)
                T.matmul(bank(m % 3), PICK[:, m % NS, :], BS[:, b * S:b * S + S], start=True, stop=True).then_inc(b_ps, 1)

            def sum_states(m):
                k, n = m // NS, m % NS
                if n == 0 and k:
                    pe.wait_ge(y_read, k)
                pe.wait_ge(g_done, m + 1)
                T.matmul(bank(6), ident, G[:, m % GN, :], start=(n == 0), stop=(n == NS - 1)).then_inc(ysum, 1)

            for m in range(UNITS + 3):
                if m < UNITS:
                    b_rows(m)
                if m >= 3:
                    sum_states(m - 3)
                if m < UNITS and m % NS == 2 and m // NS + 1 < UNITS // NS:
                    delta_in(m // NS + 1)
            pe.wait_ge(ld_wo, 16)
            pe.wait_ge(y_done, UNITS // NS)
            for i in range(NT):
                if i >= 2:
                    pe.wait_ge(x_scan, i - 1)
                for c in range(DC):
                    mm = T.matmul(bank(i % 2), GS[:, c, i * P:i * P + P], WO[:, c, :], start=(c == 0), stop=(c == DC - 1))
                mm.then_inc(wo_ps, 1)
            if STOP < 4:
                return

            transpose_ln(3)
            pe.wait_ge(x_scan, NT)
            pe.wait_ge(ld_moe, 64)
            pe.wait_ge(ln_ev, 4 * NT)
            for i in range(NT):
                if i >= 2:
                    pe.wait_ge(lg_ev, i - 1)
                for c in range(EC):
                    mm = T.matmul(bank(4 + i % 2)[:, 0:LC], XNT[:, c, i * P:i * P + P], LA[:, c, :], start=(c == 0), stop=(c == EC - 1))
                mm.then_inc(lg_ps, 1)
            pe.wait_ge(lg_ev, NT)
            for i in range(NT + 1):
                if i < NT:
                    pe.wait_ge(z_done, i + 1)
                    if i >= 2:
                        pe.wait_ge(z_ev, i - 1)
                    for c in range(8):
                        mm = T.transpose(bank(2 + 2 * (i % 2), 2)[:, c * P:c * P + P], ZF[:, i % 2, c, :], ident)
                    mm.then_inc(z_tr, 1)
                    if i >= 2:
                        pe.wait_ge(out_done, i - 1)
                    T.matmul(bank(i % 2), const("ones_row", 1), BB, start=True, stop=False)
                    for c in range(EC):
                        T.matmul(bank(i % 2), XNT[:, c, i * P:i * P + P], BW[:, c, :], start=False, stop=False)
                if i:
                    pe.wait_ge(z_ev, i)
                    for c in range(8):
                        mm = T.matmul(bank((i - 1) % 2), ZT[:, (i - 1) % 2, c, :], BF[:, c, :], start=False, stop=(c == 7))
                    mm.then_inc(out_ps, 1)


def kernel(**inputs):
    import concourse.bacc as _bacc
    from concourse.bass_utils import run_bass_kernel_spmd as _run

    STOP = 4
    a = {k: np.asarray(v) for k, v in inputs.items()}
    q = a["L0_attn_wq"].reshape(E, KV, REP * HD)
    k = a["L0_attn_wk"].reshape(E, KV, HD)
    bq, bk = a["L0_attn_bq"].reshape(1, KV, REP * HD), a["L0_attn_bk"].reshape(1, KV, HD)
    wqkv = np.concatenate([np.concatenate([q, k], 2).reshape(E, QK), a["L0_attn_wv"]], 1)
    bqkv = np.concatenate([np.concatenate([bq, bk], 2).reshape(1, QK), a["L0_attn_bv"].reshape(1, KV * HD)], 1)
    conv = np.concatenate([a["L1_attn_conv_w"], a["L1_attn_conv_b"][:, None], a["L1_attn_dt_bias"][:, None],
                           a["L1_attn_D_param"][:, None]], 1)
    wx = a["L1_attn_Wx"].T
    wxp = np.zeros((DI, SP_), np.float32)
    wxp[:, 0:RK + NS] = wx[:, 0:RK + NS]
    wxp[:, 64:SP_] = wx[:, RK + NS:]
    lnw = np.zeros((SP_, 1), np.float32)
    lnw[0:RK, 0] = a["L1_attn_dt_ln_w"]
    lnw[RK:RK + NS, 0] = a["L1_attn_b_ln_w"]
    lnw[64:SP_, 0] = a["L1_attn_c_ln_w"]
    arrays = {
        "x": a["L0_attn_x"].reshape(NB * S, E), "cst": CONST, "wqkv": wqkv, "bqkv": bqkv,
        "w1": a["L0_ffn_w1"], "w2": a["L0_ffn_w2"], "w3": a["L0_ffn_w3"],
        "w_in": a["L1_attn_W_in"].T, "conv": conv, "wx": wxp, "lnw": lnw, "wdt": a["L1_attn_Wdt"].T,
        "acol": a["L1_attn_A"].reshape(DC, P, NS).transpose(1, 0, 2).reshape(P, DC * NS), "w_out": a["L1_attn_W_out"].T,
        "base_w": a["L1_ffn_base_w"].T, "base_b": a["L1_ffn_base_b"].reshape(1, E),
        "lora_a": np.concatenate([a["L1_ffn_A"].T, a["L1_ffn_router_w"].T], 1),
        "lora_b": a["L1_ffn_B"].transpose(0, 2, 1).reshape(NE * RR, E),
    }
    arrays = {n: np.ascontiguousarray(v) for n, v in arrays.items()}
    nc = _bacc.Bacc("TRN2", target_bir_lowering=False, num_devices=1)
    args = [nc.dram_tensor(n, v.shape, F32, kind="ExternalInput").ap() for n, v in arrays.items()]
    out = nc.dram_tensor("out", (NB * S, E), F32, kind="ExternalOutput").ap()
    build(nc, STOP, *args, out)
    r = _run(nc, [arrays], core_ids=[0])
    return r.results[0]["out"].reshape(NB, S, E)
```

```python
from contextlib import ExitStack

import numpy as np

import concourse.bass as bass
from concourse import mybir

F32 = mybir.dt.float32
BF16 = mybir.dt.bfloat16
U32 = mybir.dt.uint32
ALU = mybir.AluOpType
ACT = mybir.ActivationFunctionType
AXX = mybir.AxisListType.X

P = 128
NB, S, E = 2, 512, 512
NT = NB * S // P
TS_ = S // P
EC = E // P
BANK = 512
H, KV, HD = 32, 8, 16
REP = H // KV
GC = (REP + 1) * HD
QK = KV * GC
NG = NB * KV
PARTS = 6
KROWS = PARTS * HD
HF = 1376
NH = -(-HF // P)
BLK = 64
EDGES_N = 15
W1, W2, W3 = range(3)
SIGN_TILES = (2, 4, 6, 8, 10)
PIECES = [(W1, 0), (W2, 0), (W3, 0), (W3, 1), (W3, 2), (W3, 3), (W2, 2), (W3, 4), (W2, 4), (W3, 5), (W2, 6), (W3, 6),
          (W3, 7), (W2, 8), (W3, 8), (W2, 10), (W3, 9), (W3, 10)]
SIGN_STEPS = EDGES_N * len(PIECES)
EARLY_MAX = 82
by_vector = lambda h: 0 if h == 0 else 1 if h in SIGN_TILES else 2
W3_AFTER = {0: (0, 1), 1: (2, 3), 3: (4,), 4: (5,), 6: (6,), 8: (7,), 9: (8,), 10: (9, 10)}
STEPS_BY = [80, 98, 114, 141, 154, 180, 193, 221, 234, 257, 270]
for h_, by in enumerate(STEPS_BY):
    assert h_ not in SIGN_TILES or by >= EDGES_N * (PIECES.index((W2, h_)) + 1)
    assert all(by + 13 >= EDGES_N * (PIECES.index((W3, p)) + 1) for p in W3_AFTER.get(h_, ()))
Y_RANGES = ((0, 4), (4, 8), (8, NH))
Y_AFTER = {4: [(0, i) for i in range(0, 4)], 6: [(0, i) for i in range(4, 8)], 8: [(1, i) for i in range(0, 4)]}
Y_LAST = [(1, i) for i in range(4, 8)]
DI, NS, RK, KC = 1024, 16, 32, 4
DC = DI // P
SP_ = 80
UNITS = DC * NB * NS
NE, RR = 16, 64
LC = RR + NE

NF4 = np.array([-1.0, -0.6961928009986877, -0.5250730514526367, -0.39491748809814453, -0.28444138169288635,
                -0.18477343022823334, -0.09105003625154495, 0.0, 0.07958029955625534, 0.16093020141124725,
                0.24611230194568634, 0.33791524171829224, 0.44070982933044434, 0.5626170039176941,
                0.7229568362236023, 1.0], np.float32)
EDGES = (NF4[:-1] + NF4[1:]) * np.float32(0.5)
STEPS = NF4[1:] - NF4[:-1]


def sign_args():
    out = []
    for e in EDGES:
        up = np.nextafter(e, np.float32(np.inf))
        for s in (1.5, 1.25, 1.125, 1.75, 1.0625, 1.875, 1.375, 1.625):
            c = np.float32(-float(e) * s)
            for c in (c, np.nextafter(c, np.float32(-1e9)), np.nextafter(c, np.float32(1e9))):
                if float(e) * s < -float(c) < float(up) * s:
                    break
            else:
                continue
            break
        else:
            raise AssertionError("no scale separates the edge")
        out.append((s, float(c)))
    return out


SIGNS = sign_args()

CONSTS = {}


def constants():
    at, parts = 0, []

    def put(name, a):
        nonlocal at
        full = np.zeros((P, a.shape[1]), np.float32)
        full[:a.shape[0]] = a
        CONSTS[name] = (at, a.shape[1])
        parts.append(full)
        at += a.shape[1]

    p = np.arange(P)
    put("ident", np.eye(P, dtype=np.float32))
    mean = np.zeros((SP_, SP_), np.float32)
    for a, n in ((0, RK), (RK, NS), (64, NS)):
        mean[a:a + n, a:a + n] = 1.0 / n
    put("mean", mean)
    pick = np.zeros((SP_, NS), np.float32)
    for part in range(3):
        pick[32 * part:32 * part + NS] = np.eye(NS)
    put("pick", pick)
    freq = (1.0 / 10000.0 ** (np.arange(0, HD, 2, dtype=np.float32) / np.float32(HD))).astype(np.float32)
    ang = np.arange(S, dtype=np.float32)[:, None] * freq[None, :]
    for name, f in (("cos", np.cos), ("sin", np.sin)):
        t = f(ang).astype(np.float32)
        t = np.concatenate([t, t], 1).reshape(TS_, P, HD).transpose(1, 0, 2).reshape(P, TS_ * HD)
        put(name, t)
    put("iota", np.tile(np.arange(NE, dtype=np.float32), (P, 1)))
    put("edge_bias", np.tile(np.array([c for _, c in SIGNS], np.float32), (P, 1)))
    put("eps", np.full((P, 1), 1e-6, np.float32))
    put("one", np.ones((P, 1), np.float32))
    put("mhalf", np.full((P, 4), -0.5, np.float32))
    return np.concatenate(parts, 1)


CONST = constants()


def build(nc, x, cst, wqkv, bqkv, w1, w2, w3, w_in, conv, wx, lnw, wdt, acol, w_out, base_w, base_b, lora_a, lora_b, out):
    ctx = ExitStack()
    with ctx:
        sem = lambda name: ctx.enter_context(nc.semaphore(name))
        arena = ctx.enter_context(nc.sbuf_tensor("arena", [P, 53200], F32))
        psum = ctx.enter_context(nc.psum_tensor("psum", [P, 8 * BANK], F32))

        def at(off, n, rows=P):
            return arena[0:rows, off:off + n]

        def at16(off, n, rows=P):
            return arena[0:rows, off:off + n // 2].bitcast(BF16)

        def bank(b, n=1, rows=P):
            return psum[0:rows, b * BANK:(b + n) * BANK]

        X = at(0, NT * E).rearrange("p (i e) -> p i e", e=E)
        XNT = at(4096, EC * NB * S).rearrange("p (c t) -> p c t", c=EC)
        NCST = CONST.shape[1]
        C = at(8192, NCST)
        const = lambda name, rows=P: C[0:rows, CONSTS[name][0]:CONSTS[name][0] + CONSTS[name][1]]
        assert NCST <= 1408
        small = 9600
        ST6 = at(small, 48).rearrange("p (i s) -> p i s", s=6)
        MV = at(small + 48, 16).rearrange("p (i s) -> p i s", s=2)
        VARE = at(small + 64, 8)
        RSTD = at(small + 72, 8)
        identb = at16(small + 80, P)
        XN = at(small + 144, 2 * E).rearrange("p (k e) -> p k e", e=E)
        R0 = small + 144 + 1024
        ident = const("ident")
        o = R0
        WQ = at(o, EC * 768).rearrange("p (c n) -> p c n", c=EC); o += EC * 768
        BQ = at(o, 768); o += 768
        R = at(o, NT * QK).rearrange("p (i n) -> p i n", i=NT); o += NT * QK
        V1 = at(o, NT * KV * 32).rearrange("p (i k d) -> p i k d", i=NT, k=KV); o += NT * KV * 32
        QC = at(o, QK).rearrange("p (h d) -> p h d", d=HD); o += QK
        QS = at(o, QK).rearrange("p (h d) -> p h d", d=HD); o += QK
        SKW = TS_ * 5 * KROWS
        SK = at16(o, 2 * SKW).rearrange("p (k t s q d) -> p k t s q d", k=2, t=TS_, s=5, d=HD)
        SKF = at16(o, 2 * SKW).rearrange("p (k t s c) -> p k t s c", k=2, t=TS_, s=5); o += SKW
        RES = at(o, TS_ * GC).rearrange("p (t s d) -> p t s d", t=TS_, d=HD); o += TS_ * GC
        LO = at16(o, TS_ * GC).rearrange("p (t s d) -> p t s d", t=TS_, d=HD); o += TS_ * GC // 2
        QT = at16(o, 4 * 5 * S).rearrange("p (k s t) -> p k s t", k=4, s=5); o += 4 * 5 * S // 2
        PR = at(o, 3 * REP * S).rearrange("p (k j t) -> p k j t", k=3, j=REP); o += 3 * REP * S
        OS = at(o, 2 * S).rearrange("p (k t) -> p k t", k=2); o += 2 * S
        MX = at(o, 32).rearrange("p (k t j) -> p k t j", k=2, t=TS_); o += 32
        MS = at16(o, 64).rearrange("p (k t m j) -> p k t m j", k=2, t=TS_, m=2)
        MSF = at16(o, 64).rearrange("p (k t c) -> p k t c", k=2, t=TS_); o += 32
        MTS = at16(o, 2 * S).rearrange("p (k t) -> p k t", k=2); o += S
        REC = at(o, 16).rearrange("p (t j) -> p t j", j=REP); o += 16
        TMP = at(o, TS_ * REP * HD).rearrange("p (t j d) -> p t j d", t=TS_, j=REP); o += TS_ * REP * HD
        assert o <= 39460, o
        o = R0
        HT = at(o, NH * NB * S).rearrange("p (h t) -> p h t", h=NH); o += NH * NB * S
        DQ3 = at(o, NH * E).rearrange("p (h e) -> p h e", h=NH); o += NH * E
        DQT = at(o, 2 * 2 * E).rearrange("p (k w c h) -> p k w c h", k=2, w=2, c=EC); o += 2 * 2 * E
        SG = at(o, NB * S); o += NB * S
        NTB = at(o, 2 * 2 * E).rearrange("p (k n) -> p k n", k=2); o += 4 * E
        NACC = at(o, 2 * E); o += 2 * E
        DQ = at(o, 2 * 2 * E).rearrange("p (k w e) -> p k w e", k=2, w=2); o += 4 * E
        assert o <= 39460, o
        AM3 = at(39460, 4 * 86).rearrange("p (q n) -> p q n", q=4)
        AMX = at(39804, 172).rearrange("p (g b) -> p g b", g=4)
        W3A = at(39976, 2 * BANK).rearrange("p (k n) -> p k n", k=2)
        W3F = at(41000, 4 * HF)
        W3R = at(41000, 4 * HF).rearrange("p (j r h) -> p j r h", j=2, r=2)
        W3G = at(41000, 4 * HF).rearrange("p (g h) -> p g h", g=4)
        RING = 4
        WR = at(46504, RING * 2 * E).rearrange("p (k w e) -> p k w e", k=RING, w=2)
        o = 46504 + RING * 2 * E
        W3M = at(o, 2 * BANK).rearrange("p (k n) -> p k n", k=2); o += 2 * BANK
        W3T = at(o, 2 * BANK).rearrange("p (k n) -> p k n", k=2); o += 2 * BANK
        AM = at(o, RING * 4 * 16).rearrange("p (k q n) -> p k q n", k=RING, q=4); o += RING * 64
        assert o <= 53200, o
        WI = at(41000, EC * 2 * DI).rearrange("p (c n) -> p c n", c=EC)
        U = at(R0, DC * NB * S).rearrange("p (c t) -> p c t", c=DC)
        GS = at(R0 + 8192, DC * NB * S).rearrange("p (c t) -> p c t", c=DC)
        CR = at(R0 + 16384, NS * NB * S).rearrange("p (n t) -> p n t", n=NS)
        CV = at(49192, 2 * NB * S).rearrange("p (k t) -> p k t", k=2)
        WX = at(51240, DC * SP_).rearrange("p (c n) -> p c n", c=DC)
        AC = at(51880, P)
        CP = at(52008, DC * 7).rearrange("p (c n) -> p c n", n=7)
        LW = at(52064, 1, SP_)
        WD = at(52065, DI, RK)
        o = R0 + 32768
        SS = at(o, NB * S, SP_)
        SQ = at(o + 1024, NB * S, SP_)
        RMS = at(o + 2048, NB * S, SP_)
        PN = at(o + 3072, NB * S, SP_)
        WB = at16(o + 4096, 3 * NB * S, SP_).rearrange("p (k t) -> p k t", k=3)
        BS = at16(4096, NB * S, SP_)
        CS = WB[:, 2, :]
        RES2 = at(o + 1024, NB * S, SP_)
        PICK = at16(4096 + 512, NS * P, SP_).rearrange("p (n m) -> p n m", n=NS)
        GN = 5
        G = at(4096 + 1536, GN * S).rearrange("p (k t) -> p k t", k=GN)
        D = at(o, 2 * S).rearrange("p (k t) -> p k t", k=2)
        SPL = at(o + 1024, 2 * S).rearrange("p (k t) -> p k t", k=2)
        MXB = at(o + 4096, 2 * S).rearrange("p (k t) -> p k t", k=2)
        DU = at(49192, 2 * S).rearrange("p (k t) -> p k t", k=2)
        DB = [at(o + 5120, S), at(50728, S), at(51240, S)]
        HS = [at(o + 2048, S), at(o + 2560, S), at(50216, S), XN[:, 1, :]]
        YT = XN[:, 0, :]
        WO = at(R0, DC * E).rearrange("p (c n) -> p c n", c=DC)
        o = R0 + 16384
        BF = at(o, NE * RR * E // P).rearrange("p (c n) -> p c n", c=NE * RR // P); o += NE * RR * E // P
        BW = at(o, EC * E).rearrange("p (c n) -> p c n", c=EC); o += EC * E
        LA = at(o, EC * LC).rearrange("p (c n) -> p c n", c=EC); o += EC * LC
        BB = at(o, E); o += E
        LG = at(o, NT * LC).rearrange("p (i n) -> p i n", i=NT); o += NT * LC
        PB = at(o, NT * NE).rearrange("p (i n) -> p i n", i=NT); o += NT * NE
        OH1 = at(o, NT * NE).rearrange("p (i n) -> p i n", i=NT); o += NT * NE
        OH2 = at(o, NT * NE).rearrange("p (i n) -> p i n", i=NT); o += NT * NE
        V8 = at(o, NT * 8).rearrange("p (i n) -> p i n", i=NT); o += NT * 8
        I8 = at(o, NT * 8).bitcast(U32).rearrange("p (i n) -> p i n", i=NT); o += NT * 8
        IF = at(o, NT * 2).rearrange("p (i n) -> p i n", i=NT); o += NT * 2
        W12 = at(o, NT * 2).rearrange("p (i n) -> p i n", i=NT); o += NT * 2
        R8 = at(o, 4 * NT).rearrange("p (q i) -> p q i", q=4); o += 4 * NT
        Z = at(o, 2 * NE * RR).rearrange("p (k e r) -> p k e r", k=2, e=NE)
        ZF = at(o, 2 * NE * RR).rearrange("p (k c n) -> p k c n", k=2, c=8); o += 2 * NE * RR
        ZT = at(o, 2 * NE * RR).rearrange("p (k c n) -> p k c n", k=2, c=8); o += 2 * NE * RR
        assert o <= R0 + 32768

        ld_x = [sem("ld_x0"), sem("ld_x1")]
        ld_const, ld_qkv, ld_w3, ld_wi, ld_scan, ld_wo, ld_moe = (
            sem(n) for n in ("ld_const", "ld_qkv", "ld_w3", "ld_wi", "ld_scan", "ld_wo", "ld_moe"))
        ld_w12 = [sem("ld_w12_%d" % k) for k in range(4)]
        init_done = sem("init_done")
        ln_var, ln_rstd, ln_xn, ln_tr, ln_ev = (sem(n) for n in ("ln_var", "ln_rstd", "ln_xn", "ln_tr", "ln_ev"))
        qkv_done, rope_read, rope_done, v_done = (sem(n) for n in ("qkv_done", "rope_read", "rope_done", "v_done"))
        sk_ready, sk_tr, qt_ev = (sem(n) for n in ("sk_ready", "sk_tr", "qt_ev"))
        max_ps, max_read, ms_ready, mt_tr, mt_ev, ld_rows = (
            sem(n) for n in ("max_ps", "max_read", "ms_ready", "mt_tr", "mt_ev", "ld_rows"))
        st_ps, exp_done, pv_done, os_ev, et_tr, et_used, x_attn = (
            sem(n) for n in ("st_ps", "exp_done", "pv_done", "os_ev", "et_tr", "et_used", "x_attn"))
        am_done, w2_v, w3_v, w3_t, w3_add, w3_dq, w3_tr, w3_ev = (
            sem(n) for n in ("am_done", "w2_v", "w3_v", "w3_t", "w3_add", "w3_dq", "w3_tr", "w3_ev"))
        nf_v, dq_done, dq_tr, dq_ev, gu_ps, silu_done, ht_done, y_ps, x_ffn = (
            sem(n) for n in ("nf_v", "dq_done", "dq_tr", "dq_ev", "gu_ps", "silu_done", "ht_done", "y_ps", "x_ffn"))
        u_ps, conv_done, u_done, g_ps, gs_done, ssm_ps, ss_ev, sq_done, ms_ps, rr_done, pn_done = (
            sem(n) for n in ("u_ps", "conv_done", "u_done", "g_ps", "gs_done", "ssm_ps", "ss_ev", "sq_done",
                             "ms_ps", "rr_done", "pn_done"))
        pick_done, bs_done, c_ps, c_ev_act, c_ev_dve = (
            sem(n) for n in ("pick_done", "bs_done", "c_ps", "c_ev_act", "c_ev_dve"))
        dt_ps, sp_done, mx_done, d_done, du_done = (sem(n) for n in ("dt_ps", "sp_done", "mx_done", "d_done", "du_done"))
        b_ps, da_done, dbu_done, scan_done, g_done, ysum, y_read, y_done = (
            sem(n) for n in ("b_ps", "da_done", "dbu_done", "scan_done", "g_done", "ysum", "y_read", "y_done"))
        abs_done = sem("abs_done")
        wo_ps, x_scan = sem("wo_ps"), sem("x_scan")
        lg_ps, lg_ev, lg_sub, lg_exp, route_done, z_done, z_tr, z_ev, out_ps, out_done, st_out = (
            sem(n) for n in ("lg_ps", "lg_ev", "lg_sub", "lg_exp", "route_done", "z_done", "z_tr", "z_ev", "out_ps",
                             "out_done", "st_out"))
        bias_done = sem("bias_done")
        dve_step, act_step, pool_step = sem("dve_step"), sem("act_step"), sem("pool_step")

        ROWS_LD = 2 * REP * 16

        class Steps:

            def __init__(self, eng, s):
                self.eng, self.s, self.n = eng, s, 0

            def step(self, ins):
                self.n += 1
                ins.then_inc(self.s, 1)
                return self.n

            def wait(self, n=None):
                self.eng.wait_ge(self.s, self.n if n is None else n)

        block = ctx.enter_context(nc.Block())
        V, A, G_, T = nc.vector, nc.scalar, nc.gpsimd, nc.tensor
        ht_rows = lambda h: min(P, HF - h * P)
        early = lambda slot: min(slot * 9 // 10 + max(0, slot - 60) * 2 // 10, EARLY_MAX)
        adds_after = lambda s: (EDGES_N - 1) * (s // EDGES_N) + s % EDGES_N
        SLOT = lambda n, t: TS_ * (n + 3) + t

        def piece(q):
            m, h = PIECES[q]
            return W3G[:, :, h * P:h * P + ht_rows(h)] if m == W3 else WR[0:ht_rows(h), h % RING, m, :]

        def like(buf, q):
            m, h = PIECES[q]
            n = ht_rows(h)
            return buf[:, 0:4 * n].rearrange("p (g h) -> p g h", g=4) if m == W3 else buf[0:n]

        STEP_SUM = float(np.float32(float(NF4[0]) + float(STEPS.astype(np.float64).sum()) / 2))

        @block.sync
        def _(sp):
            sp.dma_start(C, cst).then_inc(ld_const, 16)
            xv = x.rearrange("(i p) e -> p i e", p=P)
            sp.dma_start(X[:, 0:TS_, :], xv[:, 0:TS_, :]).then_inc(ld_x[0], 16)
            sp.dma_start(WQ, wqkv.rearrange("(c p) n -> p c n", p=P)).then_inc(ld_qkv, 16)
            sp.dma_start(BQ, bqkv.broadcast_to([P, 768])).then_inc(ld_qkv, 16)
            sp.dma_start(X[:, TS_:NT, :], xv[:, TS_:NT, :]).then_inc(ld_x[1], 16)
            def load_w12(h):
                n = ht_rows(h)
                sp.dma_start(WR[0:n, h % RING, 0, :], w1[h * P:h * P + n, :]).then_inc(ld_w12[h % RING], 16)
                sp.dma_start(WR[0:n, h % RING, 1, :], w2[h * P:h * P + n, :]).then_inc(ld_w12[h % RING], 16)

            load_w12(0)
            sp.dma_start(W3F.rearrange("p (j n) -> p j n", j=2),
                         w3.rearrange("(j p r) h -> p j (r h)", p=P, r=2)).then_inc(ld_w3, 16)

            for h in range(1, RING):
                load_w12(h)
            for g in range(NG):
                sp.wait_ge(mt_ev, g + 1)
                for m in range(2):
                    for j in range(REP):
                        sp.dma_start(QT[KROWS + m:KROWS + m + 1, g % 4, j, :],
                                     MTS[REP * m + j:REP * m + j + 1, g % 2, :]).then_inc(ld_rows, 16)
            for h in range(RING, NH):
                sp.wait_ge(dq_done, 2 * (h - RING + 1))
                load_w12(h)
            sp.wait_ge(dq_done, 2 * NH)
            sp.wait_ge(w3_add, (EDGES_N - 1) * len(PIECES))
            sp.dma_start(CP, conv.rearrange("(c p) n -> p c n", p=P)).then_inc(ld_scan, 16)
            sp.wait_ge(w3_tr, NH)
            sp.dma_start(WI, w_in.rearrange("(c p) n -> p c n", p=P)).then_inc(ld_wi, 16)
            sp.dma_start(WX, wx.rearrange("(c p) n -> p c n", p=P)).then_inc(ld_scan, 16)
            sp.dma_start(AC, acol).then_inc(ld_scan, 16)
            sp.dma_start(LW, lnw).then_inc(ld_scan, 16)
            sp.dma_start(WD, wdt).then_inc(ld_scan, 16)
            sp.wait_ge(y_done, UNITS // NS // 2)
            sp.dma_start(WO, w_out.rearrange("(c p) n -> p c n", p=P)).then_inc(ld_wo, 16)
            sp.wait_ge(g_done, UNITS)
            sp.dma_start(BF, lora_b.rearrange("(c p) n -> p c n", p=P)).then_inc(ld_moe, 16)
            sp.dma_start(BW, base_w.rearrange("(c p) n -> p c n", p=P)).then_inc(ld_moe, 16)
            sp.dma_start(LA, lora_a.rearrange("(c p) n -> p c n", p=P)).then_inc(ld_moe, 16)
            sp.dma_start(BB, base_b.broadcast_to([P, E])).then_inc(ld_moe, 16)
            ov = out.rearrange("(i p) e -> p i e", p=P)
            for i in range(NT):
                sp.wait_ge(out_done, i + 1)
                sp.dma_start(ov[:, i, :], X[:, i, :]).then_inc(st_out, 16)
            sp.wait_ge(st_out, 16 * NT)

        @block.vector
        def _(dve):
            own = Steps(dve, dve_step)

            def statistics(k, half):
                tiles = range(TS_ * half, TS_ * half + TS_)
                if k == 0:
                    dve.wait_ge(ld_x[half], 16)
                else:
                    dve.wait_ge((None, x_attn, x_ffn, x_scan)[k],
                                (None, KV * (half + 1), 2 * NT + TS_ * (half + 1), TS_ * (half + 1))[k])
                if k:
                    dve.wait_ge(ln_xn, NT * k)
                for i in tiles:
                    n = own.step(V.bn_stats(ST6[:, i, :], X[:, i, :]))
                for i in tiles:
                    own.wait(n - TS_ + 1 + i % TS_)
                    m = own.step(V.bn_aggr(MV[:, i, :], ST6[:, i, :]))
                own.wait(m)
                V.tensor_scalar(VARE[:, tiles[0]:tiles[0] + TS_], MV[:, tiles[0]:tiles[0] + TS_, 1], 1e-5, None,
                                ALU.add).then_inc(ln_var, 1)

            def normalise(k, tiles=range(NT)):
                for i in tiles:
                    if i % TS_ == 0:
                        dve.wait_ge(ln_rstd, 2 * k + i // TS_ + 1)
                    if NT * k + i >= 2:
                        dve.wait_ge(ln_tr, NT * k + i - 1)
                    V.tensor_scalar(XN[:, i % 2, :], X[:, i, :], MV[:, i, 0:1], RSTD[:, i:i + 1],
                                    ALU.subtract, ALU.mult).then_inc(ln_xn, 1)

            def layernorm(k):
                for half in range(2):
                    statistics(k, half)
                normalise(k)

            dve.wait_ge(ld_const, 16)
            V.tensor_copy(identb, ident).then_inc(init_done, 1)
            V.memset(V1, 0.0).then_inc(init_done, 1)
            dve.wait_ge(init_done, 2)
            V.memset(V1[:, :, :, HD:HD + 1], 1.0).then_inc(init_done, 1)
            V.memset(QT[KROWS:KROWS + 2, :, REP, :], 1.0).then_inc(init_done, 1)
            layernorm(0)

            def rope(i):
                base = (i % 2) * 2 * BANK
                dve.wait_ge(qkv_done, i + 1)
                if i == 0:
                    dve.wait_ge(ld_qkv, 32)
                own.step(V.tensor_tensor(psum[:, base:base + 768], psum[:, base:base + 768], BQ, ALU.add))
                own.wait()
                ps = psum[:, base:base + QK].rearrange("p (h d) -> p h d", d=HD)
                t = i % TS_
                cos, sin = (const(n)[:, t * HD:t * HD + HD].unsqueeze(1).broadcast_to([P, QK // HD, HD])
                            for n in ("cos", "sin"))
                if i:
                    dve.wait_ge(rope_done, i)
                own.step(V.tensor_tensor(QC, ps, cos, ALU.mult))
                V.tensor_tensor(QS, ps, sin, ALU.mult).then_inc(rope_read, 1)
                dve.wait_ge(rope_read, i + 1)
                r = R[:, i, :].rearrange("p (h d) -> p h d", d=HD)
                V.tensor_tensor(r[:, :, 0:HD // 2], QC[:, :, 0:HD // 2], QS[:, :, HD // 2:HD], ALU.subtract)
                V.tensor_tensor(r[:, :, HD // 2:HD], QS[:, :, 0:HD // 2], QC[:, :, HD // 2:HD], ALU.add)\
                 .then_inc(rope_done, 1)

            def w3_prepare(part):
                blocks = W3F.rearrange("p (n k) -> p n k", k=BLK)
                if part < 2:
                    half = slice(43 * part, 43 * part + 43)
                    dve.wait_ge(ld_w3, 16)
                    own.step(V.tensor_reduce(AM3[:, 0, half], blocks[:, half], AXX, ALU.max, apply_absolute_value=True))
                elif part == 2:
                    own.wait()
                    own.step(V.tensor_copy(AMX.rearrange("p g b -> p (g b)").rearrange("p (n k) -> p n k", k=2),
                                           AM3[:, 0, :].unsqueeze(2).broadcast_to([P, 86, 2])))
                    own.step(V.tensor_scalar(AM3[:, 1, :], AM3[:, 0, :], 0.0, None, ALU.is_equal))
                    own.wait()
                    own.step(V.tensor_tensor(AM3[:, 2, :], AM3[:, 0, :], AM3[:, 1, :], ALU.add))
                    own.wait()
                    own.step(V.reciprocal(AM3[:, 3, :], AM3[:, 2, :]))
                else:
                    half = slice(43 * (part - 3), 43 * (part - 3) + 43)
                    own.wait()
                    V.tensor_tensor(blocks[:, half], blocks[:, half],
                                    AM3[:, 3, half].unsqueeze(2).broadcast_to([P, 43, BLK]), ALU.mult).then_inc(w3_v, 1)

            def prepare(h):
                n = ht_rows(h)
                am = AM[0:n, h % RING]
                raw = WR[0:n, h % RING].rearrange("p w e -> p (w e)").rearrange("p (b k) -> p b k", k=BLK)
                dve.wait_ge(ld_w12[h % RING], 32 * (h // RING + 1))
                if h >= RING:
                    dve.wait_ge(dq_done, 2 * (h - RING + 1))
                own.step(V.tensor_reduce(am[:, 0, :], raw, AXX, ALU.max, apply_absolute_value=True))
                own.wait()
                own.step(V.tensor_scalar(am[:, 1, :], am[:, 0, :], 0.0, None, ALU.is_equal))
                own.wait()
                own.step(V.tensor_tensor(am[:, 2, :], am[:, 0, :], am[:, 1, :], ALU.add))
                own.wait()
                V.reciprocal(am[:, 3, :], am[:, 2, :]).then_inc(am_done, 1)

            def first_tile():
                dve.wait_ge(am_done, 1)
                for w in range(2):
                    v = WR[:, 0, w, :].rearrange("p (b k) -> p b k", k=BLK)
                    V.tensor_tensor(v, v, AM[:, 0, 3, w * (E // BLK):(w + 1) * (E // BLK)].unsqueeze(2)
                                    .broadcast_to([P, E // BLK, BLK]), ALU.mult).then_inc(w2_v, 1)

            for i in range(NT):
                rope(i)
                if i == 1:
                    prepare(0)
                    first_tile()
                if i >= 3:
                    w3_prepare(i - 3)

            def row_max(g, t, j):
                if t == 0 and j == 0 and g >= 2:
                    dve.wait_ge(ms_ready, g - 1)
                n = (g * TS_ + t) * REP + j
                dve.wait_ge(max_ps, n + 1)
                V.tensor_reduce(MX[:, g % 2, t, j:j + 1], bank(n % 2), AXX, ALU.max, negate=True).then_inc(max_read, 1)

            def evac_stack(g, r):
                n = 3 * g + r
                dve.wait_ge(sk_tr, n + 1)
                w = 2 if r < 2 else 1
                V.tensor_copy(QT[0:KROWS, g % 4, 2 * r:2 * r + w, :],
                              bank(7)[0:KROWS].bitcast(BF16)[:, 0:w * S].rearrange("p (s t) -> p s t", s=w))\
                 .then_inc(qt_ev, 1)

            def finish(g):
                b, kv = g // KV, g % KV
                dve.wait_ge(et_tr, g + 1)
                o_ps = bank(7).rearrange("p (t j d) -> p t j d", t=TS_, d=32)
                if g:
                    dve.wait_ge(et_used, g)
                    dve.wait_ge(x_attn, g)
                own.step(V.reciprocal(REC, o_ps[:, :, :, HD]))
                own.wait()
                V.tensor_tensor(TMP, o_ps[:, :, :, 0:HD],
                                REC.unsqueeze(3).broadcast_to([P, TS_, REP, HD]), ALU.mult).then_inc(et_used, 1)
                dve.wait_ge(et_used, g + 1)
                xs = X[:, TS_ * b:TS_ * b + TS_, REP * HD * kv:REP * HD * kv + REP * HD]
                V.tensor_tensor(xs, xs, TMP.rearrange("p t j d -> p t (j d)"), ALU.add).then_inc(x_attn, 1)

            for n in range(-3, NG + 2):
                for t in range(TS_):
                    for j in range(REP):
                        if 0 <= n + 2 < NG:
                            row_max(n + 2, t, j)
                        if j == 0 and t and 0 <= n + 3 < NG:
                            evac_stack(n + 3, t - 1)
                        if j == 0 and t == 0 and 0 <= n - 2:
                            finish(n - 2)
                    if n == NG - 1:
                        if t == 0:
                            statistics(1, 0)
                        else:
                            prepare(t)

            dve.wait_ge(et_tr, NG)
            dve.wait_ge(pv_done, NG * TS_)

            def nf4(h):
                n = ht_rows(h)
                ws = by_vector(h)
                am, wide = AM[0:n, h % RING], ws * E
                v = WR[0:n, h % RING].rearrange("p w e -> p (w e)")[:, 0:wide]
                acc = NACC[0:n, 0:wide]
                b3 = lambda a: a.rearrange("p (b k) -> p b k", k=BLK)
                rb = lambda a: a.unsqueeze(2).broadcast_to([n, wide // BLK, BLK])
                dve.wait_ge(am_done, h + 1)
                if ws == 0:
                    scale_codes(h)
                    return
                V.tensor_tensor(b3(v), b3(v), rb(am[:, 3, 0:wide // BLK]), ALU.mult).then_inc(nf_v, 1)
                dve.wait_ge(nf_v, h)
                dve.wait_ge(dq_done, 2 * h)

                def edge(i):
                    return own.step(V.tensor_scalar(NTB[0:n, i % 2, 0:wide], v, float(EDGES[i]), float(STEPS[i]),
                                                    ALU.is_gt, ALU.mult))

                edge(0)
                last = edge(1)
                own.wait(last)
                added = own.step(V.scalar_tensor_tensor(acc, NTB[0:n, 0, 0:wide], float(NF4[0]), NTB[0:n, 1, 0:wide],
                                                        ALU.add, ALU.add))
                own.wait(added)
                made = edge(2)
                for i in range(3, EDGES_N + 1):
                    before = added
                    if i < EDGES_N:
                        nxt = edge(i)
                    own.wait(max(made, before))
                    added = own.step(V.tensor_tensor(acc, acc, NTB[0:n, (i - 1) % 2, 0:wide], ALU.add))
                    if i < EDGES_N:
                        made = nxt
                        own.wait(added)
                    if i in (10, 12, 14):
                        out_add(h - 1, i // 2 - 5)
                    if i == 6 and h + 3 < NH:
                        prepare(h + 3)
                    if i == 12 and ws == 2:
                        hidden(h - 1, 0)
                        hidden(h - 1, 1)
                own.wait(added)
                scale_codes(h)

            def scale_codes(h):
                n, ws, am = ht_rows(h), by_vector(h), AM[0:ht_rows(h), h % RING]
                b3 = lambda a: a.rearrange("p (b k) -> p b k", k=BLK)
                for w in range(2):
                    if h >= 2:
                        dve.wait_ge(dq_tr, 2 * (h - 2) + w + 1)
                    dst = DQ[0:n, h % 2, w].rearrange("p (b k) -> p b k", k=BLK)
                    scale = am[:, 0, w * (E // BLK):(w + 1) * (E // BLK)].unsqueeze(2).broadcast_to([n, E // BLK, BLK])
                    if w < ws:
                        V.tensor_tensor(dst, b3(NACC[0:n, w * E:w * E + E]), scale, ALU.mult).then_inc(dq_done, 1)
                    else:
                        dve.wait_ge(w3_add, (EDGES_N - 1) * (PIECES.index((w, h)) + 1))
                        V.scalar_tensor_tensor(dst, b3(WR[0:n, h % RING, w, :]), STEP_SUM, scale, ALU.add, ALU.mult)\
                         .then_inc(dq_done, 1)

            def w3_finish(h):
                n = ht_rows(h)
                dve.wait_ge(w3_add, (EDGES_N - 1) * (PIECES.index((W3, h)) + 1))
                per = P // (BLK // 2)
                nb = n // (BLK // 2)
                for g in range(4):
                    w = W3G[:, g, h * P:h * P + n].rearrange("p (b k) -> p b k", k=BLK // 2)
                    ins = V.scalar_tensor_tensor(w, w, STEP_SUM, AMX[:, g, per * h:per * h + nb].unsqueeze(2)
                                                 .broadcast_to([P, nb, BLK // 2]), ALU.add, ALU.mult)
                ins.then_inc(w3_dq, 1)

            def hidden(h, b):
                n, t = ht_rows(h), slice(b * S, b * S + S)
                dve.wait_ge(silu_done, 2 * h + b + 1)
                V.tensor_tensor(HT[0:n, h, t], SG[0:n, t], bank(4 + b)[0:n], ALU.mult).then_inc(ht_done, 1)

            def out_add(h, k):
                if k < len(Y_AFTER.get(h, ())):
                    out_tile(*Y_AFTER[h][k])

            def out_tile(rng, i):
                n = NT * rng + i
                dve.wait_ge(y_ps, n + 1)
                if rng:
                    dve.wait_ge(x_ffn, n - NT + 1)
                V.tensor_tensor(X[:, i, :], X[:, i, :], bank(6 + n % 2), ALU.add).then_inc(x_ffn, 1)

            statistics(1, 1)
            nf4(0)
            normalise(1)
            for p in W3_AFTER[0]:
                w3_finish(p)
            for h in range(1, NH):
                nf4(h)
                out_add(h - 1, 3)
                if by_vector(h) < 2:
                    hidden(h - 1, 0)
                    hidden(h - 1, 1)
                for p in W3_AFTER.get(h, ()):
                    w3_finish(p)
            hidden(NH - 1, 0)
            hidden(NH - 1, 1)
            for rng, i in Y_LAST + [(2, i) for i in range(NT)]:
                out_tile(rng, i)
                if (rng, i) == (2, TS_ - 1):
                    statistics(2, 0)

            statistics(2, 1)
            normalise(2)
            dve.wait_ge(ld_scan, 16 * 5)
            for c in range(DC):
                dve.wait_ge(u_ps, c + 1)
                if c >= 2:
                    dve.wait_ge(u_done, c - 1)
                ps = bank(0, 2).rearrange("p (b t) -> p b t", b=NB)
                cv = CV[:, c % 2, :].rearrange("p (b t) -> p b t", b=NB)
                own.step(V.tensor_scalar(cv, ps, CP[:, c, KC - 1:KC], CP[:, c, KC:KC + 1], ALU.mult, ALU.add))
                for lag in range(1, KC):
                    own.wait()
                    ins = V.scalar_tensor_tensor(cv[:, :, lag:S], ps[:, :, 0:S - lag], CP[:, c, KC - 1 - lag:KC - lag],
                                                 cv[:, :, lag:S], ALU.mult, ALU.add)
                    if lag < KC - 1:
                        own.step(ins)
                    else:
                        ins.then_inc(conv_done, 1)
            dve.wait_ge(g_ps, DC)
            own.step(V.memset(BS, 0.0))
            own.step(V.memset(CS, 0.0))
            V.tensor_copy(PICK, const("pick", SP_).unsqueeze(2).broadcast_to([SP_, NS, P])).then_inc(pick_done, 1)
            own.wait()
            dve.wait_ge(rr_done, 1)
            dve.wait_ge(ss_ev, 1)
            V.scalar_tensor_tensor(PN, SS, LW[:, 0:1], RMS, ALU.mult, ALU.mult).then_inc(pn_done, 1)
            dve.wait_ge(pn_done, 1)
            for dst, a in ((CS, 64), (BS, RK)):
                src, hi, mid, res = (t[a:a + NS] for t in (PN, WB[:, 0], WB[:, 1], RES2))
                own.step(V.tensor_copy(hi, src))
                own.wait()
                own.step(V.tensor_tensor(res, src, hi, ALU.subtract))
                own.wait()
                own.step(V.tensor_copy(mid, res))
                own.wait()
                own.step(V.tensor_copy(dst[0:NS], hi))
                own.step(V.tensor_copy(dst[32:32 + NS], mid))
                V.tensor_tensor(dst[64:64 + NS], res, mid, ALU.subtract).then_inc(bs_done, 1)
            def delta_max(k):
                dve.wait_ge(abs_done, k + 1)
                if k >= 2:
                    dve.wait_ge(d_done, k - 1)
                V.tensor_scalar(MXB[:, k % 2, :], bank(6 + k % 2), CP[:, k // NB, 5:6], 0.0, ALU.add, ALU.max).then_inc(mx_done, 1)

            def delta(k):
                dve.wait_ge(mx_done, k + 1)
                dve.wait_ge(sp_done, k + 1)
                if k >= 2:
                    dve.wait_ge(da_done, NS * (k - 1))
                    dve.wait_ge(du_done, k - 1)
                V.tensor_tensor(D[:, k % 2, :], MXB[:, k % 2, :], SPL[:, k % 2, :], ALU.add).then_inc(d_done, 1)

            def times_b(m):
                dve.wait_ge(b_ps, m + 1)
                if m % NS == 0:
                    dve.wait_ge(du_done, m // NS + 1)
                if m >= 3:
                    dve.wait_ge(scan_done, m - 2)
                V.tensor_tensor(DB[m % 3], DU[:, m // NS % 2, :], bank(m % 3), ALU.mult).then_inc(dbu_done, 1)

            def scan(m):
                dve.wait_ge(dbu_done, m + 1)
                dve.wait_ge(da_done, m + 1)
                if m >= 4:
                    dve.wait_ge(g_done, m - 3)
                V.tensor_tensor_scan(HS[m % 4], bank(3 + m % 3), DB[m % 3], 0.0, ALU.mult, ALU.add)\
                 .then_inc(scan_done, 1)

            def gate(k):
                c, b = k // NB, k % NB
                dve.wait_ge(ysum, NS * (k + 1))
                if k:
                    dve.wait_ge(y_done, k)
                V.scalar_tensor_tensor(YT, U[:, c, b * S:b * S + S], CP[:, c, 6:7], bank(6 + k % 2), ALU.mult,
                                       ALU.add).then_inc(y_read, 1)

            NK = UNITS // NS
            for n in range(1, NS, 2):
                dve.wait_ge(c_ps, n + 1)
                V.tensor_copy(CR[:, n, :], bank(2 * (n % 3), 2)).then_inc(c_ev_dve, 1)
                if n == 7:
                    dve.wait_ge(bs_done, 2)
                    delta_max(0)
                if n == 11:
                    delta(0)
            dve.wait_ge(c_ev_act, NS // 2)
            times_b(0)
            for m in range(UNITS):
                k, n = m // NS, m % NS
                if m + 1 < UNITS:
                    times_b(m + 1)
                scan(m)
                if k >= 1 and n == 3:
                    gate(k - 1)
                if k + 1 < NK:
                    if n == 9:
                        delta_max(k + 1)
                    if n == 13:
                        delta(k + 1)
            gate(NK - 1)
            for i in range(NT):
                dve.wait_ge(wo_ps, i + 1)
                V.tensor_tensor(X[:, i, :], X[:, i, :], bank(i % 2), ALU.add).then_inc(x_scan, 1)
                if i == TS_ - 1:
                    statistics(3, 0)
                if i >= TS_:
                    normalise(3, (i - TS_,))

            statistics(3, 1)
            normalise(3, range(TS_, NT))
            dve.wait_ge(ld_moe, 64)
            dve.wait_ge(ln_xn, 4 * NT)
            V.tensor_tensor(X, X, BB.unsqueeze(1).broadcast_to([P, NT, E]), ALU.add).then_inc(bias_done, 1)
            dve.wait_ge(bias_done, 1)
            r8 = lambda q: R8[:, q, :]
            rb = lambda a, n: a.unsqueeze(2).broadcast_to([P, NT, n])
            dve.wait_ge(lg_ev, NT)
            own.step(V.tensor_reduce(r8(0), LG[:, :, RR:LC], AXX, ALU.max))
            own.wait()
            V.tensor_tensor(PB, LG[:, :, RR:LC], rb(r8(0), NE), ALU.subtract).then_inc(lg_sub, 1)
            dve.wait_ge(lg_exp, 1)
            own.step(V.reduce_sum(r8(1), PB, AXX))
            own.wait()
            own.step(V.reciprocal(r8(2), r8(1)))
            own.wait()
            own.step(V.tensor_tensor(OH1, PB, rb(r8(2), NE), ALU.mult))
            own.wait()
            for i in range(NT):
                own.step(V.max(V8[:, i, :], OH1[:, i, :]))
            for i in range(NT):
                own.wait()
                own.step(V.max_index(I8[:, i, :], V8[:, i, :], OH1[:, i, :]))
            own.wait()
            own.step(V.tensor_copy(IF, I8[:, :, 0:2]))
            own.step(V.tensor_tensor(r8(3), V8[:, :, 0], V8[:, :, 1], ALU.add))
            own.wait()
            own.step(V.tensor_scalar(r8(0), r8(3), 1e-6, None, ALU.add))
            own.wait()
            own.step(V.reciprocal(r8(1), r8(0)))
            own.wait()
            own.step(V.tensor_scalar(r8(2), r8(1), 0.5, None, ALU.mult))
            own.wait()
            own.step(V.tensor_tensor(W12, V8[:, :, 0:2], rb(r8(2), 2), ALU.mult))
            iota = const("iota").unsqueeze(1).broadcast_to([P, NT, NE])
            for k, oh in enumerate((OH1, OH2)):
                own.wait()
                own.step(V.tensor_tensor(oh, iota, rb(IF[:, :, k], NE), ALU.is_equal))
                own.wait()
                own.step(V.tensor_tensor(oh, oh, rb(W12[:, :, k], NE), ALU.mult))
            own.wait()
            own.step(V.tensor_tensor(PB, OH1, OH2, ALU.add))
            own.wait()

            def low_rank(i):
                if i >= 2:
                    dve.wait_ge(z_tr, i - 1)
                V.tensor_tensor(Z[:, i % 2], PB[:, i, :].unsqueeze(2).broadcast_to([P, NE, RR]),
                                LG[:, i, 0:RR].unsqueeze(1).broadcast_to([P, NE, RR]), ALU.mult).then_inc(z_done, 1)

            for i in range(NT + 1):
                if i < NT:
                    low_rank(i)
                if i:
                    dve.wait_ge(out_ps, i)
                    V.tensor_tensor(X[:, i - 1, :], X[:, i - 1, :], bank((0, 1, 6, 7)[(i - 1) % 4]), ALU.add)\
                     .then_inc(out_done, 1)

        @block.gpsimd
        def _(pool):
            own = Steps(pool, pool_step)

            def rstd(k):
                for half in range(2):
                    pool.wait_ge(ln_var, 2 * k + half + 1)
                    G_.tensor_tensor(RSTD[:, TS_ * half:TS_ * half + TS_], VARE[:, TS_ * half:TS_ * half + TS_],
                                     const("mhalf"), ALU.pow).then_inc(ln_rstd, 1)

            pool.wait_ge(ld_const, 16)
            rstd(0)

            def sums(lo, hi):
                for s in range(lo, hi):
                    q, i = divmod(s, EDGES_N)
                    if i:
                        k = adds_after(s)
                        pool.wait_ge(w3_t, s + 1)
                        if k > 1:
                            pool.wait_ge(w3_add, k - 1)
                        acc = like(W3A[:, q % 2], q)
                        dst = piece(q) if i == EDGES_N - 1 else acc
                        G_.tensor_tensor(dst, acc, like(W3T[:, s % 2], q), ALU.add).then_inc(w3_add, 1)
                    if i == EDGES_N // 2 + 1 and q + 1 < len(PIECES) and PIECES[q + 1][0] != W3 and q > 0:
                        h = PIECES[q + 1][1]
                        n = ht_rows(h)
                        pool.wait_ge(am_done, h + 1)
                        w = piece(q + 1).rearrange("p (b k) -> p b k", k=BLK)
                        G_.tensor_tensor(w, w, AM[0:n, h % RING, 3, E // BLK:2 * E // BLK].unsqueeze(2)
                                         .broadcast_to([n, E // BLK, BLK]), ALU.mult).then_inc(w2_v, 1)

            def stack(g, part):
                b, kv = g // KV, g % KV
                r = R[:, TS_ * b:TS_ * b + TS_, GC * kv:GC * kv + GC].rearrange("p t (s d) -> p t s d", d=HD)
                sk = SK[:, g % 2]
                q, k = sk[:, :, 0:REP], sk[:, :, REP]
                if part == 0:
                    pool.wait_ge(rope_done, TS_ * (b + 1))
                    if g >= 2:
                        pool.wait_ge(sk_tr, 3 * (g - 1))
                    if g:
                        pool.wait_ge(sk_ready, g)
                    own.step(G_.tensor_copy(sk[:, :, :, 0, :], r))
                    own.wait()
                    own.step(G_.tensor_tensor(RES, r, sk[:, :, :, 0, :], ALU.subtract))
                elif part == 1:
                    own.wait()
                    own.step(G_.tensor_copy(sk[:, :, :, 4, :], RES))
                    own.wait()
                    own.step(G_.tensor_tensor(LO, RES, sk[:, :, :, 4, :], ALU.subtract))
                elif part == 2:
                    for dst, src in ((1, 0), (2, 0), (3, 4)):
                        own.step(G_.tensor_copy(q[:, :, :, dst, :], q[:, :, :, src, :]))
                else:
                    for dst, src in ((1, 4), (3, 0), (5, 0)):
                        own.step(G_.tensor_copy(k[:, :, dst, :], k[:, :, src, :]))
                    own.wait()
                    own.step(G_.tensor_copy(q[:, :, :, 5, :], LO[:, :, 0:REP]))
                    own.wait()
                    G_.tensor_copy(k[:, :, 2, :], LO[:, :, REP]).then_inc(sk_ready, 1)

            def split_max(g):
                pool.wait_ge(max_read, TS_ * REP * (g + 1))
                if g >= 2:
                    pool.wait_ge(mt_tr, g - 1)
                own.step(G_.tensor_copy(MS[:, g % 2, :, 0, :], MX[:, g % 2]))
                own.wait()
                G_.tensor_tensor(MS[:, g % 2, :, 1, :], MX[:, g % 2], MS[:, g % 2, :, 0, :], ALU.subtract)\
                  .then_inc(ms_ready, 1)

            for part in range(4):
                stack(0, part)
            for n in range(-3, NG + 1):
                for t in range(TS_):
                    if n + 4 < NG:
                        stack(n + 4, t)
                    sums(early(SLOT(n, t)), early(SLOT(n, t) + 1))
                if 0 <= n + 2 < NG:
                    split_max(n + 2)

            s0 = early(SLOT(NG, TS_))
            rstd(1)
            sums(s0, SIGN_STEPS)
            rstd(2)

            def times_u(k):
                pool.wait_ge(d_done, k + 1)
                if k >= 2:
                    pool.wait_ge(dbu_done, NS * (k - 1))
                G_.tensor_tensor(DU[:, k % 2, :], D[:, k % 2, :], U[:, k // NB, k % NB * S:k % NB * S + S], ALU.mult)\
                  .then_inc(du_done, 1)

            def times_gate(k):
                pool.wait_ge(y_read, k + 1)
                g = GS[:, k // NB, k % NB * S:k % NB * S + S]
                G_.tensor_tensor(g, g, YT, ALU.mult).then_inc(y_done, 1)

            times_u(0)
            pool.wait_ge(c_ev_act, NS // 2)
            pool.wait_ge(c_ev_dve, NS // 2)
            for m in range(UNITS):
                b = m // NS % NB
                if m % NS == 4 and m > NS:
                    times_gate(m // NS - 1)
                if m % NS == 13 and m + NS < UNITS:
                    times_u(m // NS + 1)
                pool.wait_ge(scan_done, m + 1)
                if m >= GN:
                    pool.wait_ge(ysum, m - GN + 1)
                G_.tensor_tensor(G[:, m % GN, :], HS[m % 4], CR[:, m % NS, b * S:b * S + S], ALU.mult).then_inc(g_done, 1)
            times_gate(UNITS // NS - 1)
            rstd(3)

        @block.scalar
        def _(act):
            own = Steps(act, act_step)

            def evac_ln(k):
                for i in range(NT):
                    act.wait_ge(ln_tr, NT * k + i + 1)
                    A.activation(XNT[:, :, i * P:i * P + P], bank(6 + i % 2).rearrange("p (c t) -> p c t", c=EC), ACT.Copy)\
                     .then_inc(ln_ev, 1)

            evac_ln(0)
            act.wait_ge(init_done, 4)
            for i in range(NT):
                act.wait_ge(rope_read, i + 1)
                base = (i % 2) * 2 * BANK + QK
                A.activation(V1[:, i, :, 0:HD], psum[:, base:base + KV * HD].rearrange("p (k d) -> p k d", d=HD), ACT.Copy)\
                 .then_inc(v_done, 1)

            def exps(step, q):
                if q == 0 and step >= 3:
                    act.wait_ge(pv_done, step - 2)
                n = 2 * step + q
                act.wait_ge(st_ps, n + 1)
                A.activation(PR[:, step % 3, 2 * q:2 * q + 2, :],
                             bank(2 + 2 * q, 2).rearrange("p (j t) -> p j t", j=2), ACT.Exp, scale=HD ** -0.5)\
                 .then_inc(exp_done, 1)

            made = {}

            def sign(s):
                q, i = divmod(s, EDGES_N)
                if i == 0 and PIECES[q][0] == W3:
                    act.wait_ge(w3_v, 2)
                if i == 0 and PIECES[q][0] != W3:
                    act.wait_ge(w2_v, sum(m != W3 for m, _ in PIECES[:q + 1]))
                if s >= 2:
                    act.wait_ge(w3_t, s - 1)
                rows = P if PIECES[q][0] == W3 else ht_rows(PIECES[q][1])
                made[s] = own.step(A.activation(like(W3M[:, s % 2], q), piece(q), ACT.Sign, scale=float(SIGNS[i][0]),
                                                bias=const("edge_bias", rows)[:, i:i + 1]))

            def signs(lo, hi):
                for s in range(lo, hi):
                    q, i = divmod(s, EDGES_N)
                    if s == 0:
                        sign(0)
                    if s + 1 < SIGN_STEPS:
                        sign(s + 1)
                    own.wait(made[s])
                    if i == 0:
                        dst = W3A[:, q % 2]
                        if q >= 2:
                            act.wait_ge(w3_add, (EDGES_N - 1) * (q - 1))
                    else:
                        dst = W3T[:, s % 2]
                        if s >= 3:
                            act.wait_ge(w3_add, adds_after(s - 2))
                    A.activation(like(dst, q), like(W3M[:, s % 2], q), ACT.Copy, scale=float(STEPS[i]) / 2)\
                     .then_inc(w3_t, 1)

            for n in range(-3, NG + 1):
                for t in range(TS_):
                    if 0 <= n < NG:
                        exps(TS_ * n + t, 0)
                    signs(early(SLOT(n, t)), early(SLOT(n, t) + 1))
                    if t == 1 and 0 <= n + 1 < NG:
                        act.wait_ge(mt_tr, n + 2)
                        if n + 1 >= 2:
                            act.wait_ge(ld_rows, ROWS_LD * n)
                        A.activation(MTS[0:2 * REP, (n + 1) % 2, :], bank(7)[0:2 * REP].bitcast(BF16)[:, 0:S], ACT.Copy)\
                         .then_inc(mt_ev, 1)
                    if 0 <= n < NG:
                        exps(TS_ * n + t, 1)
                    if t == 0:
                        if n >= 1:
                            act.wait_ge(pv_done, TS_ * n)
                            if n >= 3:
                                act.wait_ge(et_tr, n - 2)
                            A.activation(OS[:, (n - 1) % 2, :], bank(6), ACT.Copy).then_inc(os_ev, 1)

            s = early(SLOT(NG, TS_))
            signs(s, s + 1)
            s += 1
            evac_ln(1)
            for h in range(NH):
                n = ht_rows(h)
                signs(s, STEPS_BY[h])
                s = STEPS_BY[h]
                for w in range(2):
                    act.wait_ge(dq_tr, 2 * h + w + 1)
                    if h >= 2:
                        act.wait_ge(gu_ps, 2 * (h - 1))
                    A.activation(DQT[:, h % 2, w, :, 0:n], bank(w).rearrange("p (c h) -> p c h", c=EC)[:, :, 0:n], ACT.Copy)\
                     .then_inc(dq_ev, 1)
                for b in range(2):
                    to = min(STEPS_BY[h] + (8, 13)[b], SIGN_STEPS) if h < NH - 1 else SIGN_STEPS
                    signs(s, to)
                    s = to
                    act.wait_ge(gu_ps, 2 * h + b + 1)
                    if h:
                        act.wait_ge(ht_done, 2 * (h - 1) + b + 1)
                    A.activation(SG[0:n, b * S:b * S + S], bank(2 + b)[0:n], ACT.Silu).then_inc(silu_done, 1)
                for p in W3_AFTER.get(h, ()):
                    m = ht_rows(p)
                    act.wait_ge(w3_tr, p + 1)
                    A.activation(DQ3[0:m, p, :].rearrange("p (j q r) -> p j r q", j=2, r=2),
                                 bank(p % 2)[0:m].rearrange("p (j r q) -> p j r q", j=2, r=2), ACT.Copy).then_inc(w3_ev, 1)

            evac_ln(2)
            for c in range(DC):
                act.wait_ge(conv_done, c + 1)
                A.activation(U[:, c, :], CV[:, c % 2, :], ACT.Silu).then_inc(u_done, 1)
                act.wait_ge(g_ps, c + 1)
                A.activation(GS[:, c, :], bank(2, 2), ACT.Silu).then_inc(gs_done, 1)
            act.wait_ge(ssm_ps, 1)
            A.activation(SQ, bank(4, 2)[0:SP_], ACT.Square).then_inc(sq_done, 1)
            A.activation(SS, bank(4, 2)[0:SP_], ACT.Copy).then_inc(ss_ev, 1)
            act.wait_ge(ms_ps, 1)
            own.step(A.activation(RMS, bank(6, 2)[0:SP_], ACT.Ln, bias=const("eps", SP_)))
            own.wait()
            A.activation(RMS, RMS, ACT.Exp, scale=-0.5).then_inc(rr_done, 1)
            def softplus(k, part):
                buf = SPL[:, k % 2, :]
                if part == 0:
                    act.wait_ge(dt_ps, k + 1)
                    if k >= 2:
                        act.wait_ge(d_done, k - 1)
                    A.activation(buf, bank(6 + k % 2), ACT.Abs, bias=CP[:, k // NB, 5:6]).then_inc(abs_done, 1)
                elif part == 1:
                    act.wait_ge(abs_done, k + 1)
                    own.step(A.activation(buf, buf, ACT.Exp, scale=-1.0))
                else:
                    own.wait()
                    A.activation(buf, buf, ACT.Ln, bias=const("one")).then_inc(sp_done, 1)

            for n in range(0, NS, 2):
                act.wait_ge(c_ps, n + 1)
                A.activation(CR[:, n, :], bank(2 * (n % 3), 2), ACT.Copy).then_inc(c_ev_act, 1)
                if n in (2, 4, 6):
                    if n == 2:
                        act.wait_ge(bs_done, 2)
                    softplus(0, n // 2 - 1)
            act.wait_ge(c_ev_dve, NS // 2)
            act.wait_ge(c_ev_act, NS // 2)
            SP_AT = (10, 11, 12)
            for m in range(UNITS):
                k, n = m // NS, m % NS
                if n == 0:
                    act.wait_ge(d_done, k + 1)
                if m >= 3:
                    act.wait_ge(scan_done, m - 2)
                A.activation(bank(3 + m % 3), D[:, k % 2, :], ACT.Exp, scale=AC[:, NS * (k // NB) + n:NS * (k // NB) + n + 1])\
                 .then_inc(da_done, 1)
                if n in SP_AT and k + 1 < UNITS // NS:
                    softplus(k + 1, SP_AT.index(n))

            evac_ln(3)
            for i in range(NT):
                act.wait_ge(lg_ps, i + 1)
                A.activation(LG[:, i, :], bank(4 + i % 2)[:, 0:LC], ACT.Copy).then_inc(lg_ev, 1)
            act.wait_ge(lg_sub, 1)
            A.activation(PB, PB, ACT.Exp).then_inc(lg_exp, 1)
            for i in range(NT):
                act.wait_ge(z_tr, i + 1)
                if i >= 2:
                    act.wait_ge(out_ps, i - 1)
                A.activation(ZT[:, i % 2], bank(2 + 2 * (i % 2), 2).rearrange("p (c n) -> p c n", c=8), ACT.Copy)\
                 .then_inc(z_ev, 1)

        @block.tensor
        def _(pe):
            def transpose_ln(k, tiles=range(NT)):
                for i in tiles:
                    pe.wait_ge(ln_xn, NT * k + i + 1)
                    if i >= 2:
                        pe.wait_ge(ln_ev, NT * k + i - 1)
                    for c in range(EC):
                        mm = T.transpose(bank(6 + i % 2)[:, c * P:c * P + P], XN[:, i % 2, c * P:c * P + P], ident)
                    mm.then_inc(ln_tr, 1)

            pe.wait_ge(ld_const, 16)
            transpose_ln(0)
            pe.wait_ge(ld_qkv, 32)
            for i in range(NT):
                pe.wait_ge(ln_ev, i + 1)
                if i >= 2:
                    pe.wait_ge(rope_read, i - 1)
                    pe.wait_ge(v_done, i - 1)
                for a, n in ((0, BANK), (BANK, 768 - BANK)):
                    o_ = psum[:, (i % 2) * 2 * BANK + a:(i % 2) * 2 * BANK + a + n]
                    for c in range(EC):
                        mm = T.matmul(o_, XNT[:, c, i * P:i * P + P], WQ[:, c, a:a + n], start=(c == 0), stop=(c == EC - 1))
                mm.then_inc(qkv_done, 1)

            used = {"mt": 0, "qt": 0, "et": 0}

            def bank7_free():
                for s_, n_ in ((mt_ev, used["mt"]), (qt_ev, used["qt"]), (et_used, used["et"])):
                    if n_:
                        pe.wait_ge(s_, n_)

            def turn_stack(g, r):
                pe.wait_ge(sk_ready, g + 1)
                bank7_free()
                used["qt"] += 1
                dst = bank(7)[0:KROWS].bitcast(BF16)
                for s in range(2 * r, min(2 * r + 2, 5)):
                    for t in range(TS_):
                        c = ((s - 2 * r) * TS_ + t) * P
                        mm = T.transpose(dst[:, c:c + P], SKF[:, g % 2, t, s, :], identb)
                mm.then_inc(sk_tr, 1)

            def score_rows(g, t, j):
                pe.wait_ge(qt_ev, 3 * (g + 1))
                n = (g * TS_ + t) * REP + j
                if n >= 2:
                    pe.wait_ge(max_read, n - 1)
                T.matmul(bank(n % 2), QT[0:KROWS, g % 4, j, t * P:t * P + P], QT[0:KROWS, g % 4, REP, :],
                         start=True, stop=True).then_inc(max_ps, 1)

            def turn_max(g):
                pe.wait_ge(ms_ready, g + 1)
                bank7_free()
                used["mt"] += 1
                for t in range(TS_):
                    mm = T.transpose(bank(7)[0:2 * REP].bitcast(BF16)[:, t * P:t * P + P], MSF[:, g % 2, t, :], identb)
                mm.then_inc(mt_tr, 1)

            def score_cols(g, t, q):
                pe.wait_ge(ld_rows, ROWS_LD * (g + 1))
                n = 2 * (g * TS_ + t) + q
                if n >= 2:
                    pe.wait_ge(exp_done, n - 1)
                for j in range(2 * q, 2 * q + 2):
                    mm = T.matmul(bank(2 + j), QT[0:KROWS + 2, g % 4, REP, t * P:t * P + P],
                                  QT[0:KROWS + 2, g % 4, j, :], start=True, stop=True)
                mm.then_inc(st_ps, 1)

            def values(step):
                g, t = step // TS_, step % TS_
                pe.wait_ge(exp_done, 2 * step + 2)
                if t == 0 and g:
                    pe.wait_ge(os_ev, g)
                for j in range(REP):
                    mm = T.matmul(bank(6)[32 * j:32 * j + 32], V1[:, TS_ * (g // KV) + t, g % KV, :],
                                  PR[:, step % 3, j, :], start=(t == 0), stop=(t == TS_ - 1))
                mm.then_inc(pv_done, 1)

            def turn_out(g):
                pe.wait_ge(os_ev, g + 1)
                bank7_free()
                used["et"] += 1
                for t in range(TS_):
                    mm = T.transpose(bank(7)[:, t * P:t * P + P], OS[:, g % 2, t * P:t * P + P], ident)
                mm.then_inc(et_tr, 1)

            pe.wait_ge(init_done, 4)
            pe.wait_ge(rope_read, NT)
            pe.wait_ge(v_done, NT)
            for n in range(-3, NG + 1):
                for t in range(TS_):
                    for j in range(REP):
                        if 0 <= n + 2 < NG:
                            score_rows(n + 2, t, j)
                        if j < 2 and 0 <= n < NG:
                            score_cols(n, t, j)
                        if j == 1 and t == 1 and 0 <= n + 1 < NG:
                            turn_max(n + 1)
                        if j == 2 and 0 <= TS_ * n + t - 1 < TS_ * NG:
                            values(TS_ * n + t - 1)
                    if t < 3 and 0 <= n + 3 < NG:
                        turn_stack(n + 3, t)
                    if t == 3 and n >= 1:
                        turn_out(n - 1)

            bank7_free()
            pe.wait_ge(os_ev, NG)
            transpose_ln(1)
            def turn_w12(h):
                n = ht_rows(h)
                for w in range(2):
                    pe.wait_ge(dq_done, 2 * h + w + 1)
                    if h and w == 0:
                        pe.wait_ge(dq_ev, 2 * h)
                        pe.wait_ge(w3_ev, max(1, sum(len(W3_AFTER.get(k, ())) for k in range(h))))
                    for c in range(EC):
                        mm = T.transpose(bank(w)[:, c * P:c * P + n], DQ[0:n, h % 2, w, c * P:c * P + P], ident[0:n, 0:n])
                    mm.then_inc(dq_tr, 1)

            def turn_w3(p):
                n = ht_rows(p)
                pe.wait_ge(w3_dq, p + 1)
                if p >= 2:
                    pe.wait_ge(w3_ev, p - 1)
                for j in range(2):
                    for r in range(2):
                        mm = T.transpose(bank(p % 2)[0:n, (2 * j + r) * P:(2 * j + r) * P + P],
                                         W3R[:, j, r, p * P:p * P + n], ident)
                mm.then_inc(w3_tr, 1)

            def out_part(rng, i):
                k, (lo, hi) = NT * rng + i, Y_RANGES[rng]
                pe.wait_ge(ht_done, 2 * hi)
                pe.wait_ge(w3_ev, hi)
                if k == 0:
                    pe.wait_ge(ln_ev, 2 * NT)
                if k >= 2:
                    pe.wait_ge(x_ffn, k - 1)
                for h in range(lo, hi):
                    n = ht_rows(h)
                    mm = T.matmul(bank(6 + k % 2), HT[0:n, h, i * P:i * P + P], DQ3[0:n, h, :],
                                  start=(h == lo), stop=(h == hi - 1))
                mm.then_inc(y_ps, 1)

            for h in range(NH):
                n = ht_rows(h)
                turn_w12(h)
                pe.wait_ge(dq_ev, 2 * (h + 1))
                if h == 0:
                    pe.wait_ge(ln_ev, 2 * NT)
                for b in range(NB):
                    if h:
                        pe.wait_ge(ht_done, 2 * (h - 1) + b + 1)
                    for w in range(2):
                        for c in range(EC):
                            mm = T.matmul(bank(2 + 2 * w + b)[0:n], DQT[:, h % 2, w, c, 0:n], XNT[:, c, b * S:b * S + S],
                                          start=(c == 0), stop=(c == EC - 1))
                    mm.then_inc(gu_ps, 1)
                for p in W3_AFTER.get(h, ()):
                    if p < 2:
                        pe.wait_ge(dq_ev, 2 * (h + 1))
                    turn_w3(p)
                for rng, i in Y_AFTER.get(h, ()):
                    out_part(rng, i)
            for rng, i in Y_LAST + [(2, i) for i in range(NT)]:
                out_part(rng, i)

            transpose_ln(2)
            pe.wait_ge(x_ffn, 3 * NT)
            pe.wait_ge(ld_wi, 16)
            pe.wait_ge(ld_scan, 16 * 5)
            pe.wait_ge(ln_ev, 3 * NT)

            def to_ssm(c):
                pe.wait_ge(u_done, c + 1)
                for b in range(NB):
                    mm = T.matmul(bank(4 + b)[0:SP_], WX[:, c, :], U[:, c, b * S:b * S + S], start=(c == 0), stop=(c == DC - 1))
                if c == DC - 1:
                    mm.then_inc(ssm_ps, 1)

            for c in range(DC):
                for half in range(2):
                    if c:
                        pe.wait_ge((conv_done, gs_done)[half], c)
                    for b in range(NB):
                        for e in range(EC):
                            mm = T.matmul(bank(2 * half + b), WI[:, e, half * DI + c * P:half * DI + c * P + P],
                                          XNT[:, e, b * S:b * S + S], start=(e == 0), stop=(e == EC - 1))
                    mm.then_inc((u_ps, g_ps)[half], 1)
                if c >= 1:
                    to_ssm(c - 1)
            to_ssm(DC - 1)
            pe.wait_ge(sq_done, 1)
            for b in range(NB):
                mm = T.matmul(bank(6 + b)[0:SP_], const("mean", SP_), SQ[:, b * S:b * S + S], start=True, stop=True)
            mm.then_inc(ms_ps, 1)
            pe.wait_ge(gs_done, DC)
            pe.wait_ge(pn_done, 1)

            def delta_in(k):
                if k >= 2:
                    pe.wait_ge(y_read, k - 1)
                T.matmul(bank(6 + k % 2), WD[:, k // NB * P:k // NB * P + P], PN[0:RK, k % NB * S:k % NB * S + S],
                         start=True, stop=True).then_inc(dt_ps, 1)

            pe.wait_ge(rr_done, 1)
            delta_in(0)
            pe.wait_ge(pick_done, 1)
            pe.wait_ge(bs_done, 1)
            for n in range(NS):
                if n >= 3:
                    m = n - 3
                    pe.wait_ge((c_ev_act, c_ev_dve)[m % 2], m // 2 + 1)
                for b in range(NB):
                    mm = T.matmul(bank(2 * (n % 3) + b), PICK[:, n, :], CS[:, b * S:b * S + S], start=True, stop=True)
                mm.then_inc(c_ps, 1)
            pe.wait_ge(c_ev_act, NS // 2)
            pe.wait_ge(c_ev_dve, NS // 2)
            pe.wait_ge(bs_done, 2)

            def b_rows(m):
                b = m // NS % NB
                if m >= 3:
                    pe.wait_ge(dbu_done, m - 2)
                T.matmul(bank(m % 3), PICK[:, m % NS, :], BS[:, b * S:b * S + S], start=True, stop=True).then_inc(b_ps, 1)

            def sum_states(m):
                k, n = m // NS, m % NS
                if n == 0:
                    pe.wait_ge(mx_done, k + 1)
                pe.wait_ge(g_done, m + 1)
                T.matmul(bank(6 + k % 2), ident, G[:, m % GN, :], start=(n == 0), stop=(n == NS - 1)).then_inc(ysum, 1)

            for m in range(UNITS + 4):
                if m < UNITS:
                    b_rows(m)
                if m >= 4:
                    sum_states(m - 4)
                if m < UNITS and m % NS == 8 and m // NS + 1 < UNITS // NS:
                    delta_in(m // NS + 1)
            pe.wait_ge(ld_wo, 16)
            pe.wait_ge(y_done, UNITS // NS)
            for i in range(NT):
                if i >= 2:
                    pe.wait_ge(x_scan, i - 1)
                for c in range(DC):
                    mm = T.matmul(bank(i % 2), GS[:, c, i * P:i * P + P], WO[:, c, :], start=(c == 0), stop=(c == DC - 1))
                mm.then_inc(wo_ps, 1)
                if i > TS_:
                    transpose_ln(3, (i - TS_ - 1,))

            transpose_ln(3, range(TS_ - 1, NT))
            pe.wait_ge(x_scan, NT)
            pe.wait_ge(ld_moe, 64)
            pe.wait_ge(ln_ev, 4 * NT)
            for i in range(NT):
                if i >= 2:
                    pe.wait_ge(lg_ev, i - 1)
                for c in range(EC):
                    mm = T.matmul(bank(4 + i % 2)[:, 0:LC], XNT[:, c, i * P:i * P + P], LA[:, c, :], start=(c == 0), stop=(c == EC - 1))
                mm.then_inc(lg_ps, 1)
            out_bank = lambda i: bank((0, 1, 6, 7)[i % 4])

            def base(i):
                if i >= 4:
                    pe.wait_ge(out_done, i - 3)
                for c in range(EC):
                    T.matmul(out_bank(i), XNT[:, c, i * P:i * P + P], BW[:, c, :], start=(c == 0), stop=False)

            base(0)
            base(1)
            pe.wait_ge(lg_ev, NT)
            for i in range(NT + 1):
                if i < NT:
                    pe.wait_ge(z_done, i + 1)
                    if i >= 2:
                        pe.wait_ge(z_ev, i - 1)
                    for c in range(8):
                        mm = T.transpose(bank(2 + 2 * (i % 2), 2)[:, c * P:c * P + P], ZF[:, i % 2, c, :], ident)
                    mm.then_inc(z_tr, 1)
                if i:
                    pe.wait_ge(z_ev, i)
                    for c in range(8):
                        mm = T.matmul(out_bank(i - 1), ZT[:, (i - 1) % 2, c, :], BF[:, c, :], start=False, stop=(c == 7))
                    mm.then_inc(out_ps, 1)
                if i + 2 < NT:
                    base(i + 2)

def kernel(**inputs):
    import concourse.bacc as _bacc
    from concourse.bass_utils import run_bass_kernel_spmd as _run

    a = {k: np.asarray(v) for k, v in inputs.items()}
    q = a["L0_attn_wq"].reshape(E, KV, REP * HD)
    k = a["L0_attn_wk"].reshape(E, KV, HD)
    bq, bk = a["L0_attn_bq"].reshape(1, KV, REP * HD), a["L0_attn_bk"].reshape(1, KV, HD)
    wqkv = np.concatenate([np.concatenate([q, k], 2).reshape(E, QK), a["L0_attn_wv"]], 1)
    bqkv = np.concatenate([np.concatenate([bq, bk], 2).reshape(1, QK), a["L0_attn_bv"].reshape(1, KV * HD)], 1)
    conv = np.concatenate([a["L1_attn_conv_w"], a["L1_attn_conv_b"][:, None], a["L1_attn_dt_bias"][:, None],
                           a["L1_attn_D_param"][:, None]], 1)
    wx = a["L1_attn_Wx"].T
    wxp = np.zeros((DI, SP_), np.float32)
    wxp[:, 0:RK + NS] = wx[:, 0:RK + NS]
    wxp[:, 64:SP_] = wx[:, RK + NS:]
    lnw = np.zeros((SP_, 1), np.float32)
    lnw[0:RK, 0] = a["L1_attn_dt_ln_w"]
    lnw[RK:RK + NS, 0] = a["L1_attn_b_ln_w"]
    lnw[64:SP_, 0] = a["L1_attn_c_ln_w"]
    arrays = {
        "x": a["L0_attn_x"].reshape(NB * S, E), "cst": CONST, "wqkv": wqkv, "bqkv": bqkv,
        "w1": a["L0_ffn_w1"], "w2": a["L0_ffn_w2"], "w3": a["L0_ffn_w3"],
        "w_in": a["L1_attn_W_in"].T, "conv": conv, "wx": wxp, "lnw": lnw, "wdt": a["L1_attn_Wdt"].T,
        "acol": a["L1_attn_A"].reshape(DC, P, NS).transpose(1, 0, 2).reshape(P, DC * NS), "w_out": a["L1_attn_W_out"].T,
        "base_w": a["L1_ffn_base_w"].T, "base_b": a["L1_ffn_base_b"].reshape(1, E),
        "lora_a": np.concatenate([a["L1_ffn_A"].T, a["L1_ffn_router_w"].T], 1),
        "lora_b": a["L1_ffn_B"].transpose(0, 2, 1).reshape(NE * RR, E),
    }
    arrays = {n: np.ascontiguousarray(v) for n, v in arrays.items()}
    nc = _bacc.Bacc("TRN2", target_bir_lowering=False, num_devices=1)
    args = [nc.dram_tensor(n, v.shape, F32, kind="ExternalInput").ap() for n, v in arrays.items()]
    out = nc.dram_tensor("out", (NB * S, E), F32, kind="ExternalOutput").ap()
    build(nc, *args, out)
    r = _run(nc, [arrays], core_ids=[0])
    return r.results[0]["out"].reshape(NB, S, E)
```
